# Optimizing a Trainium2 kernel written in Bass

```python
import numpy as np
import jax
import jax.numpy as jnp

def _softmax(x, axis=-1):
    return jax.nn.softmax(x, axis=axis)

def _gelu(x):
    return jax.nn.gelu(x, approximate=True)

def _silu(x):
    return jax.nn.silu(x)

def _sigmoid(x):
    return jax.nn.sigmoid(x)

def _layernorm(x, axis=-1, eps=1e-05):
    m = jnp.mean(x, axis=axis, keepdims=True)
    v = jnp.var(x, axis=axis, keepdims=True)
    return (x - m) / jnp.sqrt(v + eps)

def _scatter_add(tgt, idx, src, axis=0):
    return tgt.at[idx].add(src)

def _segment_sum(src, seg, n):
    return jax.ops.segment_sum(src, seg, n)
kernel_name = 'mk_xattn_seq_d2_seqx_r8_b71cea'

def setup_inputs(seed: int=0):
    np.random.seed(seed)
    _w = jnp.asarray

    def _rec_inputs():
        import jax
        import jax.numpy as jnp
        _rk = jax.random.key(seed)
        x = -0.0005207 + 1.001 * jax.random.normal(jax.random.fold_in(_rk, 1), (32, 64, 256), jnp.float32)
        _lenS = 64 - jax.random.randint(jax.random.fold_in(_rk, 7), (32,), 0, max(1, 64 // 4) + 1, jnp.int32)
        _lenS2 = 64 - jax.random.randint(jax.random.fold_in(_rk, 8), (32,), 0, max(1, 64 // 4) + 1, jnp.int32)
        _ctx_2048P = jax.random.normal(jax.random.fold_in(_rk, 11), (32, 16, 256), jnp.float32)
        _ctx_2048c = jax.random.dirichlet(jax.random.fold_in(_rk, 511), 0.3 * jnp.ones((16,), jnp.float32), (32, 64))
        _ctx_2048t = jnp.einsum('bsk,bkd->bsd', _ctx_2048c, _ctx_2048P)
        _ctx_2048t = _ctx_2048t * jax.lax.rsqrt(jnp.mean(jnp.square(_ctx_2048t)) + 1e-12) * 0.953939
        ctx_2048 = 2.81802e-05 + 1.00001 * (_ctx_2048t + 0.3 * jax.random.normal(jax.random.fold_in(_rk, 611), (32, 64, 256), jnp.float32))
        _validS = jnp.arange(64)[None, :] < _lenS[:, None]
        _validS2 = jnp.arange(64)[None, :] < _lenS2[:, None]
        _causal = jnp.tril(jnp.ones((64, 64), dtype=bool))
        mask_BxS2_ik0 = jnp.where(jnp.broadcast_to(_validS2[:, :], (32, 64)), 0, 1).astype(jnp.int32)
        return (x, ctx_2048, mask_BxS2_ik0)
    x, ctx_2048, mask_BxS2_ik0 = _rec_inputs()

    def _L0_xattn_setup():
        import jax, jax.numpy as jnp
        import numpy as np
        B, Q, S1, S2 = (4, 32, 256, 256)
        D, H, K, F = (256, 16, 128, 1024)
        LN_EPS = 1e-05

        def _layer_norm(x, scale, offset):
            mu = jnp.mean(x, axis=-1, keepdims=True)
            var = jnp.var(x, axis=-1, keepdims=True)
            return (x - mu) * jax.lax.rsqrt(var + LN_EPS) * scale + offset

        def _cross_attention(q_in, kv_in, wq, bq, wk, bk, wv, bv, wo, bo, bias_k, bias_v):
            b, q_len, _ = q_in.shape
            t = kv_in.shape[1]
            qh = (q_in @ wq + bq).reshape(b, q_len, H, K)
            kh = (kv_in @ wk + bk).reshape(b, t, H, K)
            vh = (kv_in @ wv + bv).reshape(b, t, H, K)
            kh = jnp.concatenate([kh, jnp.broadcast_to(bias_k, (b, 1, H, K))], axis=1)
            vh = jnp.concatenate([vh, jnp.broadcast_to(bias_v, (b, 1, H, K))], axis=1)
            scale = jnp.sqrt(jnp.asarray(K, q_in.dtype))
            logits = jnp.einsum('bqhk,bthk->bhqt', qh, kh) / scale
            weights = jax.nn.softmax(logits, axis=-1)
            ctx = jnp.einsum('bhqt,bthk->bqhk', weights, vh).reshape(b, q_len, H * K)
            return ctx @ wo + bo

        def _forward(x, xf_1, xf_2, ln1_scale, ln1_offset, wq1, bq1, wk1, bk1, wv1, bv1, wo1, bo1, bias_k1, bias_v1, ln2_scale, ln2_offset, wq2, bq2, wk2, bk2, wv2, bv2, wo2, bo2, bias_k2, bias_v2, ln_mlp_scale, ln_mlp_offset, w_fc1, b_fc1, w_fc2, b_fc2):
            res = x
            h = _layer_norm(x, ln1_scale, ln1_offset)
            x = res + _cross_attention(h, xf_1, wq1, bq1, wk1, bk1, wv1, bv1, wo1, bo1, bias_k1, bias_v1)
            res = x
            h = _layer_norm(x, ln2_scale, ln2_offset)
            x = res + _cross_attention(h, xf_2, wq2, bq2, wk2, bk2, wv2, bv2, wo2, bo2, bias_k2, bias_v2)
            h = _layer_norm(x, ln_mlp_scale, ln_mlp_offset)
            h = jax.nn.gelu(h @ w_fc1 + b_fc1, approximate=False) @ w_fc2 + b_fc2
            return x + h
        key = jax.random.key(seed)
        ks = iter(jax.random.split(key, 64))

        def rn(shape, s=0.02):
            return jax.random.normal(next(ks), shape, jnp.float32) * s
        inp = {'x': rn((B, Q, D), 1.0), 'xf_1': rn((B, S1, D), 1.0), 'xf_2': rn((B, S2, D), 1.0)}
        for i in (1, 2):
            inp[f'ln{i}_scale'] = jnp.ones((D,), jnp.float32)
            inp[f'ln{i}_offset'] = jnp.zeros((D,), jnp.float32)
            inp[f'wq{i}'] = rn((D, H * K))
            inp[f'bq{i}'] = jnp.zeros((H * K,), jnp.float32)
            inp[f'wk{i}'] = rn((D, H * K))
            inp[f'bk{i}'] = jnp.zeros((H * K,), jnp.float32)
            inp[f'wv{i}'] = rn((D, H * K))
            inp[f'bv{i}'] = jnp.zeros((H * K,), jnp.float32)
            inp[f'wo{i}'] = rn((H * K, D))
            inp[f'bo{i}'] = jnp.zeros((D,), jnp.float32)
            inp[f'bias_k{i}'] = rn((1, 1, H, K))
            inp[f'bias_v{i}'] = rn((1, 1, H, K))
        inp['ln_mlp_scale'] = jnp.ones((D,), jnp.float32)
        inp['ln_mlp_offset'] = jnp.zeros((D,), jnp.float32)
        inp['w_fc1'] = rn((D, F))
        inp['b_fc1'] = jnp.zeros((F,), jnp.float32)
        inp['w_fc2'] = rn((F, D))
        inp['b_fc2'] = jnp.zeros((D,), jnp.float32)
        return inp
    _L0_xattn_all = _L0_xattn_setup()
    _L0_xattn_in = {k: v for k, v in _L0_xattn_all.items() if k in ('ln1_scale', 'ln1_offset', 'wq1', 'bq1', 'wk1', 'bk1', 'wv1', 'bv1', 'wo1', 'bo1', 'bias_k1', 'bias_v1', 'ln2_scale', 'ln2_offset', 'wq2', 'bq2', 'wk2', 'bk2', 'wv2', 'bv2', 'wo2', 'bo2', 'bias_k2', 'bias_v2', 'ln_mlp_scale', 'ln_mlp_offset', 'w_fc1', 'b_fc1', 'w_fc2', 'b_fc2')}
    del _L0_xattn_all

    def _L1_xattn_setup():
        import jax, jax.numpy as jnp
        import numpy as np
        B, P, K, H, NH = (4, 256, 32, 256, 16)
        DH = H // NH
        EPS = 1e-06

        def rmsnorm(x, w):
            var = jnp.mean(jnp.square(x), axis=-1, keepdims=True)
            return x * jax.lax.rsqrt(var + EPS) * w
        key = jax.random.key(seed)
        ks = jax.random.split(key, 12)
        s = 0.02
        return {'x': jax.random.normal(ks[0], (B, P, H), jnp.float32), 'latents': jax.random.normal(ks[1], (B, K, H), jnp.float32), 'attention_mask': jax.random.randint(ks[2], (B, P), 0, 2, jnp.int32), 'q_w': s * jax.random.normal(ks[3], (H, H), jnp.float32), 'q_b': jnp.zeros((H,), jnp.float32), 'kv_w': s * jax.random.normal(ks[4], (H, 2 * H), jnp.float32), 'kv_b': jnp.zeros((2 * H,), jnp.float32), 'out_w': s * jax.random.normal(ks[5], (H, H), jnp.float32), 'out_b': jnp.zeros((H,), jnp.float32), 'postnorm_w': jnp.ones((H,), jnp.float32), 'mlp_w1': s * jax.random.normal(ks[6], (H, 4 * H), jnp.float32), 'mlp_b1': jnp.zeros((4 * H,), jnp.float32), 'mlp_w2': s * jax.random.normal(ks[7], (4 * H, H), jnp.float32), 'mlp_b2': jnp.zeros((H,), jnp.float32)}
    _L1_xattn_all = _L1_xattn_setup()
    _L1_xattn_in = {k: v for k, v in _L1_xattn_all.items() if k in ('q_w', 'q_b', 'kv_w', 'kv_b', 'out_w', 'out_b', 'postnorm_w', 'mlp_w1', 'mlp_b1', 'mlp_w2', 'mlp_b2')}
    del _L1_xattn_all
    return {'x': x, 'ctx_2048': ctx_2048, 'mask_BxS2_ik0': mask_BxS2_ik0, 'L0_xattn_ln1_scale': _L0_xattn_in['ln1_scale'], 'L0_xattn_ln1_offset': _L0_xattn_in['ln1_offset'], 'L0_xattn_wq1': _L0_xattn_in['wq1'], 'L0_xattn_bq1': _L0_xattn_in['bq1'], 'L0_xattn_wk1': _L0_xattn_in['wk1'], 'L0_xattn_bk1': _L0_xattn_in['bk1'], 'L0_xattn_wv1': _L0_xattn_in['wv1'], 'L0_xattn_bv1': _L0_xattn_in['bv1'], 'L0_xattn_wo1': _L0_xattn_in['wo1'], 'L0_xattn_bo1': _L0_xattn_in['bo1'], 'L0_xattn_bias_k1': _L0_xattn_in['bias_k1'], 'L0_xattn_bias_v1': _L0_xattn_in['bias_v1'], 'L0_xattn_ln2_scale': _L0_xattn_in['ln2_scale'], 'L0_xattn_ln2_offset': _L0_xattn_in['ln2_offset'], 'L0_xattn_wq2': _L0_xattn_in['wq2'], 'L0_xattn_bq2': _L0_xattn_in['bq2'], 'L0_xattn_wk2': _L0_xattn_in['wk2'], 'L0_xattn_bk2': _L0_xattn_in['bk2'], 'L0_xattn_wv2': _L0_xattn_in['wv2'], 'L0_xattn_bv2': _L0_xattn_in['bv2'], 'L0_xattn_wo2': _L0_xattn_in['wo2'], 'L0_xattn_bo2': _L0_xattn_in['bo2'], 'L0_xattn_bias_k2': _L0_xattn_in['bias_k2'], 'L0_xattn_bias_v2': _L0_xattn_in['bias_v2'], 'L0_xattn_ln_mlp_scale': _L0_xattn_in['ln_mlp_scale'], 'L0_xattn_ln_mlp_offset': _L0_xattn_in['ln_mlp_offset'], 'L0_xattn_w_fc1': _L0_xattn_in['w_fc1'], 'L0_xattn_b_fc1': _L0_xattn_in['b_fc1'], 'L0_xattn_w_fc2': _L0_xattn_in['w_fc2'], 'L0_xattn_b_fc2': _L0_xattn_in['b_fc2'], 'L1_xattn_q_w': _L1_xattn_in['q_w'], 'L1_xattn_q_b': _L1_xattn_in['q_b'], 'L1_xattn_kv_w': _L1_xattn_in['kv_w'], 'L1_xattn_kv_b': _L1_xattn_in['kv_b'], 'L1_xattn_out_w': _L1_xattn_in['out_w'], 'L1_xattn_out_b': _L1_xattn_in['out_b'], 'L1_xattn_postnorm_w': _L1_xattn_in['postnorm_w'], 'L1_xattn_mlp_w1': _L1_xattn_in['mlp_w1'], 'L1_xattn_mlp_b1': _L1_xattn_in['mlp_b1'], 'L1_xattn_mlp_w2': _L1_xattn_in['mlp_w2'], 'L1_xattn_mlp_b2': _L1_xattn_in['mlp_b2']}

def reference(x, ctx_2048, mask_BxS2_ik0, L0_xattn_ln1_scale, L0_xattn_ln1_offset, L0_xattn_wq1, L0_xattn_bq1, L0_xattn_wk1, L0_xattn_bk1, L0_xattn_wv1, L0_xattn_bv1, L0_xattn_wo1, L0_xattn_bo1, L0_xattn_bias_k1, L0_xattn_bias_v1, L0_xattn_ln2_scale, L0_xattn_ln2_offset, L0_xattn_wq2, L0_xattn_bq2, L0_xattn_wk2, L0_xattn_bk2, L0_xattn_wv2, L0_xattn_bv2, L0_xattn_wo2, L0_xattn_bo2, L0_xattn_bias_k2, L0_xattn_bias_v2, L0_xattn_ln_mlp_scale, L0_xattn_ln_mlp_offset, L0_xattn_w_fc1, L0_xattn_b_fc1, L0_xattn_w_fc2, L0_xattn_b_fc2, L1_xattn_q_w, L1_xattn_q_b, L1_xattn_kv_w, L1_xattn_kv_b, L1_xattn_out_w, L1_xattn_out_b, L1_xattn_postnorm_w, L1_xattn_mlp_w1, L1_xattn_mlp_b1, L1_xattn_mlp_w2, L1_xattn_mlp_b2):
    import jax
    import jax.numpy as jnp

    def _L0_xattn_ref(x, xf_1, xf_2, ln1_scale, ln1_offset, wq1, bq1, wk1, bk1, wv1, bv1, wo1, bo1, bias_k1, bias_v1, ln2_scale, ln2_offset, wq2, bq2, wk2, bk2, wv2, bv2, wo2, bo2, bias_k2, bias_v2, ln_mlp_scale, ln_mlp_offset, w_fc1, b_fc1, w_fc2, b_fc2):
        import jax, jax.numpy as jnp
        import numpy as np
        B, Q, S1, S2 = (4, 32, 256, 256)
        D, H, K, F = (256, 16, 128, 1024)
        LN_EPS = 1e-05

        def _layer_norm(x, scale, offset):
            mu = jnp.mean(x, axis=-1, keepdims=True)
            var = jnp.var(x, axis=-1, keepdims=True)
            return (x - mu) * jax.lax.rsqrt(var + LN_EPS) * scale + offset

        def _cross_attention(q_in, kv_in, wq, bq, wk, bk, wv, bv, wo, bo, bias_k, bias_v):
            b, q_len, _ = q_in.shape
            t = kv_in.shape[1]
            qh = (q_in @ wq + bq).reshape(b, q_len, H, K)
            kh = (kv_in @ wk + bk).reshape(b, t, H, K)
            vh = (kv_in @ wv + bv).reshape(b, t, H, K)
            kh = jnp.concatenate([kh, jnp.broadcast_to(bias_k, (b, 1, H, K))], axis=1)
            vh = jnp.concatenate([vh, jnp.broadcast_to(bias_v, (b, 1, H, K))], axis=1)
            scale = jnp.sqrt(jnp.asarray(K, q_in.dtype))
            logits = jnp.einsum('bqhk,bthk->bhqt', qh, kh) / scale
            weights = jax.nn.softmax(logits, axis=-1)
            ctx = jnp.einsum('bhqt,bthk->bqhk', weights, vh).reshape(b, q_len, H * K)
            return ctx @ wo + bo

        def _forward(x, xf_1, xf_2, ln1_scale, ln1_offset, wq1, bq1, wk1, bk1, wv1, bv1, wo1, bo1, bias_k1, bias_v1, ln2_scale, ln2_offset, wq2, bq2, wk2, bk2, wv2, bv2, wo2, bo2, bias_k2, bias_v2, ln_mlp_scale, ln_mlp_offset, w_fc1, b_fc1, w_fc2, b_fc2):
            res = x
            h = _layer_norm(x, ln1_scale, ln1_offset)
            x = res + _cross_attention(h, xf_1, wq1, bq1, wk1, bk1, wv1, bv1, wo1, bo1, bias_k1, bias_v1)
            res = x
            h = _layer_norm(x, ln2_scale, ln2_offset)
            x = res + _cross_attention(h, xf_2, wq2, bq2, wk2, bk2, wv2, bv2, wo2, bo2, bias_k2, bias_v2)
            h = _layer_norm(x, ln_mlp_scale, ln_mlp_offset)
            h = jax.nn.gelu(h @ w_fc1 + b_fc1, approximate=False) @ w_fc2 + b_fc2
            return x + h
        return _forward(x, xf_1, xf_2, ln1_scale, ln1_offset, wq1, bq1, wk1, bk1, wv1, bv1, wo1, bo1, bias_k1, bias_v1, ln2_scale, ln2_offset, wq2, bq2, wk2, bk2, wv2, bv2, wo2, bo2, bias_k2, bias_v2, ln_mlp_scale, ln_mlp_offset, w_fc1, b_fc1, w_fc2, b_fc2)

    def _L1_xattn_ref(x, latents, attention_mask, q_w, q_b, kv_w, kv_b, out_w, out_b, postnorm_w, mlp_w1, mlp_b1, mlp_w2, mlp_b2):
        import jax, jax.numpy as jnp
        import numpy as np
        B, P, K, H, NH = (4, 256, 32, 256, 16)
        DH = H // NH
        EPS = 1e-06

        def rmsnorm(x, w):
            var = jnp.mean(jnp.square(x), axis=-1, keepdims=True)
            return x * jax.lax.rsqrt(var + EPS) * w
        b, p, _ = x.shape
        k_len = latents.shape[1]
        residual = latents
        h = jnp.concatenate([x, latents], axis=1)
        q = (latents @ q_w + q_b).reshape(b, k_len, NH, DH)
        kv = (h @ kv_w + kv_b).reshape(b, p + k_len, NH, DH, 2)
        kmat, v = (kv[..., 0], kv[..., 1])
        attn = jnp.einsum('bkhd,bnhd->bhkn', q, kmat) / DH
        full_mask = jnp.concatenate([attention_mask.astype(bool), jnp.ones((b, k_len), bool)], axis=-1)
        attn = jnp.where(full_mask[:, None, None, :], attn, -jnp.inf)
        attn = jax.nn.softmax(attn.astype(jnp.float32), axis=-1).astype(q.dtype)
        attn_out = jnp.einsum('bhkn,bnhd->bkhd', attn, v).reshape(b, k_len, H)
        attn_out = attn_out @ out_w + out_b + residual
        out = rmsnorm(attn_out, postnorm_w)
        out = jax.nn.gelu(out @ mlp_w1 + mlp_b1) @ mlp_w2 + mlp_b2
        return out + residual
    x = _L0_xattn_ref(x, ctx_2048, ctx_2048, L0_xattn_ln1_scale, L0_xattn_ln1_offset, L0_xattn_wq1, L0_xattn_bq1, L0_xattn_wk1, L0_xattn_bk1, L0_xattn_wv1, L0_xattn_bv1, L0_xattn_wo1, L0_xattn_bo1, L0_xattn_bias_k1, L0_xattn_bias_v1, L0_xattn_ln2_scale, L0_xattn_ln2_offset, L0_xattn_wq2, L0_xattn_bq2, L0_xattn_wk2, L0_xattn_bk2, L0_xattn_wv2, L0_xattn_bv2, L0_xattn_wo2, L0_xattn_bo2, L0_xattn_bias_k2, L0_xattn_bias_v2, L0_xattn_ln_mlp_scale, L0_xattn_ln_mlp_offset, L0_xattn_w_fc1, L0_xattn_b_fc1, L0_xattn_w_fc2, L0_xattn_b_fc2)
    x = _L1_xattn_ref(ctx_2048, x, mask_BxS2_ik0, L1_xattn_q_w, L1_xattn_q_b, L1_xattn_kv_w, L1_xattn_kv_b, L1_xattn_out_w, L1_xattn_out_b, L1_xattn_postnorm_w, L1_xattn_mlp_w1, L1_xattn_mlp_b1, L1_xattn_mlp_w2, L1_xattn_mlp_b2)
    return x

_drawn_inputs = setup_inputs


def setup_inputs(seed=0):
    import zlib

    import numpy as np

    out = dict(_drawn_inputs(seed))
    spreads = {'L0_xattn_ln1_scale': (1.0, 0.6),
     'L0_xattn_ln1_offset': (0.0, 0.8),
     'L0_xattn_bq1': (0.0, 0.8),
     'L0_xattn_bk1': (0.0, 2.0),
     'L0_xattn_bv1': (0.0, 0.1),
     'L0_xattn_bo1': (0.0, 0.1),
     'L0_xattn_ln2_scale': (1.0, 0.6),
     'L0_xattn_ln2_offset': (0.0, 0.8),
     'L0_xattn_bq2': (0.0, 0.8),
     'L0_xattn_bk2': (0.0, 2.0),
     'L0_xattn_bv2': (0.0, 0.1),
     'L0_xattn_bo2': (0.0, 0.1),
     'L0_xattn_ln_mlp_scale': (1.0, 0.6),
     'L0_xattn_ln_mlp_offset': (0.0, 0.693),
     'L0_xattn_b_fc1': (0.0, 0.1),
     'L0_xattn_b_fc2': (0.0, 0.1),
     'L1_xattn_q_b': (0.0, 0.8),
     'L1_xattn_kv_b': (0.0, 0.8),
     'L1_xattn_out_b': (0.0, 2.0),
     'L1_xattn_postnorm_w': (1.0, 0.6),
     'L1_xattn_mlp_b1': (0.0, 0.1),
     'L1_xattn_mlp_b2': (0.0, 0.1)}
    factors = {'L0_xattn_wq1': 8.0,
     'L0_xattn_wk1': 8.0,
     'L0_xattn_bias_k1': 64.0,
     'L0_xattn_bias_v1': 54.627,
     'L0_xattn_wq2': 8.0,
     'L0_xattn_wk2': 8.0,
     'L0_xattn_bias_k2': 64.0,
     'L0_xattn_bias_v2': 64.0,
     'L1_xattn_q_w': 8.0,
     'L1_xattn_kv_w': 8.0,
     'L1_xattn_out_w': 8.0}
    for name, (base, spread) in spreads.items():
        noise = np.random.default_rng([zlib.crc32(name.encode()), seed]).standard_normal(out[name].shape)
        drawn = base * np.exp(spread * noise) if base else spread * noise
        out[name] = jnp.asarray(drawn.astype(out[name].dtype))
    for name, factor in factors.items():
        out[name] = (out[name] * factor).astype(out[name].dtype)
    return out
```

```python
from contextlib import ExitStack

import concourse.bass as bass
from concourse import mybir

ALU = mybir.AluOpType
ACT = mybir.ActivationFunctionType
F32 = mybir.dt.float32
F32R = mybir.dt.float32r
BF16 = mybir.dt.bfloat16
I32 = mybir.dt.int32
AX_X = mybir.AxisListType.X

B, S, D = 32, 64, 256
TOK = B * S
P = 128
NT = TOK // P
DC = D // P
H, K = 16, 128
HP = H // 2
NL = 2
G = 4
GT = NT // G
GTOK = TOK // G
UNITS = HP * G
F = 1024
FC = F // P
NH, DH = 16, 16
KEYS = S + 1
LN_EPS, RMS_EPS = 1e-5, 1e-6
MASKED = -1e30
ROWS_H = 5 * NL * H
LNP = 6
C_M0 = NL * LNP
C_QB = C_M0 + 12
C_KB = C_QB + 2
C_VB = C_KB + 2
C_PN = C_VB + 2
C_B1 = C_PN + 2
ROWS_M = C_B1 + 8
OLD = 8


def program(nc, x, ctx_in, mask, wall, vech, vecm, fc1, fc2, b_fc2, qw, kw, vw, ow, out_b, w1, w2, b2, out):
    es = ExitStack()
    with es:
        def sem(name):
            return es.enter_context(nc.semaphore(name))

        def sb(name, shape, dt=F32, scope=es):
            return scope.enter_context(nc.sbuf_tensor(name, shape, dt))

        bank = [es.enter_context(nc.psum_tensor(f"bank{i}", [P, 512], F32)) for i in range(5)]
        logits = es.enter_context(nc.psum_tensor("logits", [P, 2, 512], F32))
        bank += [None, None, es.enter_context(nc.psum_tensor("bank7", [P, 512], F32))]
        PROJ = [bank[0], bank[1], bank[2], bank[7]]
        WIDE = PROJ + [logits[:, 0, :], logits[:, 1, :]]

        X = sb("X", [P, NT, D])
        SRC_HI = sb("SRC_HI", [P, 2, DC, TOK], F32R)
        SRC_LO = sb("SRC_LO", [P, 2, DC, TOK], F32R)
        ident = sb("ident", [P, P])
        PH = sb("PH", [P, 5, NL * H])
        PM = sb("PM", [P, ROWS_M])
        st = sb("st", [P, NT, 6])
        mv = sb("mv", [P, NT, 2])
        ms = sb("ms", [P, NT])
        sd = sb("sd", [P, NT])
        rs = sb("rs", [P, NT])
        XN = sb("XN", [P, 2, GT, D])
        HT = sb("HT", [P, 2, 512])

        class Norm:
            def __init__(self, tag, src, rms, eps, prm):
                self.src, self.rms, self.eps, self.prm = src, rms, eps, prm
                self.stat, self.sqrt, self.rstd = sem(tag + "_stat"), sem(tag + "_sqrt"), sem(tag + "_rstd")
                self.xn, self.turned, self.scaled = sem(tag + "_xn"), sem(tag + "_turned"), sem(tag + "_scaled")
                self.hi, self.lo = sem(tag + "_hi"), sem(tag + "_lo")
                self.stats = 2 * NT + (3 if rms else 1)

        def norm_vector(e, n, k):
            at = k * n.stats
            for t in range(NT):
                e.bn_stats(st[:, t, :], n.src[:, t, :]).then_inc(n.stat, 1)
            e.wait_ge(n.stat, at + NT)
            e.memset(ms[:, :], n.eps)
            for t in range(NT):
                e.bn_aggr(mv[:, t, :], st[:, t, :]).then_inc(n.stat, 1)
            e.wait_ge(n.stat, at + 2 * NT)
            if n.rms:
                e.tensor_tensor(mv[:, :, 0], mv[:, :, 0], mv[:, :, 0], ALU.mult).then_inc(n.stat, 1)
                e.wait_ge(n.stat, at + 2 * NT + 1)
                e.tensor_tensor(mv[:, :, 1], mv[:, :, 0], mv[:, :, 1], ALU.add).then_inc(n.stat, 1)
                e.wait_ge(n.stat, at + 2 * NT + 2)
            e.tensor_tensor(ms[:, :], mv[:, :, 1], ms[:, :], ALU.add).then_inc(n.stat, 1)
            e.wait_ge(n.sqrt, k + 1)
            e.reciprocal(rs[:, :], sd[:, :]).then_inc(n.rstd, 1)
            e.wait_ge(n.rstd, k + 1)

            def round_group(g):
                for c in range(DC):
                    e.wait_ge(n.scaled, (k * G + g) * DC + c + 1)
                    e.tensor_copy(SRC_HI[:, 1, c, g * GTOK:(g + 1) * GTOK], HT[:, c, :]).then_inc(n.hi, 1)

            for g in range(G):
                if g >= 2:
                    e.wait_ge(n.turned, (k * G + g - 1) * DC)
                for p in range(GT):
                    t = g * GT + p
                    if n.rms:
                        i = e.tensor_scalar(XN[:, g % 2, p, :], n.src[:, t, :], rs[:, t:t + 1], None, ALU.mult)
                    else:
                        i = e.tensor_scalar(XN[:, g % 2, p, :], n.src[:, t, :], mv[:, t, 0:1], rs[:, t:t + 1],
                                            ALU.subtract, ALU.mult)
                i.then_inc(n.xn, 1)
                if g >= 1:
                    round_group(g - 1)
            round_group(G - 1)

        def norm_scalar(e, n, k):
            e.wait_ge(n.stat, (k + 1) * n.stats)
            e.activation(sd[:, :], ms[:, :], ACT.Sqrt).then_inc(n.sqrt, 1)
            for g in range(G):
                for c in range(DC):
                    q = (k * G + g) * DC + c
                    e.wait_ge(n.turned, q + 1)
                    if g >= 1:
                        e.wait_ge(n.lo, q - 1)
                    piece = PROJ[2 * (g % 2) + c][:, :]
                    if n.rms:
                        i = e.activation(HT[:, c, :], piece, ACT.Copy, scale=n.prm[:, c:c + 1])
                    else:
                        i = e.activation(HT[:, c, :], piece, ACT.Identity, scale=n.prm[:, c:c + 1],
                                         bias=n.prm[:, 2 + c:3 + c])
                    i.then_inc(n.scaled, 1)

        def norm_gpsimd(e, n, k):
            for g in range(G):
                for c in range(DC):
                    e.wait_ge(n.hi, (k * G + g) * DC + c + 1)
                    toks = slice(g * GTOK, (g + 1) * GTOK)
                    e.tensor_tensor(SRC_LO[:, 1, c, toks], HT[:, c, :], SRC_HI[:, 1, c, toks].bitcast(F32),
                                    ALU.subtract).then_inc(n.lo, 1)

        def norm_tensor(e, n, k):
            for g in range(G):
                e.wait_ge(n.xn, k * G + g + 1)
                if g >= 2:
                    e.wait_ge(n.scaled, (k * G + g - 1) * DC)
                for c in range(DC):
                    for p in range(GT):
                        i = e.transpose(PROJ[2 * (g % 2) + c][:, p * P:(p + 1) * P],
                                        XN[:, g % 2, p, c * P:(c + 1) * P], ident[:, :])
                    i.then_inc(n.turned, 1)
            e.wait_ge(n.lo, (k + 1) * G * DC)

        def three(e, dst, a_hi, a_lo, b_hi, b_lo, start, stop, **kw):
            e.matmul(dst, a_hi, b_hi, start=start, stop=False, **kw)
            e.matmul(dst, a_hi, b_lo, start=False, stop=False, **kw)
            return e.matmul(dst, a_lo, b_hi, start=False, stop=stop, **kw)

        with ExitStack() as ph:
            cin = sb("cin", [P, NT, D], scope=ph)
            vh = sb("vh", [ROWS_H // 2, 2, P], scope=ph)
            vm = sb("vm", [ROWS_M, P], scope=ph)
            one = sb("one", [P, P], scope=ph)
            vec_in, x_in = sem("vec_in"), sem("x_in")
            ctx_g = [sem(f"ctx_in{g}") for g in range(G)]
            ident_one, ident_done = sem("ident_one"), sem("ident_done")
            vec_turned, vec_copied = sem("vec_turned"), sem("vec_copied")
            ctx_turned, ctx_hi, ctx_lo = sem("ctx_turned"), sem("ctx_hi"), sem("ctx_lo")
            with nc.Block() as block:
                @block.sync
                def _(e):
                    xt = ctx_in.rearrange("(t p) d -> p t d", p=P)
                    for g in range(G):
                        e.dma_start(cin[:, g * GT:(g + 1) * GT, :], xt[:, g * GT:(g + 1) * GT, :]).then_inc(ctx_g[g], 16)
                    e.dma_start(X[:, :, :], x.rearrange("(t p) d -> p t d", p=P)).then_inc(x_in, 16)
                    e.wait_ge(x_in, 16)

                @block.scalar
                def _(e):
                    e.dma_start(vh[:, :, :], vech.rearrange("(a r) k -> r a k", a=2)).then_inc(vec_in, 16)
                    e.dma_start(vm[:, :], vecm).then_inc(vec_in, 16)
                    for g in range(G):
                        for c in range(DC):
                            e.wait_ge(ctx_turned, g * DC + c + 1)
                            e.activation(SRC_HI[:, 0, c, g * GTOK:(g + 1) * GTOK], PROJ[2 * (g % 2) + c][:, :],
                                         ACT.Copy).then_inc(ctx_hi, 1)

                @block.gpsimd
                def _(e):
                    e.memset(one[:, :], 1.0).then_inc(ident_one, 1)
                    e.wait_ge(ident_one, 1)
                    e.affine_select(out=ident[:, :], in_=one[:, :], compare_op=ALU.is_equal, fill=0.0, base=0,
                                    pattern=[[-1, P]], channel_multiplier=1).then_inc(ident_done, 1)

                @block.vector
                def _(e):
                    e.wait_ge(vec_turned, 1)
                    half = ROWS_H // 2
                    e.tensor_copy(PH[:, :, :].rearrange("p j h -> p (j h)"),
                                  bank[3][:, 0:ROWS_H]).then_inc(vec_copied, 1)
                    e.tensor_copy(PM[:, :], bank[3][:, ROWS_H:ROWS_H + ROWS_M]).then_inc(vec_copied, 1)
                    for g in range(G):
                        for c in range(DC):
                            e.wait_ge(ctx_hi, g * DC + c + 1)
                            dst = (slice(None), 0, c, slice(g * GTOK, (g + 1) * GTOK))
                            e.tensor_tensor(SRC_LO[dst], PROJ[2 * (g % 2) + c][:, :], SRC_HI[dst].bitcast(F32),
                                            ALU.subtract).then_inc(ctx_lo, 1)

                @block.tensor
                def _(e):
                    e.wait_ge(ident_done, 1)
                    e.wait_ge(vec_in, 32)
                    half = ROWS_H // 2
                    for a in range(2):
                        e.transpose(bank[3][:, a * half:(a + 1) * half], vh[:, a, :], ident[0:half, 0:half])
                    e.transpose(bank[3][:, ROWS_H:ROWS_H + ROWS_M], vm[:, :],
                                ident[0:ROWS_M, 0:ROWS_M]).then_inc(vec_turned, 1)
                    for g in range(G):
                        e.wait_ge(ctx_g[g], 16)
                        if g >= 2:
                            e.wait_ge(ctx_lo, (g - 1) * DC)
                        for c in range(DC):
                            for p in range(GT):
                                i = e.transpose(PROJ[2 * (g % 2) + c][:, p * P:(p + 1) * P],
                                                cin[:, g * GT + p, c * P:(c + 1) * P], ident[:, :])
                            i.then_inc(ctx_turned, 1)

        with ExitStack() as ph:
            W = [sb(f"W{a}", [P, 4, DC, 256], scope=ph) for a in range(2)]
            WHI = [sb(f"WHI{a}", [P, 4, DC, 256], F32R, scope=ph) for a in range(2)]
            WLO = [sb(f"WLO{a}", [P, 4, DC, 256], F32R, scope=ph) for a in range(2)]
            PB = [sb(f"PB{a}", [P, 5, 2], scope=ph) for a in range(2)]
            E2 = [sb(f"E2{a}", [P, 2, 32], scope=ph) for a in range(2)]
            EA = sb("EA", [P, NL * H, 32], scope=ph)
            EB = sb("EB", [P, NL * H, 32], scope=ph)
            BWT = sb("BWT", [P, DC, 32], scope=ph)
            BW = sb("BW", [32, D], scope=ph)
            PTB = sb("PTB", [P, NT, 32], scope=ph)
            PTT = sb("PTT", [32, 2, 512], scope=ph)
            CUR = sb("CUR", [P, LNP], scope=ph)
            QT = sb("QT", [P, 2, GTOK], scope=ph)
            KT = sb("KT", [P, 2, GTOK // S, KEYS], scope=ph)
            V = [sb(f"V{a}", [P, GT, 256], scope=ph) for a in range(2)]
            mx = sb("mx", [P, 2 * GT], scope=ph)
            sub = sb("sub", [P, 2 * GT, KEYS], scope=ph)
            ex = sb("ex", [P, 2 * GT, KEYS], scope=ph)
            sm = sb("sm", [P, 2 * GT], scope=ph)
            ri = sb("ri", [P, 2 * GT], scope=ph)
            PD = sb("PD", [P, 2 * GT, P], scope=ph)
            PTS = sb("PTS", [P, 2, 512], scope=ph)
            CHI = sb("CHI", [P, 2, GTOK], F32R, scope=ph)
            CLO = sb("CLO", [P, 2, GTOK], F32R, scope=ph)
            norm = Norm("ln", X, False, LN_EPS, CUR)
            SCALE = float(K) ** -0.5
            BWTN = HP + 2

            w_in = [sem(f"w_in{a}") for a in range(2)]
            w_split, w_hi, bw_done = sem("w_split"), sem("w_hi"), sem("bw_done")
            e_made, cur_set = sem("e_made"), sem("cur_set")
            q_done, k_done, v_done, s_done = sem("q_done"), sem("k_done"), sem("v_done"), sem("s_done")
            t_done, c_done, o_done = sem("t_done"), sem("c_done"), sem("o_done")
            q_out, k_out, v_out, exp_done = sem("q_out"), sem("k_out"), sem("v_out"), sem("exp_done")
            pt_out, c_hi, c_lo, kb_set = sem("pt_out"), sem("c_hi"), sem("c_lo"), sem("kb_set")
            mx_done, sub_done, sm_done, ri_done = sem("mx_done"), sem("sub_done"), sem("sm_done"), sem("ri_done")
            p_ready, x_settled, bwt_sum = sem("p_ready"), sem("x_settled"), sem("bwt_sum")
            bw_turned, bw_out, ptb_turned, ptb_out = sem("bw_turned"), sem("bw_out"), sem("ptb_turned"), sem("ptb_out")
            bias_done, bias_added = sem("bias_done"), sem("bias_added")

            def slots(e, L, slot):
                slot(L, L * UNITS, 0, L * HP, None)
                with e.Fori(0, UNITS // OLD - 1) as i:
                    for u in range(OLD):
                        slot(L, L * UNITS + i * OLD + u + 1, u + 1, L * HP + i * 2 + (u + 1) // G, i * 2 + u // G)
                i = UNITS // OLD - 1
                for u in range(OLD):
                    slot(L, L * UNITS + i * OLD + u + 1, u + 1,
                         L * HP + i * 2 + (u + 1) // G if u < OLD - 1 else None, i * 2 + u // G)

            with nc.Block() as block:
                @block.sync
                def _(e):
                    for a in range(2):
                        e.dma_start(W[a][:, :, :, :],
                                    wall[a].rearrange("j (c p) n -> p j c n", p=P)).then_inc(w_in[a], 16)
                    with e.Fori(1, NL * HP // 2) as i:
                        for a in range(2):
                            m = i * 2
                            e.wait_ge(w_split, m + a - 1)
                            e.wait_ge(bw_done, m + a - 1)
                            e.dma_start(W[a][:, :, :, :], wall[m + a].rearrange("j (c p) n -> p j c n", p=P)
                                        ).then_inc(w_in[a], 16)

                @block.gpsimd
                def _(e):
                    def split(m, a):
                        e.tensor_tensor(E2[a][:, :, :], EA[:, bass.ds(2 * m, 2), :], EB[:, bass.ds(2 * m, 2), :],
                                        ALU.subtract)
                        e.tensor_copy(PB[a][:, :, :], PH[:, :, bass.ds(2 * m, 2)])
                        for j in range(4):
                            i = e.tensor_copy(WHI[a][:, j, :, :], W[a][:, j, :, :])
                        i.then_inc(w_hi, 1)
                        e.wait_ge(w_hi, m + 1)
                        for j in range(4):
                            i = e.tensor_tensor(WLO[a][:, j, :, :], W[a][:, j, :, :],
                                                WHI[a][:, j, :, :].bitcast(F32), ALU.subtract)
                        i.then_inc(w_split, 1)

                    e.wait_ge(e_made, 3)
                    for a in range(2):
                        e.wait_ge(w_in[a], 16)
                        split(a, a)
                    for L in range(NL):
                        norm_gpsimd(e, norm, L)
                        with e.Fori(HP * L // 2 + 1, min(HP * (L + 1) // 2 + 1, NL * HP // 2)) as i:
                            for a in range(2):
                                m = i * 2
                                e.wait_ge(w_in[a], 8 * m + 16)
                                e.wait_ge(o_done, 2 * G * (m + a - 1))
                                split(m + a, a)

                @block.tensor
                def _(e):
                    def slot(L, n, at, pair, hp):
                        g, a, ab = at % G, (at // G) % 2, ((at - 1) // G) % 2
                        front, back = pair is not None, hp is not None
                        toks = slice(g * GTOK, (g + 1) * GTOK)
                        if front:
                            if g == 0:
                                e.wait_ge(w_split, pair + 1)
                            for j, half, done, free in ((0, 1, q_done, v_out), (1, 0, k_done, k_out)):
                                for h in range(2):
                                    if back:
                                        e.wait_ge(free, 2 * n - 1 + h)
                                    for c in range(DC):
                                        i = three(e, PROJ[2 * j + h][:, :], WHI[a][:, j, c, h * K:(h + 1) * K],
                                                  WLO[a][:, j, c, h * K:(h + 1) * K], SRC_HI[:, half, c, toks],
                                                  SRC_LO[:, half, c, toks], c == 0, c == DC - 1)
                                    i.then_inc(done, 1)
                        if back:
                            e.wait_ge(p_ready, n)
                            e.wait_ge(x_settled, 2 * n)
                            for h in range(2):
                                for p in range(GT):
                                    i = e.transpose(bank[3 + h][:, p * P:(p + 1) * P], PD[:, h * GT + p, :],
                                                    ident[:, :])
                                i.then_inc(t_done, 1)
                        if front:
                            for j in range(2):
                                e.wait_ge(q_out, 2 * n + j + 1)
                                for p in range(2):
                                    t = g * GT + 2 * j + p
                                    for c in range(DC):
                                        i = three(e, PROJ[j][:, p * 256:(p + 1) * 256],
                                                  SRC_HI[:, 0, c, t * P:(t + 1) * P], SRC_LO[:, 0, c, t * P:(t + 1) * P],
                                                  WHI[a][:, 2, c, :], WLO[a][:, 2, c, :], c == 0, c == DC - 1)
                                i.then_inc(v_done, 1)
                        if back:
                            e.wait_ge(v_out, 2 * n)
                            for h in range(2):
                                e.wait_ge(pt_out, 2 * n - 1 + h)
                                for p in range(GT):
                                    i = e.matmul(bank[3 + h][:, p * P:(p + 1) * P],
                                                 V[(at - 1) % 2][:, p, h * K:(h + 1) * K],
                                                 PTS[:, h, p * P:(p + 1) * P], start=True, stop=True)
                                i.then_inc(c_done, 1)
                        if front:
                            e.wait_ge(q_out, 2 * n + 2)
                            e.wait_ge(k_out, 2 * n + 2)
                            e.wait_ge(kb_set, n + 1)
                            if back:
                                e.wait_ge(sub_done, n)
                            if g == G - 1:
                                for c in range(DC):
                                    for h in range(2):
                                        i = e.matmul(logits[:, 1, 448 + 32 * c:480 + 32 * c],
                                                     W[a][:, 3, h, c * P:(c + 1) * P], E2[a][:, h, :],
                                                     start=(h == 0), stop=(h == 1))
                                i.then_inc(bw_done, 1)
                            for h in range(2):
                                for q in range(GTOK // S):
                                    p, b = q // 2, q % 2
                                    i = e.matmul(logits[b * S:(b + 1) * S, h, p * KEYS:(p + 1) * KEYS],
                                                 QT[:, h, q * S:(q + 1) * S], KT[:, h, q, :], start=True, stop=True)
                            i.then_inc(s_done, 1)
                        if back:
                            e.wait_ge(c_lo, 2 * n)
                            for j in range(2):
                                for p in range(2):
                                    for h in range(2):
                                        ts = slice((2 * j + p) * P, (2 * j + p + 1) * P)
                                        i = three(e, bank[3 + j][:, p * 256:(p + 1) * 256], CHI[:, h, ts], CLO[:, h, ts],
                                                  WHI[ab][:, 3, h, :], WLO[ab][:, 3, h, :], h == 0, h == 1)
                                i.then_inc(o_done, 1)

                    with e.Fori(0, NL) as L:
                        norm_tensor(e, norm, L)
                        slots(e, L, slot)
                        e.wait_ge(bwt_sum, (L + 1) * BWTN)
                        e.wait_ge(x_settled, (L + 1) * UNITS * 2 + 2)
                        for c in range(DC):
                            i = e.transpose(bank[3][0:32, c * P:(c + 1) * P], BWT[:, c, :], ident[:, :])
                        i.then_inc(bw_turned, 1)
                        for g in range(G):
                            if g >= 2:
                                e.wait_ge(ptb_out, L * G + g - 1)
                            for p in range(GT):
                                i = e.transpose(bank[g % 2][0:32, p * P:(p + 1) * P], PTB[:, g * GT + p, :], ident[:, :])
                            i.then_inc(ptb_turned, 1)
                            e.wait_ge(bw_out, L + 1)
                            e.wait_ge(ptb_out, L * G + g + 1)
                            for j in range(2):
                                if g >= 1:
                                    e.wait_ge(bias_added, 2 * (L * G + g) - 1 + j)
                                for p in range(2):
                                    i = e.matmul(PROJ[2 + j][:, p * 256:(p + 1) * 256],
                                                 PTT[:, g % 2, (2 * j + p) * P:(2 * j + p + 1) * P], BW[:, :],
                                                 start=True, stop=True)
                                i.then_inc(bias_done, 1)

                @block.scalar
                def _(e):
                    def slot(L, n, at, pair, hp):
                        a = (at // G) % 2
                        front, back = pair is not None, hp is not None
                        if front:
                            for h in range(2):
                                e.wait_ge(q_done, 2 * n + h + 1)
                                e.activation(QT[:, h, :], PROJ[h][:, :], ACT.Identity,
                                             bias=PB[a][:, 0, h:h + 1]).then_inc(q_out, 1)
                            for h in range(2):
                                e.wait_ge(k_done, 2 * n + h + 1)
                                e.activation(KT[:, h, :, 0:S], PROJ[2 + h][:, :].rearrange("p (q k) -> p q k", k=S),
                                             ACT.Identity, bias=PB[a][:, 1, h:h + 1]).then_inc(k_out, 1)
                        if back:
                            for h in range(2):
                                e.wait_ge(t_done, 2 * n - 1 + h)
                                e.activation(PTS[:, h, :], bank[3 + h][:, :], ACT.Copy).then_inc(pt_out, 1)
                        if front:
                            for j in range(2):
                                e.wait_ge(v_done, 2 * n + j + 1)
                                e.activation(V[at % 2][:, 2 * j:2 * j + 2, :],
                                             PROJ[j][:, :].rearrange("p (t n) -> p t n", n=256),
                                             ACT.Copy).then_inc(v_out, 1)
                        if back:
                            for h in range(2):
                                e.wait_ge(c_done, 2 * n - 1 + h)
                                e.activation(CHI[:, h, :], bank[3 + h][:, :], ACT.Copy).then_inc(c_hi, 1)
                        if front:
                            e.wait_ge(sub_done, n + 1)
                            e.activation(ex[:, :, :], sub[:, :, :], ACT.Exp, scale=SCALE).then_inc(exp_done, 1)

                    with e.Fori(0, NL) as L:
                        e.wait_ge(cur_set, L + 1)
                        norm_scalar(e, norm, L)
                        slots(e, L, slot)
                        for g in range(G):
                            e.wait_ge(ptb_turned, L * G + g + 1)
                            e.activation(PTT[:, g % 2, :], bank[g % 2][0:32, :], ACT.Copy).then_inc(ptb_out, 1)

                @block.vector
                def _(e):
                    logit = logits[:, :, 0:GT * KEYS].rearrange("p h (t k) -> p h t k", k=KEYS)

                    def slot(L, n, at, pair, hp):
                        g, a, gb = at % G, (at // G) % 2, (at - 1) % G
                        front, back = pair is not None, hp is not None
                        if front:
                            if g == 0:
                                e.wait_ge(w_split, pair + 1)
                            e.tensor_copy(KT[:, :, :, S], PB[a][:, 2, :].unsqueeze(2).to_broadcast([P, 2, GTOK // S])
                                          ).then_inc(kb_set, 1)
                        if back:
                            e.wait_ge(exp_done, n)
                            e.tensor_reduce(sm[:, :], ex[:, :, :], AX_X, ALU.add).then_inc(sm_done, 1)
                            e.wait_ge(sm_done, n)
                            e.reciprocal(ri[:, :], sm[:, :]).then_inc(ri_done, 1)
                            e.wait_ge(ri_done, n)
                            e.tensor_tensor(PTB[:, gb * GT:(gb + 1) * GT, bass.ds(2 * hp, 2)].rearrange("p t h -> p h t"),
                                            ex[:, :, S].rearrange("p (h t) -> p h t", h=2),
                                            ri[:, :].rearrange("p (h t) -> p h t", h=2), ALU.mult)
                            for b in range(2):
                                r = slice(b * S, (b + 1) * S)
                                i = e.tensor_tensor(PD[r, :, r], ex[r, :, 0:S],
                                                    ri[r, :].unsqueeze(2).to_broadcast([S, 2 * GT, S]), ALU.mult)
                            i.then_inc(p_ready, 1)
                            for h in range(2):
                                e.wait_ge(c_hi, 2 * n - 1 + h)
                                e.tensor_tensor(CLO[:, h, :], bank[3 + h][:, :], CHI[:, h, :].bitcast(F32),
                                                ALU.subtract).then_inc(c_lo, 1)
                        if front:
                            e.wait_ge(s_done, n + 1)
                            if g == G - 1:
                                e.wait_ge(bwt_sum, (BWTN - HP) * L + 2 + pair)
                                e.tensor_tensor(BWT[:, :, :], BWT[:, :, :],
                                                logits[:, 1, 448:512].rearrange("p (c n) -> p c n", n=32),
                                                ALU.add).then_inc(bwt_sum, 1)
                            e.tensor_reduce(mx[:, :].rearrange("p (h t) -> p h t", h=2), logit, AX_X,
                                            ALU.max).then_inc(mx_done, 1)
                            e.wait_ge(mx_done, n + 1)
                            e.tensor_tensor(sub[:, :, :].rearrange("p (h t) k -> p h t k", h=2), logit,
                                            mx[:, :].rearrange("p (h t) -> p h t", h=2).unsqueeze(3)
                                            .to_broadcast([P, 2, GT, KEYS]), ALU.subtract).then_inc(sub_done, 1)
                        if back:
                            for j in range(2):
                                e.wait_ge(o_done, 2 * n - 1 + j)
                                xs = X[:, gb * GT + 2 * j:gb * GT + 2 * j + 2, :]
                                e.tensor_tensor(xs, xs, bank[3 + j][:, :].rearrange("p (t n) -> p t n", n=256),
                                                ALU.add).then_inc(x_settled, 1)

                    e.memset(EA[:, :, :], 0.0).then_inc(e_made, 1)
                    e.memset(EB[:, :, :], 0.0).then_inc(e_made, 1)
                    e.memset(PD[:, :, :], 0.0)
                    e.memset(PTB[:, :, :], 1.0).then_inc(x_settled, 2)
                    e.wait_ge(e_made, 2)
                    for t, j in ((EA, 4), (EB, 3)):
                        flat = t[:, :, :].rearrange("p m n -> p (m n)")
                        for L in range(NL):
                            e.tensor_copy(flat[:, L * H * 32:L * H * 32 + (H - 1) * 33 + 1:33],
                                          PH[:, j, L * H:(L + 1) * H])
                    e.tensor_scalar(EB[:, :, H], PH[:, 3, :], -1.0, None, ALU.mult).then_inc(e_made, 1)
                    with e.Fori(0, NL) as L:
                        e.wait_ge(x_settled, 2 * UNITS * L + 2)
                        e.tensor_copy(CUR[:, :], PM[:, bass.ds(L * LNP, LNP)]).then_inc(cur_set, 1)
                        e.memset(BWT[:, :, :], 0.0).then_inc(bwt_sum, 1)
                        e.wait_ge(cur_set, L + 1)
                        e.wait_ge(bwt_sum, BWTN * L + 1)
                        e.tensor_copy(BWT[:, :, H + 1], CUR[:, 4:6]).then_inc(bwt_sum, 1)
                        norm_vector(e, norm, L)
                        slots(e, L, slot)
                        e.wait_ge(bw_turned, L + 1)
                        e.tensor_copy(BW[:, :], bank[3][0:32, 0:D]).then_inc(bw_out, 1)
                        for g in range(G):
                            for j in range(2):
                                e.wait_ge(bias_done, 2 * (L * G + g) + j + 1)
                                xs = X[:, g * GT + 2 * j:g * GT + 2 * j + 2, :]
                                e.tensor_tensor(xs, xs, PROJ[2 + j][:, :].rearrange("p (t n) -> p t n", n=256),
                                                ALU.add).then_inc(bias_added, 1)
                        e.wait_ge(bias_added, 2 * G * (L + 1))

        def mlp(tag, norm, b1, w1d, w2d, b2d, func, dst):
            with ExitStack() as ph:
                w1r, w2r = sb(tag + "w1r", [P, DC, F], scope=ph), sb(tag + "w2r", [P, FC, D], scope=ph)
                w1h, w2h = sb(tag + "w1h", [P, DC, F], F32R, scope=ph), sb(tag + "w2h", [P, FC, D], F32R, scope=ph)
                w1l, w2l = sb(tag + "w1l", [P, DC, F], F32R, scope=ph), sb(tag + "w2l", [P, FC, D], F32R, scope=ph)
                b2b = sb(tag + "b2b", [P, D], scope=ph)
                gf = sb(tag + "gf", [P, 2, 512], scope=ph)
                gh, gl = sb(tag + "gh", [P, 2, 512], F32R, scope=ph), sb(tag + "gl", [P, 2, 512], F32R, scope=ph)
                w1_in, w2_in, b2_in = sem(tag + "w1_in"), sem(tag + "w2_in"), sem(tag + "b2_in")
                w_hi, w_lo = sem(tag + "w_hi"), sem(tag + "w_lo")
                up_done, g_full, g_hi, g_lo = sem(tag + "up"), sem(tag + "full"), sem(tag + "hi"), sem(tag + "lo")
                down_used, y_added, b2_added = sem(tag + "dn"), sem(tag + "ya"), sem(tag + "b2a")
                stored = sem(tag + "st")
                with nc.Block() as block:
                    @block.sync
                    def _(e):
                        e.dma_start(w1r[:, :, :], w1d.rearrange("(c p) f -> p c f", p=P)).then_inc(w1_in, 16)
                        e.dma_start(w2r[:, :, :], w2d.rearrange("(c p) f -> p c f", p=P)).then_inc(w2_in, 16)
                        e.dma_start(b2b[:, :], b2d.partition_broadcast(P)).then_inc(b2_in, 16)
                        if dst is not None:
                            for g in range(G):
                                e.wait_ge(y_added, 2 * (g + 1))
                                e.dma_start(dst[:, g * GT:(g + 1) * GT, :], X[:, g * GT:(g + 1) * GT, :]).then_inc(stored, 16)
                            e.wait_ge(stored, 16 * G)

                    @block.gpsimd
                    def _(e):
                        for w, (r, h, l, there) in enumerate(((w1r, w1h, w1l, w1_in), (w2r, w2h, w2l, w2_in))):
                            e.wait_ge(there, 16)
                            e.tensor_copy(h[:, :, :], r[:, :, :]).then_inc(w_hi, 1)
                            e.wait_ge(w_hi, w + 1)
                            e.tensor_tensor(l[:, :, :], r[:, :, :], h[:, :, :].bitcast(F32), ALU.subtract).then_inc(w_lo, 1)
                        norm_gpsimd(e, norm, 0)
                        with e.Fori(0, G) as g:
                            for j in range(FC):
                                q = g * FC + j
                                e.wait_ge(g_hi, q + 1)
                                e.tensor_tensor(gl[:, j % 2, :], gf[:, j % 2, :], gh[:, j % 2, :].bitcast(F32),
                                                ALU.subtract).then_inc(g_lo, 1)

                    @block.scalar
                    def _(e):
                        norm_scalar(e, norm, 0)
                        with e.Fori(0, G) as g:
                            for j in range(FC):
                                q = g * FC + j
                                e.wait_ge(up_done, q + 1)
                                if j >= 2:
                                    e.wait_ge(g_lo, q - 1)
                                e.activation(gf[:, j % 2, :], PROJ[j % 4][:, :], func,
                                             bias=b1[:, j:j + 1]).then_inc(g_full, 1)

                    @block.vector
                    def _(e):
                        norm_vector(e, norm, 0)
                        e.wait_ge(b2_in, 16)
                        for g in range(G):
                            xs = X[:, g * GT:(g + 1) * GT, :]
                            e.tensor_tensor(xs, xs, b2b[:, :].unsqueeze(1).to_broadcast([P, GT, D]),
                                            ALU.add).then_inc(b2_added, 1)
                        e.wait_ge(b2_added, G)
                        with e.Fori(0, G) as g:
                            for j in range(FC):
                                q = g * FC + j
                                e.wait_ge(g_full, q + 1)
                                if j >= 2:
                                    e.wait_ge(down_used, q - 1)
                                e.tensor_copy(gh[:, j % 2, :], gf[:, j % 2, :]).then_inc(g_hi, 1)
                            for j in range(2):
                                e.wait_ge(down_used, FC * (g + 1))
                                xs = X[:, bass.ds(g * GT + 2 * j, 2), :]
                                e.tensor_tensor(xs, xs, bank[3 + j][:, :].rearrange("p (t n) -> p t n", n=256),
                                                ALU.add).then_inc(y_added, 1)

                    @block.tensor
                    def _(e):
                        norm_tensor(e, norm, 0)
                        e.wait_ge(w_lo, 2)
                        with e.Fori(0, G) as g:
                            toks = bass.ds(g * GTOK, GTOK)
                            for s in range(FC + 2):
                                if s < FC:
                                    q = g * FC + s
                                    if s >= 4:
                                        e.wait_ge(g_full, q - 3)
                                    for c in range(DC):
                                        fs = slice(s * P, (s + 1) * P)
                                        i = three(e, PROJ[s % 4][:, :], w1h[:, c, fs], w1l[:, c, fs],
                                                  SRC_HI[:, 1, c, toks], SRC_LO[:, 1, c, toks], c == 0, c == DC - 1)
                                    i.then_inc(up_done, 1)
                                if s >= 2:
                                    j = s - 2
                                    e.wait_ge(g_lo, g * FC + j + 1)
                                    for t in range(GT):
                                        ts = slice(t * P, (t + 1) * P)
                                        i = three(e, bank[3 + t // 2][:, (t % 2) * 256:(t % 2 + 1) * 256],
                                                  gh[:, j % 2, ts], gl[:, j % 2, ts], w2h[:, j, :], w2l[:, j, :],
                                                  j == 0 and t % 2 == 0, j == FC - 1, skip_group_check=True)
                                    i.then_inc(down_used, 1)
                            e.wait_ge(y_added, 2 * g + 2)

        norm0 = Norm("lm", X, False, LN_EPS, PM[:, C_M0:C_M0 + 4])
        mlp("m0", norm0, PM[:, C_M0 + 4:C_M0 + 12], fc1, fc2, b_fc2, ACT.Gelu, None)

        NK = 2 * S
        GH = NH // DC
        JP = GH // 2
        VW = 2 * DH + 1
        HALF = slice(0, S), slice(S, P)
        with ExitStack() as l1:
            KL = sb("KL", [P, DC, B, NK], scope=l1)
            VL = sb("VL", [P, B, NH // 2, VW], scope=l1)
            QL = sb("QL", [P, DC, TOK], scope=l1)
            MA = sb("MA", [P, B, NK], BF16, scope=l1)
            ONE = sb("ONE", [P, P], BF16, scope=l1)
            HM = sb("HM", [P, GH], scope=l1)
            swap = sb("swap", [P, P], scope=l1)
            KQ = KL[:, :, :, :].rearrange("p m (t a) (h k) -> p m t (a h) k", a=2, h=2)
            MQ = MA[0:1, :, :].rearrange("p (t a) (h k) -> p t (a h) k", a=2, h=2)
            QB, KB, VB = PM[:, C_QB:C_QB + 2], PM[:, C_KB:C_KB + 2], PM[:, C_VB:C_VB + 2]
            with ExitStack() as ph:
                wr = sb("wr", [P, 3, DC, D], scope=ph)
                wh = sb("wh", [P, 3, DC, D], F32R, scope=ph)
                wl = sb("wl", [P, 3, DC, D], F32R, scope=ph)
                wr_in, mask_in, wh_done, wl_done = sem("wr_in"), sem("mask_in"), sem("wh_done"), sem("wl_done")
                xl_turned, xl_hi, xl_lo = sem("xl_turned"), sem("xl_hi"), sem("xl_lo")
                one_set, ma_set, v_one = sem("one_set"), sem("ma_set"), sem("v_one")
                ql_done, ql_out, vl_done, vl_out = sem("ql_done"), sem("ql_out"), sem("vl_done"), sem("vl_out")
                swap_set = sem("swap_set")
                mrow = XN[0:1, :, :, :].rearrange("p a t d -> p (a t d)").bitcast(I32)
                VBK = [bank[3], bank[4], bank[7]]
                with nc.Block() as block:
                    @block.sync
                    def _(e):
                        for j, w in enumerate((qw, kw, vw)):
                            e.dma_start(wr[:, j, :, :], w.rearrange("(c p) n -> p c n", p=P)).then_inc(wr_in, 16)
                        e.dma_start(mrow, mask.rearrange("(a b) s -> a (b s)", a=1)).then_inc(mask_in, 16)

                    @block.gpsimd
                    def _(e):
                        e.wait_ge(wr_in, 48)
                        e.tensor_copy(wh[:, :, :, :], wr[:, :, :, :]).then_inc(wh_done, 1)
                        e.wait_ge(wh_done, 1)
                        e.tensor_tensor(wl[:, :, :, :], wr[:, :, :, :], wh[:, :, :, :].bitcast(F32),
                                        ALU.subtract).then_inc(wl_done, 1)
                        e.memset(VL[:, :, :, 2 * DH], 1.0).then_inc(v_one, 1)
                        e.memset(ONE[:, :], 0.0).then_inc(one_set, 1)
                        e.memset(MA[:, :, :], 0.0).then_inc(ma_set, 1)
                        e.wait_ge(one_set, 1)
                        e.memset(ONE[0:1, :], 1.0).then_inc(one_set, 1)

                    @block.scalar
                    def _(e):
                        for g in range(G):
                            for c in range(DC):
                                e.wait_ge(xl_turned, g * DC + c + 1)
                                e.activation(SRC_HI[:, 1, c, g * GTOK:(g + 1) * GTOK], PROJ[2 * (g % 2) + c][:, :],
                                             ACT.Copy).then_inc(xl_hi, 1)
                        q = 0
                        for g in range(G):
                            for m in range(DC):
                                e.wait_ge(ql_done, q + 1)
                                e.activation(QL[:, m, g * GTOK:(g + 1) * GTOK], bank[q % 3][:, :], ACT.Identity,
                                             bias=QB[:, m:m + 1]).then_inc(ql_out, 1)
                                q += 1
                        for g in range(G):
                            for half in range(2):
                                for m in range(DC):
                                    e.wait_ge(ql_done, q + 1)
                                    part = bank[q % 3][:, :].rearrange("p (t a k) -> p t a k", a=2, k=S)
                                    tiles = slice(g * GT, (g + 1) * GT)
                                    if half == 0:
                                        i = e.activation(KQ[:, m, tiles, 0:4:3, :], part, ACT.Identity, bias=KB[:, m:m + 1])
                                    else:
                                        e.activation(KQ[:, m, tiles, 2, :], part[:, :, 0, :], ACT.Identity, bias=KB[:, m:m + 1])
                                        i = e.activation(KQ[:, m, tiles, 1, :], part[:, :, 1, :], ACT.Identity, bias=KB[:, m:m + 1])
                                    i.then_inc(ql_out, 1)
                                    q += 1

                    @block.vector
                    def _(e):
                        e.tensor_copy(swap[:, 0:S], ident[:, S:P]).then_inc(swap_set, 1)
                        e.tensor_copy(swap[:, S:P], ident[:, 0:S]).then_inc(swap_set, 1)
                        e.tensor_reduce(HM[:, :], ident[:, :].rearrange("p (h d) -> p h d", d=DH), AX_X, ALU.add)
                        for g in range(G):
                            for c in range(DC):
                                e.wait_ge(xl_hi, g * DC + c + 1)
                                toks = slice(g * GTOK, (g + 1) * GTOK)
                                e.tensor_tensor(SRC_LO[:, 1, c, toks], PROJ[2 * (g % 2) + c][:, :],
                                                SRC_HI[:, 1, c, toks].bitcast(F32), ALU.subtract).then_inc(xl_lo, 1)
                        e.wait_ge(mask_in, 16)
                        e.wait_ge(ma_set, 1)
                        e.tensor_scalar(MQ[:, :, 0:4:3, :], mrow.rearrange("p (t a s) -> p t a s", a=2, s=S), 0.0, MASKED,
                                        ALU.is_equal, ALU.mult).then_inc(ma_set, 1)
                        e.wait_ge(v_one, 1)
                        for t in range(NT):
                            e.wait_ge(vl_done, t + 1)
                            part = VBK[t % 3][:, :].rearrange("p (h j d) -> p h j d", h=2, d=2 * DH)
                            e.tensor_copy(VL[HALF[0], 2 * t:2 * t + 2, :, 0:2 * DH], part[HALF[0], :, :, :])
                            e.tensor_copy(VL[HALF[1], 2 * t + 1, :, 0:2 * DH], part[HALF[1], 0, :, :])
                            e.tensor_copy(VL[HALF[1], 2 * t, :, 0:2 * DH], part[HALF[1], 1, :, :]).then_inc(vl_out, 1)

                    @block.tensor
                    def _(e):
                        e.wait_ge(swap_set, 2)
                        for g in range(G):
                            if g >= 2:
                                e.wait_ge(xl_lo, (g - 1) * DC)
                            for c in range(DC):
                                for p in range(GT):
                                    i = e.transpose(PROJ[2 * (g % 2) + c][:, p * P:(p + 1) * P],
                                                    X[:, g * GT + p, c * P:(c + 1) * P], swap[:, :])
                                i.then_inc(xl_turned, 1)
                        e.wait_ge(xl_lo, G * DC)
                        e.wait_ge(wl_done, 1)
                        q = 0
                        for g in range(G):
                            for m in range(DC):
                                if q >= 3:
                                    e.wait_ge(ql_out, q - 2)
                                toks, cols = slice(g * GTOK, (g + 1) * GTOK), slice(m * P, (m + 1) * P)
                                for c in range(DC):
                                    i = three(e, bank[q % 3][:, :], wh[:, 0, c, cols], wl[:, 0, c, cols],
                                              SRC_HI[:, 1, c, toks], SRC_LO[:, 1, c, toks], c == 0, c == DC - 1)
                                i.then_inc(ql_done, 1)
                                q += 1
                        for g in range(G):
                            toks = slice(g * GTOK, (g + 1) * GTOK)
                            for half in range(2):
                                for m in range(DC):
                                    e.wait_ge(ql_out, q - 2)
                                    cols = slice(m * P, (m + 1) * P)
                                    for c in range(DC):
                                        i = three(e, bank[q % 3][:, :], wh[:, 1, c, cols], wl[:, 1, c, cols],
                                                  SRC_HI[:, half, c, toks], SRC_LO[:, half, c, toks], c == 0, c == DC - 1)
                                    i.then_inc(ql_done, 1)
                                    q += 1
                            for t in range(g * GT, (g + 1) * GT):
                                if t >= 3:
                                    e.wait_ge(vl_out, t - 2)
                                ks = slice(t * P, (t + 1) * P)
                                for half in range(2):
                                    for c in range(DC):
                                        i = three(e, VBK[t % 3][:, half * 256:(half + 1) * 256],
                                                  SRC_HI[:, half, c, ks], SRC_LO[:, half, c, ks],
                                                  wh[:, 2, c, :], wl[:, 2, c, :], c == 0, c == DC - 1)
                                i.then_inc(vl_done, 1)

            with ExitStack() as ph:
                QE = [sb(f"QE{a}", [P, GH, S], scope=ph) for a in range(2)]
                PTL = [sb(f"PTL{a}", [P, JP, P], scope=ph) for a in range(2)]
                SUB = [XN[:, a, 0:2, :].rearrange("p t d -> p (t d)") for a in range(2)]
                EXP = [XN[:, a, 2:4, :].rearrange("p t d -> p (t d)") for a in range(2)]
                ml = [sb(f"ml{a}", [P, JP], scope=ph) for a in range(2)]
                rl = [sb(f"rl{a}", [P, JP], scope=ph) for a in range(2)]
                AN = [sb(f"AN{a}", [P, DC, JP, DH], scope=ph) for a in range(2)]
                AT = [sb(f"AT{a}", [P, 2, S], scope=ph) for a in range(2)]
                qe_set, sl_done, ml_done = sem("qe_set"), sem("sl_done"), sem("ml_done")
                subl_done, expl_done, tl_done, tl_out = sem("subl_done"), sem("expl_done"), sem("tl_done"), sem("tl_out")
                al_done, rl_done, an_done = sem("al_done"), sem("rl_done"), sem("an_done")
                at_done, at_out, ao_hi, ao_lo = sem("at_done"), sem("at_out"), sem("ao_hi"), sem("ao_lo")
                STEPS = B * DC
                LT, LP, LA = 2, 3, 6

                def steps(e, slot):
                    for s in range(LA + 1):
                        slot(s, s, 0)
                    rest = (STEPS - LA - 1) // 4
                    with e.Fori(0, rest) as i:
                        for r in range(LA + 1, LA + 5):
                            slot(i * 4 + r, r, i * 2)
                    for s in range(LA + 1 + rest * 4, STEPS + LA):
                        slot(s, s, 0)

                def runs(r, lag):
                    return 0 <= r - lag < STEPS

                with nc.Block() as block:
                    @block.gpsimd
                    def _(e):
                        def slot(s, r, b0):
                            if runs(r, 0):
                                if r >= 2:
                                    e.wait_ge(sl_done, s - 1)
                                other = r // 2 + (1 if r // 2 % 2 == 0 else -1)
                                q = QL[:, r % 2, bass.ds((b0 + other) * S, S)]
                                e.tensor_tensor(QE[r % 2][:, :, :], q.unsqueeze(1).to_broadcast([P, GH, S]),
                                                HM[:, :].unsqueeze(2).to_broadcast([P, GH, S]),
                                                ALU.mult).then_inc(qe_set, 1)
                            if runs(r, LA) and (r - LA) % 2 == 0:
                                b = b0 + (r - LA) // 2
                                e.wait_ge(ao_hi, b + 1)
                                toks = bass.ds(b * S, S)
                                e.tensor_tensor(SRC_LO[:, 1, :, toks], AT[(r - LA) // 2 % 2][:, :, :],
                                                SRC_HI[:, 1, :, toks].bitcast(F32), ALU.subtract).then_inc(ao_lo, 1)

                        steps(e, slot)

                    @block.tensor
                    def _(e):
                        def slot(s, r, b0):
                            if runs(r, 0):
                                b = b0 + r // 2
                                e.wait_ge(qe_set, s + 1)
                                if r >= 2:
                                    e.wait_ge(subl_done, s - 1)
                                e.matmul(bank[r % 2][:, :].rearrange("p (j k) -> p j k", k=NK), ONE[:, :],
                                         MA[:, b, :].unsqueeze(1).to_broadcast([P, JP, NK]), start=True, stop=False,
                                         skip_group_check=True)
                                for j in range(JP):
                                    i = e.matmul(bank[r % 2][:, j * NK:(j + 1) * NK], QE[r % 2][:, 2 * j:2 * j + 2, :],
                                                 KL[:, r % 2, b, :], start=False, stop=(j == JP - 1),
                                                 skip_group_check=True)
                                i.then_inc(sl_done, 1)
                            if runs(r, LT):
                                a = (r - LT) % 2
                                e.wait_ge(expl_done, s - LT + 1)
                                if r - LT >= 2:
                                    e.wait_ge(tl_out, s - LT - 1)
                                for j in range(JP):
                                    i = e.transpose(PROJ[2 + a][:, j * P:(j + 1) * P], EXP[a][:, j * NK:(j + 1) * NK],
                                                    ident[:, :])
                                i.then_inc(tl_done, 1)
                            if runs(r, LP):
                                a, b = (r - LP) % 2, b0 + (r - LP) // 2
                                e.wait_ge(tl_out, s - LP + 1)
                                if r - LP >= 2:
                                    e.wait_ge(an_done, s - LP - 1)
                                for j in range(JP):
                                    i = e.matmul(bank[3 + a][:, j * VW:(j + 1) * VW], PTL[a][:, j, :],
                                                 VL[:, b, a * JP + j, :], start=True, stop=True)
                                i.then_inc(al_done, 1)
                            if runs(r, LA) and (r - LA) % 2 == 0:
                                b, c = b0 + (r - LA) // 2, (r - LA) // 2 % 2
                                e.wait_ge(an_done, 2 * b + 2)
                                if r - LA >= 4:
                                    e.wait_ge(at_out, 2 * b - 2)
                                e.transpose(logits[:, c, 0:P], AN[c][:, :, :, :].rearrange("p m j d -> p (m j d)"),
                                            ident[:, :]).then_inc(at_done, 1)

                        steps(e, slot)

                    @block.scalar
                    def _(e):
                        def slot(s, r, b0):
                            if runs(r, LT):
                                a = (r - LT) % 2
                                e.wait_ge(tl_done, s - LT + 1)
                                e.activation(PTL[a][:, :, :].rearrange("p j k -> p (j k)"), PROJ[2 + a][:, :],
                                             ACT.Copy).then_inc(tl_out, 1)
                            if runs(r, LA) and (r - LA) % 2 == 0:
                                b, c = b0 + (r - LA) // 2, (r - LA) // 2 % 2
                                e.wait_ge(at_done, b + 1)
                                if r - LA >= 4:
                                    e.wait_ge(ao_lo, b - 1)
                                for h in range(2):
                                    e.activation(AT[c][:, h, :], logits[:, c, h * S:(h + 1) * S], ACT.Identity,
                                                 bias=VB[:, h:h + 1]).then_inc(at_out, 1)
                            if runs(r, 0):
                                e.wait_ge(subl_done, s + 1)
                                e.activation(EXP[r % 2], SUB[r % 2], ACT.Exp, scale=1.0 / DH).then_inc(expl_done, 1)

                        steps(e, slot)

                    @block.vector
                    def _(e):
                        def slot(s, r, b0):
                            if runs(r, 0):
                                a = r % 2
                                e.wait_ge(sl_done, s + 1)
                                lg = bank[a][:, :].rearrange("p (j k) -> p j k", k=NK)
                                e.tensor_reduce(ml[a][:, :], lg, AX_X, ALU.max).then_inc(ml_done, 1)
                                e.wait_ge(ml_done, s + 1)
                                if r >= 2:
                                    e.wait_ge(expl_done, s - 1)
                                e.tensor_tensor(SUB[a].rearrange("p (j k) -> p j k", k=NK), lg,
                                                ml[a][:, :].unsqueeze(2).to_broadcast([P, JP, NK]),
                                                ALU.subtract).then_inc(subl_done, 1)
                            if runs(r, LP):
                                a, c = (r - LP) % 2, (r - LP) // 2 % 2
                                e.wait_ge(al_done, s - LP + 1)
                                res = bank[3 + a][:, 0:JP * VW].rearrange("p (j d) -> p j d", d=VW)
                                e.reciprocal(rl[a][:, :], res[:, :, 2 * DH]).then_inc(rl_done, 1)
                                e.wait_ge(rl_done, s - LP + 1)
                                if a == 0 and r - LP >= 4:
                                    e.wait_ge(at_done, b0 + (r - LP) // 2 - 1)
                                for h in range(2):
                                    i = e.tensor_tensor(AN[c][HALF[h], a, :, :], res[HALF[h], :, h * DH:(h + 1) * DH],
                                                        rl[a][HALF[h], :].unsqueeze(2).to_broadcast([S, JP, DH]), ALU.mult)
                                i.then_inc(an_done, 1)
                            if runs(r, LA) and (r - LA) % 2 == 0:
                                b, c = b0 + (r - LA) // 2, (r - LA) // 2 % 2
                                e.wait_ge(at_out, 2 * b + 2)
                                e.tensor_copy(SRC_HI[:, 1, :, bass.ds(b * S, S)], AT[c][:, :, :]).then_inc(ao_hi, 1)

                        steps(e, slot)

        Y = sb("Y", [P, NT, D])
        with ExitStack() as ph:
            owr = sb("owr", [P, 2, D], scope=ph)
            owh, owl = sb("owh", [P, 2, D], F32R, scope=ph), sb("owl", [P, 2, D], F32R, scope=ph)
            obb = sb("obb", [P, D], scope=ph)
            ow_in, ob_in, owh_done, owl_done = sem("ow_in"), sem("ob_in"), sem("owh_done"), sem("owl_done")
            y_base, y_prod, y_sum = sem("y_base"), sem("y_prod"), sem("y_sum")
            with nc.Block() as block:
                @block.sync
                def _(e):
                    e.dma_start(owr[:, :, :], ow.rearrange("e p n -> p e n")).then_inc(ow_in, 16)
                    e.dma_start(obb[:, :], out_b.partition_broadcast(P)).then_inc(ob_in, 16)

                @block.gpsimd
                def _(e):
                    e.wait_ge(ow_in, 16)
                    e.tensor_copy(owh[:, :, :], owr[:, :, :]).then_inc(owh_done, 1)
                    e.wait_ge(owh_done, 1)
                    e.tensor_tensor(owl[:, :, :], owr[:, :, :], owh[:, :, :].bitcast(F32),
                                    ALU.subtract).then_inc(owl_done, 1)

                @block.vector
                def _(e):
                    e.wait_ge(ob_in, 16)
                    for g in range(G):
                        ts = slice(g * GT, (g + 1) * GT)
                        e.tensor_tensor(Y[:, ts, :], X[:, ts, :], obb[:, :].unsqueeze(1).to_broadcast([P, GT, D]),
                                        ALU.add).then_inc(y_base, 1)
                    e.wait_ge(y_base, G)
                    for v in range(NT // 2):
                        e.wait_ge(y_prod, v + 1)
                        ys = Y[:, 2 * v:2 * v + 2, :]
                        e.tensor_tensor(ys, ys, PROJ[v % 4][:, :].rearrange("p (t n) -> p t n", n=256),
                                        ALU.add).then_inc(y_sum, 1)
                    e.wait_ge(y_sum, NT // 2)

                @block.tensor
                def _(e):
                    e.wait_ge(owl_done, 1)
                    for v in range(NT // 2):
                        if v >= 4:
                            e.wait_ge(y_sum, v - 3)
                        for t in (2 * v, 2 * v + 1):
                            ts = slice(t * P, (t + 1) * P)
                            for h in range(2):
                                i = three(e, PROJ[v % 4][:, (t % 2) * 256:(t % 2 + 1) * 256], SRC_HI[:, 1, h, ts],
                                          SRC_LO[:, 1, h, ts], owh[:, h, :], owl[:, h, :], h == 0, h == 1)
                        i.then_inc(y_prod, 1)

        norm1 = Norm("rn", Y, True, RMS_EPS, PM[:, C_PN:C_PN + 2])
        mlp("m1", norm1, PM[:, C_B1:C_B1 + 8], w1, w2, b2, ACT.Gelu_apprx_tanh,
            out.rearrange("(t p) d -> p t d", p=P))


def kernel(**inputs):
    import numpy as np
    import concourse.bacc as bacc
    from concourse.bass_utils import run_bass_kernel_spmd

    def given(name):
        return np.asarray(inputs[name])

    def both(name):
        return [given(f"L0_xattn_{name}{i}") for i in (1, 2)]

    def pairs(ws):
        return np.stack([w.reshape(D, HP, 2 * K).transpose(1, 0, 2) for w in ws])

    def rows(*vs):
        return np.concatenate([v.reshape(-1, P) for v in vs])

    kv_w, kv_b = given("L1_xattn_kv_w").reshape(D, D, 2), given("L1_xattn_kv_b").reshape(D, 2)
    arrays = {
        "x": given("x").reshape(TOK, D),
        "ctx": given("ctx_2048").reshape(TOK, D),
        "mask": given("mask_BxS2_ik0"),
        "wall": np.stack([pairs(both("wq")), pairs(both("wk")), pairs(both("wv")),
                          np.stack([w.reshape(HP, 2 * K, D) for w in both("wo")])], axis=2
                         ).reshape(NL * HP, 4, 256, 256),
        "vech": rows(*both("bq"), *both("bk"), *both("bias_k"), *both("bv"), *both("bias_v")),
        "vecm": rows(*[given(f"L0_xattn_{n}") for i in (1, 2)
                       for n in (f"ln{i}_scale", f"ln{i}_offset", f"bo{i}")],
                     given("L0_xattn_ln_mlp_scale"), given("L0_xattn_ln_mlp_offset"), given("L0_xattn_b_fc1"),
                     given("L1_xattn_q_b"), kv_b[:, 0],
                     kv_b[:, 1].reshape(NH // 2, 2, DH).transpose(1, 0, 2),
                     given("L1_xattn_postnorm_w"), given("L1_xattn_mlp_b1")),
        "fc1": given("L0_xattn_w_fc1"), "fc2": given("L0_xattn_w_fc2"), "b_fc2": given("L0_xattn_b_fc2"),
        "qw": given("L1_xattn_q_w"), "kw": kv_w[:, :, 0], "vw": kv_w[:, :, 1],
        "ow": given("L1_xattn_out_w").reshape(NH // 2, 2, DH, D).transpose(1, 0, 2, 3).reshape(2, P, D),
        "out_b": given("L1_xattn_out_b"),
        "w1": given("L1_xattn_mlp_w1"), "w2": given("L1_xattn_mlp_w2"), "b2": given("L1_xattn_mlp_b2"),
    }
    nc = bacc.Bacc("TRN2", target_bir_lowering=False, num_devices=1)
    arrays = {f"in_{k}": np.ascontiguousarray(v) for k, v in arrays.items()}
    args = [nc.dram_tensor(k, v.shape, mybir.dt.from_np(v.dtype), kind="ExternalInput").ap()
            for k, v in arrays.items()]
    out = nc.dram_tensor("out", (TOK, D), F32, kind="ExternalOutput").ap()
    program(nc, *args, out)
    r = run_bass_kernel_spmd(nc, [arrays], core_ids=[0])
    return r.results[0]["out"].reshape(B, S, D)
```

```python
from contextlib import ExitStack

import concourse.bass as bass
from concourse import mybir

ALU = mybir.AluOpType
ACT = mybir.ActivationFunctionType
F32 = mybir.dt.float32
F32R = mybir.dt.float32r
BF16 = mybir.dt.bfloat16
I32 = mybir.dt.int32
AX_X = mybir.AxisListType.X

B, S, D = 32, 64, 256
TOK = B * S
P = 128
NT = TOK // P
DC = D // P
H, K = 16, 128
HP = H // 2
NL = 2
G = 4
GT = NT // G
GTOK = TOK // G
UNITS = HP * G
F = 1024
FC = F // P
NH, DH = 16, 16
KEYS = S + 1
LN_EPS, RMS_EPS = 1e-5, 1e-6
MASKED = -1e30
ROWS_H = 5 * NL * H
LNP = 6
C_M0 = NL * LNP
C_QB = C_M0 + 12
C_KB = C_QB + 2
C_VB = C_KB + 2
C_PN = C_VB + 2
C_B1 = C_PN + 2
ROWS_M = C_B1 + 8
OLD = 8


def program(nc, x, ctx_in, mask, wall, vech, vecm, b_fc2, qw, kw, vw, ow, out_b, w1, w2, b2, out):
    es = ExitStack()
    with es:
        def sem(name):
            return es.enter_context(nc.semaphore(name))

        def sb(name, shape, dt=F32, scope=es):
            return scope.enter_context(nc.sbuf_tensor(name, shape, dt))

        bank = [es.enter_context(nc.psum_tensor(f"bank{i}", [P, 512], F32)) for i in range(5)]
        logits = es.enter_context(nc.psum_tensor("logits", [P, 2, 512], F32))
        bank += [None, None, es.enter_context(nc.psum_tensor("bank7", [P, 512], F32))]
        PROJ = [bank[0], bank[1], bank[2], bank[7]]
        WIDE = PROJ + [logits[:, 0, :], logits[:, 1, :]]

        X = sb("X", [P, NT, D])
        SRC_HI = sb("SRC_HI", [P, 2, DC, TOK], F32R)
        SRC_LO = sb("SRC_LO", [P, 2, DC, TOK], F32R)
        ident = sb("ident", [P, P])
        PH = sb("PH", [P, 5, NL * H + 4])
        PM = sb("PM", [P, ROWS_M])
        st = sb("st", [P, NT, 6])
        mv = sb("mv", [P, NT, 2])
        ms = sb("ms", [P, NT])
        sd = sb("sd", [P, NT])
        rs = sb("rs", [P, NT])
        XN = sb("XN", [P, 2, GT, D])
        HT = sb("HT", [P, 2, 512])

        class Norm:
            def __init__(self, tag, src, rms, eps, prm):
                self.src, self.rms, self.eps, self.prm = src, rms, eps, prm
                self.stat, self.sqrt, self.rstd = sem(tag + "_stat"), sem(tag + "_sqrt"), sem(tag + "_rstd")
                self.xn, self.turned, self.scaled = sem(tag + "_xn"), sem(tag + "_turned"), sem(tag + "_scaled")
                self.hi, self.lo = sem(tag + "_hi"), sem(tag + "_lo")
                self.stats = 2 * GT + (3 if rms else 1)

        def norm_stats(e, n, k, g):
            at, ts = (k * G + g) * n.stats, slice(g * GT, (g + 1) * GT)
            e.memset(ms[:, ts], n.eps)
            for t in range(g * GT, (g + 1) * GT):
                e.bn_stats(st[:, t, :], n.src[:, t, :]).then_inc(n.stat, 1)
            e.wait_ge(n.stat, at + GT)
            e.memset(rs[:, ts], 0.0)
            for t in range(g * GT, (g + 1) * GT):
                e.bn_aggr(mv[:, t, :], st[:, t, :]).then_inc(n.stat, 1)
            e.wait_ge(n.stat, at + 2 * GT)
            if n.rms:
                e.tensor_tensor(mv[:, ts, 0], mv[:, ts, 0], mv[:, ts, 0], ALU.mult).then_inc(n.stat, 1)
                e.wait_ge(n.stat, at + 2 * GT + 1)
                e.tensor_tensor(mv[:, ts, 1], mv[:, ts, 0], mv[:, ts, 1], ALU.add).then_inc(n.stat, 1)
                e.wait_ge(n.stat, at + 2 * GT + 2)
            e.tensor_tensor(ms[:, ts], mv[:, ts, 1], ms[:, ts], ALU.add).then_inc(n.stat, 1)

        def norm_sqrt(e, n, k, g):
            e.wait_ge(n.stat, (k * G + g + 1) * n.stats)
            e.activation(sd[:, g * GT:(g + 1) * GT], ms[:, g * GT:(g + 1) * GT], ACT.Sqrt).then_inc(n.sqrt, 1)

        def norm_apply(e, n, k, g):
            q = k * G + g
            e.wait_ge(n.sqrt, q + 1)
            e.reciprocal(rs[:, g * GT:(g + 1) * GT], sd[:, g * GT:(g + 1) * GT]).then_inc(n.rstd, 1)
            e.wait_ge(n.rstd, q + 1)
            if g >= 2 or not (isinstance(k, int) and k == 0):
                e.wait_ge(n.turned, (q - 1) * DC)
            for p in range(GT):
                t = g * GT + p
                if n.rms:
                    i = e.tensor_scalar(XN[:, g % 2, p, :], n.src[:, t, :], rs[:, t:t + 1], None, ALU.mult)
                else:
                    i = e.tensor_scalar(XN[:, g % 2, p, :], n.src[:, t, :], mv[:, t, 0:1], rs[:, t:t + 1],
                                        ALU.subtract, ALU.mult)
            i.then_inc(n.xn, 1)

        def norm_turn(e, n, k, g):
            e.wait_ge(n.xn, k * G + g + 1)
            for c in range(DC):
                for p in range(GT):
                    i = e.transpose(PROJ[2 + c][:, p * P:(p + 1) * P], XN[:, g % 2, p, c * P:(c + 1) * P], ident[:, :])
                i.then_inc(n.turned, 1)

        def norm_scale(e, n, k, g):
            for c in range(DC):
                q = (k * G + g) * DC + c
                e.wait_ge(n.turned, q + 1)
                if g >= 1 or not (isinstance(k, int) and k == 0):
                    e.wait_ge(n.lo, q - 1)
                piece = PROJ[2 + c][:, :]
                if n.rms:
                    i = e.activation(HT[:, c, :], piece, ACT.Copy, scale=n.prm[:, c:c + 1])
                else:
                    i = e.activation(HT[:, c, :], piece, ACT.Identity, scale=n.prm[:, c:c + 1],
                                     bias=n.prm[:, 2 + c:3 + c])
                i.then_inc(n.scaled, 1)

        def norm_hi(e, n, k, g):
            for c in range(DC):
                e.wait_ge(n.scaled, (k * G + g) * DC + c + 1)
                e.tensor_copy(SRC_HI[:, 1, c, g * GTOK:(g + 1) * GTOK], HT[:, c, :]).then_inc(n.hi, 1)

        def norm_lo(e, n, k, g):
            for c in range(DC):
                e.wait_ge(n.hi, (k * G + g) * DC + c + 1)
                toks = slice(g * GTOK, (g + 1) * GTOK)
                e.tensor_tensor(SRC_LO[:, 1, c, toks], HT[:, c, :], SRC_HI[:, 1, c, toks].bitcast(F32),
                                ALU.subtract).then_inc(n.lo, 1)

        def three(e, dst, a_hi, a_lo, b_hi, b_lo, start, stop, **kw):
            e.matmul(dst, a_hi, b_hi, start=start, stop=False, **kw)
            e.matmul(dst, a_hi, b_lo, start=False, stop=False, **kw)
            return e.matmul(dst, a_lo, b_hi, start=False, stop=stop, **kw)

        CUR = sb("CUR", [P, 4])
        wh = sb("wh", [P, 3, DC, D], F32R)
        wl = sb("wl", [P, 3, DC, D], F32R)
        wr_in, wh_done, wl_done = sem("wr_in"), sem("wh_done"), sem("wl_done")
        wt = es.enter_context(ExitStack())
        W = [sb(f"W{a}", [P, 4, DC, 256], scope=wt) for a in range(2)]
        WHI = [sb(f"WHI{a}", [P, 4, DC, 256], F32R, scope=wt) for a in range(2)]
        WLO = [sb(f"WLO{a}", [P, 4, DC, 256], F32R, scope=wt) for a in range(2)]
        SETS = NL * HP + 2
        w_in = [sem(f"w_in{a}") for a in range(2)]
        w_hi, w_split = sem("w_hi"), sem("w_split")
        norm = Norm("ln", X, False, LN_EPS, CUR)

        with ExitStack() as ph:
            vh = HT[0:ROWS_H // 2, 0, 0:2 * P].rearrange("p (a k) -> p a k", k=P)
            vm, one = HT[0:ROWS_M, 0, 2 * P:3 * P], HT[:, 1, 0:P]
            PB = [sb(f"PB{a}", [P, 5, 2], scope=ph) for a in range(2)]
            E2 = [sb(f"E2{a}", [P, 2, 32], scope=ph) for a in range(2)]
            EA = sb("EA", [P, 2 * SETS, 32], scope=ph)
            EB = sb("EB", [P, 2 * SETS, 32], scope=ph)
            BWT = sb("BWT", [P, DC, 32], scope=ph)
            BW = sb("BW", [32, D], scope=ph)
            PTB = sb("PTB", [P, NT, 32], scope=ph)
            PTT = sb("PTT", [32, 2, 512], scope=ph)
            QT = sb("QT", [P, 2, GTOK], scope=ph)
            KT = sb("KT", [P, 2, GTOK // S, KEYS], scope=ph)
            V = [sb(f"V{a}", [P, GT, 256], scope=ph) for a in range(2)]
            cin = V
            mx = sb("mx", [P, 2 * GT], scope=ph)
            sub = sb("sub", [P, 2 * GT, KEYS], scope=ph)
            ex = sb("ex", [P, 2 * GT, KEYS], scope=ph)
            sm = sb("sm", [P, 2 * GT], scope=ph)
            ri = sb("ri", [P, 2 * GT], scope=ph)
            PD = sb("PD", [P, 2 * GT, P], scope=ph)
            PTS = sb("PTS", [P, 2, 512], scope=ph)
            CHI = sb("CHI", [P, 2, GTOK], F32R, scope=ph)
            CLO = sb("CLO", [P, 2, GTOK], F32R, scope=ph)
            SCALE = float(K) ** -0.5
            BWTN = HP + 2
            LASTP = OLD - G

            vec_in = sem("vec_in")
            ctx_in_g, x_in = [sem(f"ctx_in{g}") for g in range(G)], [sem(f"x_in{g}") for g in range(G)]
            ident_one, ident_done, zeros_set = sem("ident_one"), sem("ident_done"), sem("zeros_set")
            vec_turned, vec_copied = sem("vec_turned"), sem("vec_copied")
            ctx_turned, ctx_hi, ctx_lo = sem("ctx_turned"), sem("ctx_hi"), sem("ctx_lo")
            bw_done, e_made, cur_set = sem("bw_done"), sem("e_made"), sem("cur_set")
            q_done, k_done, v_done, s_done = sem("q_done"), sem("k_done"), sem("v_done"), sem("s_done")
            t_done, c_done, o_done = sem("t_done"), sem("c_done"), sem("o_done")
            q_out, k_out, v_out, exp_done = sem("q_out"), sem("k_out"), sem("v_out"), sem("exp_done")
            pt_out, c_hi, c_lo, kb_set = sem("pt_out"), sem("c_hi"), sem("c_lo"), sem("kb_set")
            mx_done, sub_done, sm_done, ri_done = sem("mx_done"), sem("sub_done"), sem("sm_done"), sem("ri_done")
            p_ready, x_settled, bwt_sum = sem("p_ready"), sem("x_settled"), sem("bwt_sum")
            bw_turned, bw_out, ptb_turned, ptb_out = sem("bw_turned"), sem("bw_out"), sem("ptb_turned"), sem("ptb_out")

            def turning(L, at, last):
                if at == 0:
                    return L, G - 1
                if last and at > LASTP + 1:
                    return L + 1, at - LASTP - 2
                return None

            def slots(e, L, slot):
                slot(L, L * UNITS, 0, L * HP, None, False)
                with e.Fori(0, UNITS // OLD - 1) as i:
                    for u in range(OLD):
                        slot(L, L * UNITS + i * OLD + u + 1, u + 1, L * HP + i * 2 + (u + 1) // G, i * 2 + u // G, False)
                i = UNITS // OLD - 1
                for u in range(OLD):
                    slot(L, L * UNITS + i * OLD + u + 1, u + 1,
                         L * HP + i * 2 + (u + 1) // G if u < OLD - 1 else None, i * 2 + u // G, True)

            with nc.Block() as block:
                @block.sync
                def _(e):
                    def load(m, a):
                        e.dma_start(W[a][:, :, :, :], wall[m].rearrange("j (c p) n -> p j c n", p=P)).then_inc(w_in[a], 16)

                    ct, xt = (v.rearrange("(t p) d -> p t d", p=P) for v in (ctx_in, x))
                    for g in range(G):
                        ts = slice(g * GT, (g + 1) * GT)
                        if g >= 2:
                            e.wait_ge(ctx_turned, (g - 1) * DC)
                        e.dma_start(cin[g % 2][:, :, :], ct[:, ts, :]).then_inc(ctx_in_g[g], 16)
                        e.dma_start(X[:, ts, :], xt[:, ts, :]).then_inc(x_in[g], 16)
                        if g < 2:
                            load(g, g)
                    with e.Fori(1, SETS // 2) as i:
                        for a in range(2):
                            m = i * 2
                            e.wait_ge(w_split, m + a - 1)
                            e.wait_ge(bw_done, m + a - 1)
                            load(m + a, a)

                @block.gpsimd
                def _(e):
                    e.memset(one, 1.0).then_inc(ident_one, 1)
                    e.wait_ge(ident_one, 1)
                    e.affine_select(out=ident[:, :], in_=one, compare_op=ALU.is_equal, fill=0.0, base=0,
                                    pattern=[[-1, P]], channel_multiplier=1).then_inc(ident_done, 1)
                    e.memset(EA[:, :, :], 0.0)
                    e.memset(EB[:, :, :], 0.0).then_inc(e_made, 1)
                    e.memset(PTB[:, :, :], 1.0)
                    e.memset(PD[:, :, :], 0.0).then_inc(zeros_set, 1)

                    def split(m, a):
                        e.wait_ge(w_hi, m + 1)
                        for j in range(4):
                            i = e.tensor_tensor(WLO[a][:, j, :, :], W[a][:, j, :, :],
                                                WHI[a][:, j, :, :].bitcast(F32), ALU.subtract)
                        e.tensor_tensor(E2[a][:, :, :], EA[:, bass.ds(2 * m, 2), :], EB[:, bass.ds(2 * m, 2), :],
                                        ALU.subtract)
                        e.tensor_copy(PB[a][:, :, :], PH[:, :, bass.ds(2 * m, 2)]).then_inc(w_split, 1)

                    for g in range(G - 1):
                        if g == 0:
                            e.wait_ge(e_made, 3)
                            split(0, 0)
                        norm_lo(e, norm, 0, g)
                    with e.Fori(0, NL) as L:
                        norm_lo(e, norm, L, G - 1)
                        split(L * HP + 1, 1)
                        with e.Fori(0, HP // 2 - 1) as i:
                            for a in range(2):
                                split(L * HP + i * 2 + 2 + a, a)
                        split(L * HP + HP, 0)
                        for g in range(G - 1):
                            norm_lo(e, norm, L + 1, g)

                @block.tensor
                def _(e):
                    def slot(L, n, at, pair, hp, last):
                        g, a, ab = at % G, (at // G) % 2, ((at - 1) // G) % 2
                        front, back = pair is not None, hp is not None
                        toks = slice(g * GTOK, (g + 1) * GTOK)
                        norm_now, bridge = turning(L, at, last), last and at > LASTP
                        if front:
                            if g == 0:
                                e.wait_ge(w_split, pair + 1)
                            if at < G:
                                e.wait_ge(norm.lo, (L * G + at + 1) * DC)
                            if norm_now is not None:
                                e.wait_ge(norm.scaled, (norm_now[0] * G + norm_now[1]) * DC)
                            if at == 1:
                                e.wait_ge(norm.scaled, (L + 1) * G * DC)
                            if last and at > LASTP + 1:
                                e.wait_ge(ptb_out, L * G + at - LASTP - 1)
                                e.wait_ge(bw_out, L + 1)
                            for j, half, done, free in ((0, 1, q_done, v_out), (1, 0, k_done, k_out)):
                                for h in range(2):
                                    if back:
                                        e.wait_ge(free, 2 * n - 1 + h)
                                    for c in range(DC):
                                        i = three(e, PROJ[2 * j + h][:, :], WHI[a][:, j, c, h * K:(h + 1) * K],
                                                  WLO[a][:, j, c, h * K:(h + 1) * K], SRC_HI[:, half, c, toks],
                                                  SRC_LO[:, half, c, toks], c == 0, c == DC - 1)
                                    i.then_inc(done, 1)
                        if back:
                            e.wait_ge(p_ready, n)
                            e.wait_ge(x_settled, 2 * n)
                            for h in range(2):
                                for p in range(GT):
                                    i = e.transpose(bank[3 + h][:, p * P:(p + 1) * P], PD[:, h * GT + p, :],
                                                    ident[:, :])
                                i.then_inc(t_done, 1)
                        if bridge:
                            if front:
                                e.wait_ge(k_out, 2 * n + 2)
                            else:
                                e.wait_ge(norm.scaled, ((L + 1) * G + G - 2) * DC)
                            gb = at - LASTP - 1
                            for p in range(GT):
                                i = e.transpose(PROJ[2][0:32, p * P:(p + 1) * P], PTB[:, gb * GT + p, :], ident[:, :])
                            i.then_inc(ptb_turned, 1)
                            if gb == 0:
                                e.wait_ge(bwt_sum, (L + 1) * BWTN)
                                for c in range(DC):
                                    i = e.transpose(PROJ[3][0:32, c * P:(c + 1) * P], BWT[:, c, :], ident[:, :])
                                i.then_inc(bw_turned, 1)
                        if front:
                            for j in range(2):
                                e.wait_ge(q_out, 2 * n + j + 1)
                                for p in range(2):
                                    t = g * GT + 2 * j + p
                                    for c in range(DC):
                                        i = three(e, PROJ[j][:, p * 256:(p + 1) * 256],
                                                  SRC_HI[:, 0, c, t * P:(t + 1) * P], SRC_LO[:, 0, c, t * P:(t + 1) * P],
                                                  WHI[a][:, 2, c, :], WLO[a][:, 2, c, :], c == 0, c == DC - 1)
                                i.then_inc(v_done, 1)
                        if back:
                            e.wait_ge(v_out, 2 * n)
                            for h in range(2):
                                e.wait_ge(pt_out, 2 * n - 1 + h)
                                for p in range(GT):
                                    i = e.matmul(bank[3 + h][:, p * P:(p + 1) * P],
                                                 V[(at - 1) % 2][:, p, h * K:(h + 1) * K],
                                                 PTS[:, h, p * P:(p + 1) * P], start=True, stop=True)
                                i.then_inc(c_done, 1)
                        if norm_now is not None:
                            if bridge:
                                e.wait_ge(ptb_out, L * G + at - LASTP)
                            else:
                                e.wait_ge(k_out, 2 * n + 2)
                            norm_turn(e, norm, *norm_now)
                        if front:
                            e.wait_ge(q_out, 2 * n + 2)
                            e.wait_ge(k_out, 2 * n + 2)
                            e.wait_ge(kb_set, n + 1)
                            if back:
                                e.wait_ge(sub_done, n)
                            if g == 0:
                                for c in range(DC):
                                    for h in range(2):
                                        i = e.matmul(logits[:, 1, 448 + 32 * c:480 + 32 * c],
                                                     W[a][:, 3, h, c * P:(c + 1) * P], E2[a][:, h, :],
                                                     start=(h == 0), stop=(h == 1))
                                i.then_inc(bw_done, 1)
                            for h in range(2):
                                for q in range(GTOK // S):
                                    p, b = q // 2, q % 2
                                    i = e.matmul(logits[b * S:(b + 1) * S, h, p * KEYS:(p + 1) * KEYS],
                                                 QT[:, h, q * S:(q + 1) * S], KT[:, h, q, :], start=True, stop=True)
                            i.then_inc(s_done, 1)
                        if back:
                            e.wait_ge(c_lo, 2 * n)
                            if bridge:
                                e.wait_ge(bw_out, L + 1)
                                e.wait_ge(ptb_out, L * G + at - LASTP)
                            for j in range(2):
                                for p in range(2):
                                    ts = slice((2 * j + p) * P, (2 * j + p + 1) * P)
                                    dst = bank[3 + j][:, p * 256:(p + 1) * 256]
                                    if bridge:
                                        e.matmul(dst, PTT[:, (at - LASTP - 1) % 2, ts], BW[:, :], start=True, stop=False)
                                    for h in range(2):
                                        i = three(e, dst, CHI[:, h, ts], CLO[:, h, ts], WHI[ab][:, 3, h, :],
                                                  WLO[ab][:, 3, h, :], h == 0 and not bridge, h == 1)
                                i.then_inc(o_done, 1)

                    e.wait_ge(ident_done, 1)
                    e.wait_ge(vec_in, 32)
                    half = ROWS_H // 2
                    for a in range(2):
                        e.transpose(bank[3][:, a * half:(a + 1) * half], vh[:, a, :], ident[0:half, 0:half])
                    e.transpose(bank[3][:, ROWS_H:ROWS_H + ROWS_M], vm,
                                ident[0:ROWS_M, 0:ROWS_M]).then_inc(vec_turned, 1)
                    for g in range(G):
                        e.wait_ge(ctx_in_g[g], 16)
                        if g >= 1:
                            e.wait_ge(ctx_lo, g * DC)
                        for c in range(DC):
                            for p in range(GT):
                                i = e.transpose(PROJ[c][:, p * P:(p + 1) * P], cin[g % 2][:, p, c * P:(c + 1) * P],
                                                ident[:, :])
                            i.then_inc(ctx_turned, 1)
                        if g >= 1:
                            if g >= 2:
                                e.wait_ge(norm.scaled, (g - 1) * DC)
                            norm_turn(e, norm, 0, g - 1)
                    e.wait_ge(ctx_lo, G * DC)
                    with e.Fori(0, NL) as L:
                        slots(e, L, slot)

                @block.scalar
                def _(e):
                    def slot(L, n, at, pair, hp, last):
                        a = (at // G) % 2
                        front, back = pair is not None, hp is not None
                        norm_now, bridge = turning(L, at, last), last and at > LASTP
                        if front:
                            for h in range(2):
                                e.wait_ge(q_done, 2 * n + h + 1)
                                e.activation(QT[:, h, :], PROJ[h][:, :], ACT.Identity,
                                             bias=PB[a][:, 0, h:h + 1]).then_inc(q_out, 1)
                            for h in range(2):
                                e.wait_ge(k_done, 2 * n + h + 1)
                                e.activation(KT[:, h, :, 0:S], PROJ[2 + h][:, :].rearrange("p (q k) -> p q k", k=S),
                                             ACT.Identity, bias=PB[a][:, 1, h:h + 1]).then_inc(k_out, 1)
                        if norm_now is not None:
                            norm_sqrt(e, norm, *norm_now)
                        if back:
                            for h in range(2):
                                e.wait_ge(t_done, 2 * n - 1 + h)
                                e.activation(PTS[:, h, :], bank[3 + h][:, :], ACT.Copy).then_inc(pt_out, 1)
                        if bridge:
                            e.wait_ge(ptb_turned, L * G + at - LASTP)
                            e.activation(PTT[:, (at - LASTP - 1) % 2, :], PROJ[2][0:32, :], ACT.Copy).then_inc(ptb_out, 1)
                        if front:
                            for j in range(2):
                                e.wait_ge(v_done, 2 * n + j + 1)
                                e.activation(V[at % 2][:, 2 * j:2 * j + 2, :],
                                             PROJ[j][:, :].rearrange("p (t n) -> p t n", n=256),
                                             ACT.Copy).then_inc(v_out, 1)
                        if back:
                            for h in range(2):
                                e.wait_ge(c_done, 2 * n - 1 + h)
                                e.activation(CHI[:, h, :], bank[3 + h][:, :], ACT.Copy).then_inc(c_hi, 1)
                        if norm_now is not None:
                            e.wait_ge(cur_set, norm_now[0] + 1)
                            norm_scale(e, norm, *norm_now)
                        if front:
                            e.wait_ge(sub_done, n + 1)
                            e.activation(ex[:, :, :], sub[:, :, :], ACT.Exp, scale=SCALE).then_inc(exp_done, 1)

                    e.dma_start(vh, vech.rearrange("(a r) k -> r a k", a=2)).then_inc(vec_in, 16)
                    e.dma_start(vm, vecm).then_inc(vec_in, 16)
                    for g in range(G):
                        for c in range(DC):
                            e.wait_ge(ctx_turned, g * DC + c + 1)
                            e.activation(SRC_HI[:, 0, c, g * GTOK:(g + 1) * GTOK], PROJ[c][:, :],
                                         ACT.Copy).then_inc(ctx_hi, 1)
                        if g < G - 1:
                            norm_sqrt(e, norm, 0, g)
                        if g == 0:
                            e.wait_ge(cur_set, 1)
                        else:
                            norm_scale(e, norm, 0, g - 1)
                    with e.Fori(0, NL) as L:
                        slots(e, L, slot)

                @block.vector
                def _(e):
                    logit = logits[:, :, 0:GT * KEYS].rearrange("p h (t k) -> p h t k", k=KEYS)

                    def slot(L, n, at, pair, hp, last):
                        g, a, gb = at % G, (at // G) % 2, (at - 1) % G
                        front, back = pair is not None, hp is not None
                        norm_now, bridge = turning(L, at, last), last and at > LASTP
                        if front:
                            if g == 0:
                                e.wait_ge(w_split, pair + 1)
                            e.tensor_copy(KT[:, :, :, S], PB[a][:, 2, :].unsqueeze(2).to_broadcast([P, 2, GTOK // S])
                                          ).then_inc(kb_set, 1)
                        if back:
                            e.wait_ge(exp_done, n)
                            e.tensor_reduce(sm[:, :], ex[:, :, :], AX_X, ALU.add).then_inc(sm_done, 1)
                            e.wait_ge(sm_done, n)
                            e.reciprocal(ri[:, :], sm[:, :]).then_inc(ri_done, 1)
                            e.wait_ge(ri_done, n)
                            e.tensor_tensor(PTB[:, gb * GT:(gb + 1) * GT, bass.ds(2 * hp, 2)].rearrange("p t h -> p h t"),
                                            ex[:, :, S].rearrange("p (h t) -> p h t", h=2),
                                            ri[:, :].rearrange("p (h t) -> p h t", h=2), ALU.mult)
                            for b in range(2):
                                r = slice(b * S, (b + 1) * S)
                                i = e.tensor_tensor(PD[r, :, r], ex[r, :, 0:S],
                                                    ri[r, :].unsqueeze(2).to_broadcast([S, 2 * GT, S]), ALU.mult)
                            i.then_inc(p_ready, 1)
                        if bridge and gb == 0:
                            e.wait_ge(bw_turned, L + 1)
                            e.tensor_copy(BW[:, :], PROJ[3][0:32, 0:D]).then_inc(bw_out, 1)
                            e.tensor_copy(CUR[:, :], PM[:, bass.ds((L + 1) * LNP, 4)]).then_inc(cur_set, 1)
                        if norm_now is not None:
                            norm_apply(e, norm, *norm_now)
                        if front and g == 1:
                            round_set(pair + 1, 1 - a)
                        if back:
                            for h in range(2):
                                e.wait_ge(c_hi, 2 * n - 1 + h)
                                e.tensor_tensor(CLO[:, h, :], bank[3 + h][:, :], CHI[:, h, :].bitcast(F32),
                                                ALU.subtract).then_inc(c_lo, 1)
                        if front:
                            e.wait_ge(s_done, n + 1)
                            if g == 0:
                                e.wait_ge(bwt_sum, (BWTN - HP) * L + 2 + pair)
                                e.tensor_tensor(BWT[:, :, :], BWT[:, :, :],
                                                logits[:, 1, 448:512].rearrange("p (c n) -> p c n", n=32),
                                                ALU.add).then_inc(bwt_sum, 1)
                            e.tensor_reduce(mx[:, :].rearrange("p (h t) -> p h t", h=2), logit, AX_X,
                                            ALU.max).then_inc(mx_done, 1)
                            e.wait_ge(mx_done, n + 1)
                            e.tensor_tensor(sub[:, :, :].rearrange("p (h t) k -> p h t k", h=2), logit,
                                            mx[:, :].rearrange("p (h t) -> p h t", h=2).unsqueeze(3)
                                            .to_broadcast([P, 2, GT, KEYS]), ALU.subtract).then_inc(sub_done, 1)
                        if norm_now is not None:
                            norm_hi(e, norm, *norm_now)
                        if back:
                            for j in range(2):
                                e.wait_ge(o_done, 2 * n - 1 + j)
                                xs = X[:, gb * GT + 2 * j:gb * GT + 2 * j + 2, :]
                                e.tensor_tensor(xs, xs, bank[3 + j][:, :].rearrange("p (t n) -> p t n", n=256),
                                                ALU.add).then_inc(x_settled, 1)

                        if bridge:
                            e.wait_ge(x_settled, 2 * n + 2)
                            norm_stats(e, norm, L + 1, gb)

                    def round_set(m, a):
                        e.wait_ge(w_in[a], 8 * (m - a) + 16)
                        e.tensor_copy(WHI[a][:, :, :, :], W[a][:, :, :, :]).then_inc(w_hi, 1)

                    e.memset(PH[:, :, NL * H:2 * SETS], 0.0)
                    e.wait_ge(vec_turned, 1)
                    e.tensor_copy(PH[:, :, 0:NL * H], bank[3][:, 0:ROWS_H].rearrange("p (j h) -> p j h", j=5)
                                  ).then_inc(vec_copied, 1)
                    e.tensor_copy(PM[:, :], bank[3][:, ROWS_H:ROWS_H + ROWS_M]).then_inc(vec_copied, 1)
                    e.wait_ge(vec_copied, 2)
                    e.tensor_copy(CUR[:, :], PM[:, 0:4]).then_inc(cur_set, 1)
                    e.wait_ge(zeros_set, 1)
                    e.wait_ge(e_made, 1)
                    for t, j in ((EA, 4), (EB, 3)):
                        flat = t[:, :, :].rearrange("p m n -> p (m n)")
                        for L in range(NL):
                            e.tensor_copy(flat[:, L * H * 32:L * H * 32 + (H - 1) * 33 + 1:33],
                                          PH[:, j, L * H:(L + 1) * H])
                    e.tensor_scalar(EB[:, 0:NL * H, H], PH[:, 3, 0:NL * H], -1.0, None, ALU.mult).then_inc(e_made, 2)
                    for g in range(G):
                        for c in range(DC):
                            e.wait_ge(ctx_hi, g * DC + c + 1)
                            dst = (slice(None), 0, c, slice(g * GTOK, (g + 1) * GTOK))
                            e.tensor_tensor(SRC_LO[dst], PROJ[c][:, :], SRC_HI[dst].bitcast(F32),
                                            ALU.subtract).then_inc(ctx_lo, 1)
                        e.wait_ge(x_in[g], 16)
                        norm_stats(e, norm, 0, g)
                        if g < G - 1:
                            norm_apply(e, norm, 0, g)
                        if g >= 1:
                            norm_hi(e, norm, 0, g - 1)
                        if g == 0:
                            round_set(0, 0)
                    e.memset(mx[:, :], 0.0).then_inc(x_settled, 2)
                    with e.Fori(0, NL) as L:
                        e.memset(BWT[:, :, :], 0.0).then_inc(bwt_sum, 1)
                        e.wait_ge(bwt_sum, L * BWTN + 1)
                        e.tensor_copy(BWT[:, :, H + 1], PM[:, bass.ds(L * LNP + 4, 2)]).then_inc(bwt_sum, 1)
                        slots(e, L, slot)

        def mlp(tag, norm, k, b1, w, ready, b2d, func, dst, more):
            LAG, NB = 3, 4
            (w1h, w1l), (w2h, w2l) = w
            with ExitStack() as ph:
                b2b = sb(tag + "b2b", [P, D], scope=ph)
                gf = sb(tag + "gf", [P, NB, 512], scope=ph)
                gh, gl = sb(tag + "gh", [P, NB, 512], F32R, scope=ph), sb(tag + "gl", [P, NB, 512], F32R, scope=ph)
                b2_in = sem(tag + "b2_in")
                up_done, g_full, g_hi, g_lo = sem(tag + "up"), sem(tag + "full"), sem(tag + "hi"), sem(tag + "lo")
                down_used, y_added, b2_added = sem(tag + "dn"), sem(tag + "ya"), sem(tag + "b2a")
                stored = sem(tag + "st")

                def groups(e, body, tail=None):
                    body(0, True)
                    with e.Fori(1, G) as g:
                        body(g, False)
                    if tail is not None:
                        tail()

                with nc.Block() as block:
                    @block.sync
                    def _(e):
                        e.dma_start(b2b[:, :], b2d.partition_broadcast(P)).then_inc(b2_in, 16)
                        if "sync" in more:
                            more["sync"](e)
                        if dst is not None:
                            for g in range(G):
                                e.wait_ge(y_added, 2 * (g + 1))
                                e.dma_start(dst[:, g * GT:(g + 1) * GT, :], X[:, g * GT:(g + 1) * GT, :]).then_inc(stored, 16)
                            e.wait_ge(stored, 16 * G)

                    @block.gpsimd
                    def _(e):
                        def body(g, first):
                            for j in range(FC):
                                q = g * FC + j
                                e.wait_ge(g_hi, q + 1)
                                e.tensor_tensor(gl[:, j % NB, :], gf[:, j % NB, :], gh[:, j % NB, :].bitcast(F32),
                                                ALU.subtract).then_inc(g_lo, 1)
                                if first and j == 0:
                                    norm_lo(e, norm, k, G - 1)
                                    if "gpsimd" in more:
                                        more["gpsimd"](e)
                                    e.wait_ge(b2_in, 16)
                                if j == 3:
                                    xs = X[:, bass.ds(g * GT, GT), :]
                                    e.tensor_tensor(xs, xs, b2b[:, :].unsqueeze(1).to_broadcast([P, GT, D]),
                                                    ALU.add).then_inc(b2_added, 1)

                        groups(e, body)
                        if "gpsimd_end" in more:
                            more["gpsimd_end"](e)

                    @block.scalar
                    def _(e):
                        def body(g, first):
                            for j in range(FC):
                                q = g * FC + j
                                e.wait_ge(up_done, q + 1)
                                if not first or j >= NB:
                                    e.wait_ge(g_lo, q - NB + 1)
                                e.activation(gf[:, j % NB, :], PROJ[j % 4][:, :], func,
                                             bias=b1[:, j:j + 1]).then_inc(g_full, 1)
                                if first and j == 0:
                                    norm_scale(e, norm, k, G - 1)

                        norm_sqrt(e, norm, k, G - 1)
                        groups(e, body)

                    @block.vector
                    def _(e):
                        def add(g):
                            e.wait_ge(b2_added, g + 1)
                            e.wait_ge(down_used, FC * (g + 1))
                            for j in range(2):
                                xs = X[:, bass.ds(g * GT + 2 * j, 2), :]
                                e.tensor_tensor(xs, xs, bank[3 + j][:, :].rearrange("p (t n) -> p t n", n=256),
                                                ALU.add).then_inc(y_added, 1)

                        def body(g, first):
                            for j in range(FC):
                                q = g * FC + j
                                if j == LAG and not first:
                                    add(g - 1)
                                e.wait_ge(g_full, q + 1)
                                if not first or j >= NB:
                                    e.wait_ge(down_used, q - NB + 1)
                                e.tensor_copy(gh[:, j % NB, :], gf[:, j % NB, :]).then_inc(g_hi, 1)
                                if first and j == 0:
                                    norm_hi(e, norm, k, G - 1)
                                    if "vector" in more:
                                        more["vector"](e)

                        norm_apply(e, norm, k, G - 1)
                        groups(e, body, lambda: add(G - 1))
                        if "vector_end" in more:
                            more["vector_end"](e)

                    @block.tensor
                    def _(e):
                        def down(g, q, j, first):
                            e.wait_ge(g_lo, q + 1)
                            if j == 0 and not first:
                                e.wait_ge(y_added, 2 * g)
                            for t in range(GT):
                                ts = slice(t * P, (t + 1) * P)
                                i = three(e, bank[3 + t // 2][:, (t % 2) * 256:(t % 2 + 1) * 256],
                                          gh[:, j % NB, ts], gl[:, j % NB, ts], w2h[:, j // 2, j % 2, :],
                                          w2l[:, j // 2, j % 2, :], j == 0 and t % 2 == 0, j == FC - 1,
                                          skip_group_check=True)
                            i.then_inc(down_used, 1)

                        def body(g, first):
                            toks = bass.ds(g * GTOK, GTOK)
                            for j in range(FC):
                                q = g * FC + j
                                if not first or j >= 4:
                                    e.wait_ge(g_full, q - 3)
                                elif j >= 2:
                                    e.wait_ge(norm.scaled, (k + 1) * G * DC)
                                for c in range(DC):
                                    fs = slice(j % 2 * P, (j % 2 + 1) * P)
                                    i = three(e, PROJ[j % 4][:, :], w1h[:, j // 2, c, fs], w1l[:, j // 2, c, fs],
                                              SRC_HI[:, 1, c, toks], SRC_LO[:, 1, c, toks], c == 0, c == DC - 1)
                                i.then_inc(up_done, 1)
                                if first and j == 1:
                                    norm_turn(e, norm, k, G - 1)
                                if first and j == LAG:
                                    e.wait_ge(*ready[1])
                                if j >= LAG:
                                    down(g, q - LAG, j - LAG, first)
                                elif not first:
                                    down(g - 1, q - LAG, j - LAG + FC, first)
                            if first:
                                e.wait_ge(norm.lo, (k + 1) * G * DC)

                        e.wait_ge(norm.lo, (k + 1) * G * DC - DC)
                        e.wait_ge(*ready[0])
                        groups(e, body, lambda: [down(G - 1, G * FC - LAG + t, FC - LAG + t, False) for t in range(LAG)])

        def round_fc2(e):
            e.wait_ge(w_in[1], 8 * SETS)
            e.tensor_copy(WHI[1][:, :, :, :], W[1][:, :, :, :]).then_inc(w_hi, 1)

        def split_fc2(e):
            e.wait_ge(w_hi, SETS)
            e.tensor_tensor(WLO[1][:, :, :, :], W[1][:, :, :, :], WHI[1][:, :, :, :].bitcast(F32),
                            ALU.subtract).then_inc(w_split, 1)

        def load_l1(e):
            e.wait_ge(w_split, SETS - 1)
            for j, w in enumerate((qw, kw, vw)):
                e.dma_start(W[0][:, j, :, :], w.rearrange("(c p) n -> p c n", p=P)).then_inc(wr_in, 16)

        def round_l1(e):
            e.wait_ge(wr_in, 48)
            e.tensor_copy(wh[:, :, :, :], W[0][:, 0:3, :, :]).then_inc(wh_done, 1)

        def split_l1(e):
            e.wait_ge(wh_done, 1)
            e.tensor_tensor(wl[:, :, :, :], W[0][:, 0:3, :, :], wh[:, :, :, :].bitcast(F32), ALU.subtract).then_inc(wl_done, 1)

        mlp("m0", norm, NL, PM[:, C_M0 + 4:C_M0 + 12], list(zip(WHI, WLO)), ((w_split, SETS - 1), (w_split, SETS)),
            b_fc2, ACT.Gelu, None,
            {"vector": lambda e: (round_fc2(e), round_l1(e)), "gpsimd": lambda e: (split_fc2(e), split_l1(e)),
             "sync": load_l1})

        NK = 2 * S
        GH = NH // DC
        JP = GH // 2
        VW = 2 * DH + 1
        HALF = slice(0, S), slice(S, P)
        wt.close()
        with ExitStack() as l1:
            KL = sb("KL", [P, DC, B, NK], scope=l1)
            VL = sb("VL", [P, B, NH // 2, VW], scope=l1)
            QL = sb("QL", [P, DC, TOK], scope=l1)
            MA = sb("MA", [P, B, NK], BF16, scope=l1)
            ONE = sb("ONE", [P, P], BF16, scope=l1)
            HM = sb("HM", [P, GH], scope=l1)
            swap = sb("swap", [P, P], scope=l1)
            KQ = KL[:, :, :, :].rearrange("p m (t a) (h k) -> p m t (a h) k", a=2, h=2)
            MQ = MA[0:1, :, :].rearrange("p (t a) (h k) -> p t (a h) k", a=2, h=2)
            QB, KB, VB = PM[:, C_QB:C_QB + 2], PM[:, C_KB:C_KB + 2], PM[:, C_VB:C_VB + 2]
            with ExitStack() as ph:
                mask_in = sem("mask_in")
                xl_turned, xl_hi, xl_lo = sem("xl_turned"), sem("xl_hi"), sem("xl_lo")
                one_set, ma_set, v_one = sem("one_set"), sem("ma_set"), sem("v_one")
                ql_done, ql_out, vl_done, vl_out = sem("ql_done"), sem("ql_out"), sem("vl_done"), sem("vl_out")
                swap_set = sem("swap_set")
                mrow = XN[0:1, :, :, :].rearrange("p a t d -> p (a t d)").bitcast(I32)
                VBK = [bank[3], bank[4], bank[7]]
                with nc.Block() as block:
                    @block.sync
                    def _(e):
                        e.dma_start(mrow, mask.rearrange("(a b) s -> a (b s)", a=1)).then_inc(mask_in, 16)

                    @block.gpsimd
                    def _(e):
                        e.memset(VL[:, :, :, 2 * DH], 1.0).then_inc(v_one, 1)
                        e.memset(ONE[:, :], 0.0).then_inc(one_set, 1)
                        e.memset(MA[:, :, :], 0.0).then_inc(ma_set, 1)
                        e.wait_ge(one_set, 1)
                        e.memset(ONE[0:1, :], 1.0).then_inc(one_set, 1)

                    @block.scalar
                    def _(e):
                        for g in range(G):
                            for c in range(DC):
                                e.wait_ge(xl_turned, g * DC + c + 1)
                                e.activation(SRC_HI[:, 1, c, g * GTOK:(g + 1) * GTOK], PROJ[2 * (g % 2) + c][:, :],
                                             ACT.Copy).then_inc(xl_hi, 1)
                        q = 0
                        for g in range(G):
                            for m in range(DC):
                                e.wait_ge(ql_done, q + 1)
                                e.activation(QL[:, m, g * GTOK:(g + 1) * GTOK], bank[q % 3][:, :], ACT.Identity,
                                             bias=QB[:, m:m + 1]).then_inc(ql_out, 1)
                                q += 1
                        for g in range(G):
                            for half in range(2):
                                for m in range(DC):
                                    e.wait_ge(ql_done, q + 1)
                                    part = bank[q % 3][:, :].rearrange("p (t a k) -> p t a k", a=2, k=S)
                                    tiles = slice(g * GT, (g + 1) * GT)
                                    if half == 0:
                                        i = e.activation(KQ[:, m, tiles, 0:4:3, :], part, ACT.Identity, bias=KB[:, m:m + 1])
                                    else:
                                        e.activation(KQ[:, m, tiles, 2, :], part[:, :, 0, :], ACT.Identity, bias=KB[:, m:m + 1])
                                        i = e.activation(KQ[:, m, tiles, 1, :], part[:, :, 1, :], ACT.Identity, bias=KB[:, m:m + 1])
                                    i.then_inc(ql_out, 1)
                                    q += 1

                    @block.vector
                    def _(e):
                        e.tensor_copy(swap[:, 0:S], ident[:, S:P]).then_inc(swap_set, 1)
                        e.tensor_copy(swap[:, S:P], ident[:, 0:S]).then_inc(swap_set, 1)
                        e.tensor_reduce(HM[:, :], ident[:, :].rearrange("p (h d) -> p h d", d=DH), AX_X, ALU.add)
                        for g in range(G):
                            for c in range(DC):
                                e.wait_ge(xl_hi, g * DC + c + 1)
                                toks = slice(g * GTOK, (g + 1) * GTOK)
                                e.tensor_tensor(SRC_LO[:, 1, c, toks], PROJ[2 * (g % 2) + c][:, :],
                                                SRC_HI[:, 1, c, toks].bitcast(F32), ALU.subtract).then_inc(xl_lo, 1)
                        e.wait_ge(mask_in, 16)
                        e.wait_ge(ma_set, 1)
                        e.tensor_scalar(MQ[:, :, 0:4:3, :], mrow.rearrange("p (t a s) -> p t a s", a=2, s=S), 0.0, MASKED,
                                        ALU.is_equal, ALU.mult).then_inc(ma_set, 1)
                        e.wait_ge(v_one, 1)
                        for t in range(NT):
                            e.wait_ge(vl_done, t + 1)
                            part = VBK[t % 3][:, :].rearrange("p (h j d) -> p h j d", h=2, d=2 * DH)
                            e.tensor_copy(VL[HALF[0], 2 * t:2 * t + 2, :, 0:2 * DH], part[HALF[0], :, :, :])
                            e.tensor_copy(VL[HALF[1], 2 * t + 1, :, 0:2 * DH], part[HALF[1], 0, :, :])
                            e.tensor_copy(VL[HALF[1], 2 * t, :, 0:2 * DH], part[HALF[1], 1, :, :]).then_inc(vl_out, 1)

                    @block.tensor
                    def _(e):
                        e.wait_ge(swap_set, 2)
                        for g in range(G):
                            if g >= 2:
                                e.wait_ge(xl_lo, (g - 1) * DC)
                            for c in range(DC):
                                for p in range(GT):
                                    i = e.transpose(PROJ[2 * (g % 2) + c][:, p * P:(p + 1) * P],
                                                    X[:, g * GT + p, c * P:(c + 1) * P], swap[:, :])
                                i.then_inc(xl_turned, 1)
                        e.wait_ge(xl_lo, G * DC)
                        e.wait_ge(wl_done, 1)
                        q = 0
                        for g in range(G):
                            for m in range(DC):
                                if q >= 3:
                                    e.wait_ge(ql_out, q - 2)
                                toks, cols = slice(g * GTOK, (g + 1) * GTOK), slice(m * P, (m + 1) * P)
                                for c in range(DC):
                                    i = three(e, bank[q % 3][:, :], wh[:, 0, c, cols], wl[:, 0, c, cols],
                                              SRC_HI[:, 1, c, toks], SRC_LO[:, 1, c, toks], c == 0, c == DC - 1)
                                i.then_inc(ql_done, 1)
                                q += 1
                        for g in range(G):
                            toks = slice(g * GTOK, (g + 1) * GTOK)
                            for half in range(2):
                                for m in range(DC):
                                    e.wait_ge(ql_out, q - 2)
                                    cols = slice(m * P, (m + 1) * P)
                                    for c in range(DC):
                                        i = three(e, bank[q % 3][:, :], wh[:, 1, c, cols], wl[:, 1, c, cols],
                                                  SRC_HI[:, half, c, toks], SRC_LO[:, half, c, toks], c == 0, c == DC - 1)
                                    i.then_inc(ql_done, 1)
                                    q += 1
                            for t in range(g * GT, (g + 1) * GT):
                                if t >= 3:
                                    e.wait_ge(vl_out, t - 2)
                                ks = slice(t * P, (t + 1) * P)
                                for half in range(2):
                                    for c in range(DC):
                                        i = three(e, VBK[t % 3][:, half * 256:(half + 1) * 256],
                                                  SRC_HI[:, half, c, ks], SRC_LO[:, half, c, ks],
                                                  wh[:, 2, c, :], wl[:, 2, c, :], c == 0, c == DC - 1)
                                i.then_inc(vl_done, 1)

            with ExitStack() as ph:
                QE = [sb(f"QE{a}", [P, GH, S], scope=ph) for a in range(4)]
                PTL = [HT[:, a, :].rearrange("p (j k) -> p j k", k=P) for a in range(2)]
                SUB = [XN[:, a, 0:2, :].rearrange("p t d -> p (t d)") for a in range(2)]
                EXP = [XN[:, a, 2:4, :].rearrange("p t d -> p (t d)") for a in range(2)]
                ml = [sb(f"ml{a}", [P, JP], scope=ph) for a in range(2)]
                rl = [sb(f"rl{a}", [P, JP], scope=ph) for a in range(2)]
                AN = [sb(f"AN{a}", [P, DC, JP, DH], scope=ph) for a in range(2)]
                AT = [sb(f"AT{a}", [P, 2, S], scope=ph) for a in range(2)]
                qe_set, sl_done, ml_done = sem("qe_set"), sem("sl_done"), sem("ml_done")
                subl_done, expl_done, tl_done, tl_out = sem("subl_done"), sem("expl_done"), sem("tl_done"), sem("tl_out")
                al_done, rl_done, an_done = sem("al_done"), sem("rl_done"), sem("an_done")
                at_done, at_out, ao_hi, ao_lo = sem("at_done"), sem("at_out"), sem("ao_hi"), sem("ao_lo")
                STEPS = B * DC
                LT, LP, LA, LR = 2, 3, 6, 8

                def steps(e, slot):
                    for s in range(LR + 1):
                        slot(s, s, 0)
                    rest = (STEPS - LR - 1) // 4
                    with e.Fori(0, rest) as i:
                        for r in range(LR + 1, LR + 5):
                            slot(i * 4 + r, r, i * 2)
                    for s in range(LR + 1 + rest * 4, STEPS + LR):
                        slot(s, s, 0)

                def runs(r, lag):
                    return 0 <= r - lag < STEPS

                with nc.Block() as block:
                    @block.gpsimd
                    def _(e):
                        def slot(s, r, b0):
                            if runs(r, 0):
                                if r >= 4:
                                    e.wait_ge(sl_done, s - 3)
                                other = r // 2 + (1 if r // 2 % 2 == 0 else -1)
                                q = QL[:, r % 2, bass.ds((b0 + other) * S, S)]
                                e.tensor_tensor(QE[r % 4][:, :, :], q.unsqueeze(1).to_broadcast([P, GH, S]),
                                                HM[:, :].unsqueeze(2).to_broadcast([P, GH, S]),
                                                ALU.mult).then_inc(qe_set, 1)
                            if runs(r, LR) and (r - LR) % 2 == 0:
                                b = b0 + (r - LR) // 2
                                e.wait_ge(ao_hi, b + 1)
                                toks = bass.ds(b * S, S)
                                e.tensor_tensor(SRC_LO[:, 1, :, toks], AT[(r - LR) // 2 % 2][:, :, :],
                                                SRC_HI[:, 1, :, toks].bitcast(F32), ALU.subtract).then_inc(ao_lo, 1)

                        steps(e, slot)

                    @block.tensor
                    def _(e):
                        def slot(s, r, b0):
                            if runs(r, 0):
                                b = b0 + r // 2
                                e.wait_ge(qe_set, s + 1)
                                if r >= 2:
                                    e.wait_ge(subl_done, s - 1)
                                e.matmul(bank[r % 2][:, :].rearrange("p (j k) -> p j k", k=NK), ONE[:, :],
                                         MA[:, b, :].unsqueeze(1).to_broadcast([P, JP, NK]), start=True, stop=False,
                                         skip_group_check=True)
                                for j in range(JP):
                                    i = e.matmul(bank[r % 2][:, j * NK:(j + 1) * NK], QE[r % 4][:, 2 * j:2 * j + 2, :],
                                                 KL[:, r % 2, b, :], start=False, stop=(j == JP - 1),
                                                 skip_group_check=True)
                                i.then_inc(sl_done, 1)
                            if runs(r, LT):
                                a = (r - LT) % 2
                                e.wait_ge(expl_done, s - LT + 1)
                                if r - LT >= 2:
                                    e.wait_ge(tl_out, s - LT - 1)
                                for j in range(JP):
                                    i = e.transpose(PROJ[2 + a][:, j * P:(j + 1) * P], EXP[a][:, j * NK:(j + 1) * NK],
                                                    ident[:, :])
                                i.then_inc(tl_done, 1)
                            if runs(r, LP):
                                a, b = (r - LP) % 2, b0 + (r - LP) // 2
                                e.wait_ge(tl_out, s - LP + 1)
                                if r - LP >= 2:
                                    e.wait_ge(an_done, s - LP - 1)
                                for j in range(JP):
                                    i = e.matmul(bank[3 + a][:, j * VW:(j + 1) * VW], PTL[a][:, j, :],
                                                 VL[:, b, a * JP + j, :], start=True, stop=True)
                                i.then_inc(al_done, 1)
                            if runs(r, LA) and (r - LA) % 2 == 0:
                                b, c = b0 + (r - LA) // 2, (r - LA) // 2 % 2
                                e.wait_ge(an_done, 2 * b + 2)
                                if r - LA >= 4:
                                    e.wait_ge(at_out, 2 * b - 2)
                                e.transpose(logits[:, c, 0:P], AN[c][:, :, :, :].rearrange("p m j d -> p (m j d)"),
                                            ident[:, :]).then_inc(at_done, 1)

                        steps(e, slot)

                    @block.scalar
                    def _(e):
                        def slot(s, r, b0):
                            if runs(r, LT):
                                a = (r - LT) % 2
                                e.wait_ge(tl_done, s - LT + 1)
                                e.activation(HT[:, a, :], PROJ[2 + a][:, :],
                                             ACT.Copy).then_inc(tl_out, 1)
                            if runs(r, LA) and (r - LA) % 2 == 0:
                                b, c = b0 + (r - LA) // 2, (r - LA) // 2 % 2
                                e.wait_ge(at_done, b + 1)
                                if r - LA >= 4:
                                    e.wait_ge(ao_lo, b - 1)
                                for h in range(2):
                                    e.activation(AT[c][:, h, :], logits[:, c, h * S:(h + 1) * S], ACT.Identity,
                                                 bias=VB[:, h:h + 1]).then_inc(at_out, 1)
                            if runs(r, 0):
                                e.wait_ge(subl_done, s + 1)
                                e.activation(EXP[r % 2], SUB[r % 2], ACT.Exp, scale=1.0 / DH).then_inc(expl_done, 1)

                        steps(e, slot)

                    @block.vector
                    def _(e):
                        def slot(s, r, b0):
                            if runs(r, 0):
                                a = r % 2
                                e.wait_ge(sl_done, s + 1)
                                lg = bank[a][:, :].rearrange("p (j k) -> p j k", k=NK)
                                e.tensor_reduce(ml[a][:, :], lg, AX_X, ALU.max).then_inc(ml_done, 1)
                                e.wait_ge(ml_done, s + 1)
                                if r >= 2:
                                    e.wait_ge(expl_done, s - 1)
                                e.tensor_tensor(SUB[a].rearrange("p (j k) -> p j k", k=NK), lg,
                                                ml[a][:, :].unsqueeze(2).to_broadcast([P, JP, NK]),
                                                ALU.subtract).then_inc(subl_done, 1)
                            if runs(r, LP):
                                a, c = (r - LP) % 2, (r - LP) // 2 % 2
                                e.wait_ge(al_done, s - LP + 1)
                                res = bank[3 + a][:, 0:JP * VW].rearrange("p (j d) -> p j d", d=VW)
                                e.reciprocal(rl[a][:, :], res[:, :, 2 * DH]).then_inc(rl_done, 1)
                                e.wait_ge(rl_done, s - LP + 1)
                                if a == 0 and r - LP >= 4:
                                    e.wait_ge(at_done, b0 + (r - LP) // 2 - 1)
                                for h in range(2):
                                    i = e.tensor_tensor(AN[c][HALF[h], a, :, :], res[HALF[h], :, h * DH:(h + 1) * DH],
                                                        rl[a][HALF[h], :].unsqueeze(2).to_broadcast([S, JP, DH]), ALU.mult)
                                i.then_inc(an_done, 1)
                            if runs(r, LA) and (r - LA) % 2 == 0:
                                b, c = b0 + (r - LA) // 2, (r - LA) // 2 % 2
                                e.wait_ge(at_out, 2 * b + 2)
                                e.tensor_copy(SRC_HI[:, 1, :, bass.ds(b * S, S)], AT[c][:, :, :]).then_inc(ao_hi, 1)

                        steps(e, slot)

        Y = sb("Y", [P, NT, D])
        W2 = [sb(f"mlp_w{a}", [P, 4, DC, 256]) for a in range(2)]
        W2HI = [sb(f"mlp_whi{a}", [P, 4, DC, 256], F32R) for a in range(2)]
        W2LO = [sb(f"mlp_wlo{a}", [P, 4, DC, 256], F32R) for a in range(2)]
        w2_in, w2_hi, w2_split = [sem(f"mlp_w_in{a}") for a in range(2)], sem("mlp_w_hi"), sem("mlp_w_split")
        norm1 = Norm("rn", Y, True, RMS_EPS, PM[:, C_PN:C_PN + 2])
        with ExitStack() as ph:
            owr = sb("owr", [P, 2, D], scope=ph)
            owh, owl = sb("owh", [P, 2, D], F32R, scope=ph), sb("owl", [P, 2, D], F32R, scope=ph)
            obb = sb("obb", [P, D], scope=ph)
            ow_in, ob_in, owh_done, owl_done = sem("ow_in"), sem("ob_in"), sem("owh_done"), sem("owl_done")
            OB = [bank[3], bank[4]]
            y_base, y_prod, y_sum = sem("y_base"), sem("y_prod"), sem("y_sum")
            with nc.Block() as block:
                @block.sync
                def _(e):
                    e.dma_start(owr[:, :, :], ow.rearrange("e p n -> p e n")).then_inc(ow_in, 16)
                    e.dma_start(obb[:, :], out_b.partition_broadcast(P)).then_inc(ob_in, 16)
                    for a in range(2):
                        e.dma_start(W2[a][:, :, :, :], (w1, w2)[a].rearrange("j (c p) n -> p j c n", p=P)
                                    ).then_inc(w2_in[a], 16)

                @block.gpsimd
                def _(e):
                    e.wait_ge(ow_in, 16)
                    e.tensor_copy(owh[:, :, :], owr[:, :, :]).then_inc(owh_done, 1)
                    e.wait_ge(owh_done, 1)
                    e.tensor_tensor(owl[:, :, :], owr[:, :, :], owh[:, :, :].bitcast(F32),
                                    ALU.subtract).then_inc(owl_done, 1)
                    for a in range(2):
                        e.wait_ge(w2_hi, a + 1)
                        e.tensor_tensor(W2LO[a][:, :, :, :], W2[a][:, :, :, :], W2HI[a][:, :, :, :].bitcast(F32),
                                        ALU.subtract).then_inc(w2_split, 1)
                        if a == 0:
                            for g in range(G - 1):
                                norm_lo(e, norm1, 0, g)

                @block.scalar
                def _(e):
                    for g in range(G - 1):
                        norm_sqrt(e, norm1, 0, g)
                        norm_scale(e, norm1, 0, g)

                @block.vector
                def _(e):
                    e.wait_ge(ob_in, 16)
                    for g in range(G):
                        ts = slice(g * GT, (g + 1) * GT)
                        e.tensor_tensor(Y[:, ts, :], X[:, ts, :], obb[:, :].unsqueeze(1).to_broadcast([P, GT, D]),
                                        ALU.add).then_inc(y_base, 1)
                    e.wait_ge(y_base, G)
                    for g in range(G):
                        for v in (2 * g, 2 * g + 1):
                            e.wait_ge(y_prod, v + 1)
                            ys = Y[:, 2 * v:2 * v + 2, :]
                            e.tensor_tensor(ys, ys, OB[v % 2][:, :].rearrange("p (t n) -> p t n", n=256),
                                            ALU.add).then_inc(y_sum, 1)
                        e.wait_ge(y_sum, 2 * g + 2)
                        norm_stats(e, norm1, 0, g)
                        if g < G - 1:
                            norm_apply(e, norm1, 0, g)
                        if g >= 1:
                            norm_hi(e, norm1, 0, g - 1)
                        if g < 2:
                            e.wait_ge(w2_in[g], 16)
                            e.tensor_copy(W2HI[g][:, :, :, :], W2[g][:, :, :, :]).then_inc(w2_hi, 1)

                @block.tensor
                def _(e):
                    e.wait_ge(owl_done, 1)
                    for g in range(G):
                        for v in (2 * g, 2 * g + 1):
                            if v >= 2:
                                e.wait_ge(y_sum, v - 1)
                            for t in (2 * v, 2 * v + 1):
                                ts = slice(t * P, (t + 1) * P)
                                for h in range(2):
                                    i = three(e, OB[v % 2][:, (t % 2) * 256:(t % 2 + 1) * 256], SRC_HI[:, 1, h, ts],
                                              SRC_LO[:, 1, h, ts], owh[:, h, :], owl[:, h, :], h == 0, h == 1)
                            i.then_inc(y_prod, 1)
                        if g >= 1:
                            if g >= 2:
                                e.wait_ge(norm1.scaled, (g - 1) * DC)
                            norm_turn(e, norm1, 0, g - 1)

        mlp("m1", norm1, 0, PM[:, C_B1:C_B1 + 8], list(zip(W2HI, W2LO)), ((w2_split, 1), (w2_split, 2)), b2,
            ACT.Gelu_apprx_tanh, out.rearrange("(t p) d -> p t d", p=P), {})


def kernel(**inputs):
    import numpy as np
    import concourse.bacc as bacc
    from concourse.bass_utils import run_bass_kernel_spmd

    def given(name):
        return np.asarray(inputs[name])

    def both(name):
        return [given(f"L0_xattn_{name}{i}") for i in (1, 2)]

    def pairs(ws):
        return np.stack([w.reshape(D, HP, 2 * K).transpose(1, 0, 2) for w in ws])

    def sets(up, down):
        return [given(up).reshape(D, 4, 256).transpose(1, 0, 2)[None], given(down).reshape(1, 4, 256, D)]

    def rows(*vs):
        return np.concatenate([v.reshape(-1, P) for v in vs])

    kv_w, kv_b = given("L1_xattn_kv_w").reshape(D, D, 2), given("L1_xattn_kv_b").reshape(D, 2)
    arrays = {
        "x": given("x").reshape(TOK, D),
        "ctx": given("ctx_2048").reshape(TOK, D),
        "mask": given("mask_BxS2_ik0"),
        "wall": np.concatenate([np.stack([pairs(both("wq")), pairs(both("wk")), pairs(both("wv")),
                          np.stack([w.reshape(HP, 2 * K, D) for w in both("wo")])], axis=2
                         ).reshape(NL * HP, 4, 256, 256), *sets("L0_xattn_w_fc1", "L0_xattn_w_fc2")]),
        "vech": rows(*both("bq"), *both("bk"), *both("bias_k"), *both("bv"), *both("bias_v")),
        "vecm": rows(*[given(f"L0_xattn_{n}") for i in (1, 2)
                       for n in (f"ln{i}_scale", f"ln{i}_offset", f"bo{i}")],
                     given("L0_xattn_ln_mlp_scale"), given("L0_xattn_ln_mlp_offset"), given("L0_xattn_b_fc1"),
                     given("L1_xattn_q_b"), kv_b[:, 0],
                     kv_b[:, 1].reshape(NH // 2, 2, DH).transpose(1, 0, 2),
                     given("L1_xattn_postnorm_w"), given("L1_xattn_mlp_b1")),
        "b_fc2": given("L0_xattn_b_fc2"),
        "qw": given("L1_xattn_q_w"), "kw": kv_w[:, :, 0], "vw": kv_w[:, :, 1],
        "ow": given("L1_xattn_out_w").reshape(NH // 2, 2, DH, D).transpose(1, 0, 2, 3).reshape(2, P, D),
        "out_b": given("L1_xattn_out_b"),
        "w1": sets("L1_xattn_mlp_w1", "L1_xattn_mlp_w2")[0][0], "w2": sets("L1_xattn_mlp_w1", "L1_xattn_mlp_w2")[1][0], "b2": given("L1_xattn_mlp_b2"),
    }
    nc = bacc.Bacc("TRN2", target_bir_lowering=False, num_devices=1)
    arrays = {f"in_{k}": np.ascontiguousarray(v) for k, v in arrays.items()}
    args = [nc.dram_tensor(k, v.shape, mybir.dt.from_np(v.dtype), kind="ExternalInput").ap()
            for k, v in arrays.items()]
    out = nc.dram_tensor("out", (TOK, D), F32, kind="ExternalOutput").ap()
    program(nc, *args, out)
    r = run_bass_kernel_spmd(nc, [arrays], core_ids=[0])
    return r.results[0]["out"].reshape(B, S, D)
```

```python
from contextlib import ExitStack

import concourse.bass as bass
from concourse import mybir

ALU = mybir.AluOpType
ACT = mybir.ActivationFunctionType
F32 = mybir.dt.float32
F32R = mybir.dt.float32r
BF16 = mybir.dt.bfloat16
I32 = mybir.dt.int32
AX_X = mybir.AxisListType.X

B, S, D = 32, 64, 256
TOK = B * S
P = 128
NT = TOK // P
DC = D // P
H, K = 16, 128
HP = H // 2
NL = 2
G = 4
GT = NT // G
GTOK = TOK // G
UNITS = HP * G
F = 1024
FC = F // P
NH, DH = 16, 16
KEYS = S + 1
LN_EPS, RMS_EPS = 1e-5, 1e-6
MASKED = -1e30
ROWS_H = 5 * NL * H
LNP = 6
C_M0 = NL * LNP
C_QB = C_M0 + 12
C_KB = C_QB + 2
C_VB = C_KB + 2
C_PN = C_VB + 2
C_B1 = C_PN + 2
ROWS_M = C_B1 + 8
OLD = 8


def program(nc, x, ctx_in, mask, wall, vech, vecm, b_fc2, qw, kw, vw, ow, out_b, w1, w2, b2, out):
    es = ExitStack()
    with es:
        def sem(name):
            return es.enter_context(nc.semaphore(name))

        def sb(name, shape, dt=F32, scope=es):
            return scope.enter_context(nc.sbuf_tensor(name, shape, dt))

        bank = [es.enter_context(nc.psum_tensor(f"bank{i}", [P, 512], F32)) for i in range(5)]
        logits = es.enter_context(nc.psum_tensor("logits", [P, 2, 512], F32))
        bank += [None, None, es.enter_context(nc.psum_tensor("bank7", [P, 512], F32))]
        PROJ = [bank[0], bank[1], bank[2], bank[7]]
        WIDE = PROJ + [logits[:, 0, :], logits[:, 1, :]]

        X = sb("X", [P, NT, D])
        SRC_HI = sb("SRC_HI", [P, 2, DC, TOK], F32R)
        SRC_LO = sb("SRC_LO", [P, 2, DC, TOK], F32R)
        ident = sb("ident", [P, P])
        PH = sb("PH", [P, 5, NL * H + 4])
        PM = sb("PM", [P, ROWS_M])
        st = sb("st", [P, NT, 6])
        mv = sb("mv", [P, NT, 2])
        ms = sb("ms", [P, NT])
        sd = sb("sd", [P, NT])
        rs = sb("rs", [P, NT])
        XN = sb("XN", [P, 2, GT, D])
        HT = sb("HT", [P, 2, 512])

        class Norm:
            def __init__(self, tag, src, rms, eps, prm):
                self.src, self.rms, self.eps, self.prm = src, rms, eps, prm
                self.stat, self.sqrt, self.rstd = sem(tag + "_stat"), sem(tag + "_sqrt"), sem(tag + "_rstd")
                self.xn, self.turned, self.scaled = sem(tag + "_xn"), sem(tag + "_turned"), sem(tag + "_scaled")
                self.full, self.lo = sem(tag + "_full"), sem(tag + "_lo")
                self.stats = GT if rms else 2 * GT + 1

        def after(k, g, lag):
            return g >= lag or not (isinstance(k, int) and k == 0)

        def norm_stats(e, n, k, g):
            at, ts = (k * G + g) * n.stats, slice(g * GT, (g + 1) * GT)
            e.memset(ms[:, ts], n.eps)
            for t in range(g * GT, (g + 1) * GT):
                e.bn_stats(st[:, t, :], n.src[:, t, :]).then_inc(n.stat, 1)
            e.wait_ge(n.stat, at + GT)
            e.memset(rs[:, ts], 0.0)
            for t in range(g * GT, (g + 1) * GT):
                e.bn_aggr(mv[:, t, :], st[:, t, :]).then_inc(n.stat, 1)
            e.wait_ge(n.stat, at + 2 * GT)
            e.tensor_tensor(ms[:, ts], mv[:, ts, 1], ms[:, ts], ALU.add).then_inc(n.stat, 1)

        def norm_sqrt(e, n, k, g):
            if n.rms:
                for t in range(g * GT, (g + 1) * GT):
                    e.activation(n.squares[:, t % GT, :], n.src[:, t, :], ACT.Square, accum_out=ms[:, t:t + 1]).then_inc(n.stat, 1)
            e.wait_ge(n.stat, (k * G + g + 1) * n.stats)
            if n.rms:
                e.activation(sd[:, g * GT:(g + 1) * GT], ms[:, g * GT:(g + 1) * GT], ACT.Sqrt, scale=1.0 / D,
                             bias=n.eps_col[:, :]).then_inc(n.sqrt, 1)
                return
            e.activation(sd[:, g * GT:(g + 1) * GT], ms[:, g * GT:(g + 1) * GT], ACT.Sqrt).then_inc(n.sqrt, 1)

        def norm_rstd(e, n, k, g):
            e.wait_ge(n.sqrt, k * G + g + 1)
            e.reciprocal(rs[:, g * GT:(g + 1) * GT], sd[:, g * GT:(g + 1) * GT]).then_inc(n.rstd, 1)

        def norm_apply(e, n, k, g):
            q = k * G + g
            e.wait_ge(n.rstd, q + 1)
            if after(k, g, 2):
                e.wait_ge(n.turned, (q - 1) * DC)
            for p in range(GT):
                t = g * GT + p
                if n.rms:
                    i = e.tensor_scalar(XN[:, g % 2, p, :], n.src[:, t, :], rs[:, t:t + 1], None, ALU.mult)
                else:
                    i = e.tensor_scalar(XN[:, g % 2, p, :], n.src[:, t, :], mv[:, t, 0:1], rs[:, t:t + 1],
                                        ALU.subtract, ALU.mult)
            i.then_inc(n.xn, 1)

        def norm_turn(e, n, k, g, banks):
            e.wait_ge(n.xn, k * G + g + 1)
            for c in range(DC):
                for p in range(GT):
                    i = e.transpose(banks[c][:, p * P:(p + 1) * P], XN[:, g % 2, p, c * P:(c + 1) * P], ident[:, :])
                i.then_inc(n.turned, 1)

        def norm_scale(e, n, k, g, banks):
            for c in range(DC):
                q = (k * G + g) * DC + c
                e.wait_ge(n.turned, q + 1)
                if after(k, g, 1):
                    e.wait_ge(n.lo, q - 1)
                for dst, done in ((HT[:, c, :], n.full), (SRC_HI[:, 1, c, g * GTOK:(g + 1) * GTOK], n.scaled)):
                    if n.rms:
                        i = e.activation(dst, banks[c][:, :], ACT.Copy, scale=n.prm[:, c:c + 1])
                    else:
                        i = e.activation(dst, banks[c][:, :], ACT.Identity, scale=n.prm[:, c:c + 1],
                                         bias=n.prm[:, 2 + c:3 + c])
                    i.then_inc(done, 1)

        def norm_lo(e, n, k, g):
            for c in range(DC):
                e.wait_ge(n.full, (k * G + g) * DC + c + 1)
                e.wait_ge(n.scaled, (k * G + g) * DC + c + 1)
                toks = slice(g * GTOK, (g + 1) * GTOK)
                e.tensor_tensor(SRC_LO[:, 1, c, toks], HT[:, c, :], SRC_HI[:, 1, c, toks].bitcast(F32),
                                ALU.subtract).then_inc(n.lo, 1)

        def three(e, dst, a_hi, a_lo, b_hi, b_lo, start, stop, **kw):
            e.matmul(dst, a_hi, b_hi, start=start, stop=False, **kw)
            e.matmul(dst, a_hi, b_lo, start=False, stop=False, **kw)
            return e.matmul(dst, a_lo, b_hi, start=False, stop=stop, **kw)

        CUR = sb("CUR", [P, 4])
        wh = sb("wh", [P, 3, DC, D], F32R)
        wl = sb("wl", [P, 3, DC, D], F32R)
        wr_in, wh_done, wl_done = sem("wr_in"), sem("wh_done"), sem("wl_done")
        wt = es.enter_context(ExitStack())
        W = [sb(f"W{a}", [P, 4, DC, 256], scope=wt) for a in range(2)]
        WHI = [sb(f"WHI{a}", [P, 4, DC, 256], F32R, scope=wt) for a in range(2)]
        WLO = [sb(f"WLO{a}", [P, 4, DC, 256], F32R, scope=wt) for a in range(2)]
        SETS = NL * HP + 2
        w_in = [sem(f"w_in{a}") for a in range(2)]
        w_hi, w_split = sem("w_hi"), sem("w_split")
        norm = Norm("ln", X, False, LN_EPS, CUR)

        with ExitStack() as ph:
            vh = HT[0:ROWS_H // 2, 0, 0:2 * P].rearrange("p (a k) -> p a k", k=P)
            vm, one = HT[0:ROWS_M, 0, 2 * P:3 * P], HT[:, 1, 0:P]
            PB = [sb(f"PB{a}", [P, 5, 2], scope=ph) for a in range(2)]
            E2 = [sb(f"E2{a}", [P, 2, 32], scope=ph) for a in range(2)]
            EA = sb("EA", [P, 2 * SETS, 32], scope=ph)
            EB = sb("EB", [P, 2 * SETS, 32], scope=ph)
            BWT = sb("BWT", [P, DC, 32], scope=ph)
            BW = sb("BW", [32, D], scope=ph)
            PTB = sb("PTB", [P, NT, 32], scope=ph)
            PTT = sb("PTT", [32, 2, 512], scope=ph)
            QT = sb("QT", [P, 2, GTOK], scope=ph)
            KT = sb("KT", [P, 2, GTOK // S, KEYS], scope=ph)
            V = [sb(f"V{a}", [P, GT, 256], scope=ph) for a in range(2)]
            CB = PROJ[0:2], bank[3:5]
            cin = V
            mx = sb("mx", [P, 2 * GT], scope=ph)
            sub = sb("sub", [P, 2 * GT, KEYS], scope=ph)
            ex = sb("ex", [P, 2 * GT, KEYS], scope=ph)
            sm = sb("sm", [P, 2 * GT], scope=ph)
            ri = sb("ri", [P, 2 * GT], scope=ph)
            PR = sb("PR", [P, 2 * GT, S], scope=ph)
            PRT = sb("PRT", [P, 2 * GT, P], scope=ph)
            CHI = sb("CHI", [P, 2, GTOK], F32R, scope=ph)
            CLO = sb("CLO", [P, 2, GTOK], F32R, scope=ph)
            SCALE = float(K) ** -0.5
            BWTN = HP + 2
            LASTP = OLD - G

            vec_in = sem("vec_in")
            ctx_in_g, x_in = [sem(f"ctx_in{g}") for g in range(G)], [sem(f"x_in{g}") for g in range(G)]
            ident_one, ident_done, zeros_set = sem("ident_one"), sem("ident_done"), sem("zeros_set")
            vec_turned, vec_copied = sem("vec_turned"), sem("vec_copied")
            ctx_turned, ctx_hi, ctx_lo = sem("ctx_turned"), sem("ctx_hi"), sem("ctx_lo")
            bw_done, e_made, cur_set = sem("bw_done"), sem("e_made"), sem("cur_set")
            q_done, k_done, v_done, s_done = sem("q_done"), sem("k_done"), sem("v_done"), sem("s_done")
            c_done, o_done = sem("c_done"), sem("o_done")
            q_out, k_out, v_out, exp_done = sem("q_out"), sem("k_out"), sem("v_out"), sem("exp_done")
            pt_out, c_hi, c_lo, kb_set = sem("pt_out"), sem("c_hi"), sem("c_lo"), sem("kb_set")
            mx_done, sub_done, sm_done, ri_done = sem("mx_done"), sem("sub_done"), sem("sm_done"), sem("ri_done")
            p_ready, x_settled, bwt_sum = sem("p_ready"), sem("x_settled"), sem("bwt_sum")
            bw_turned, bw_out, ptb_turned, ptb_out = sem("bw_turned"), sem("bw_out"), sem("ptb_turned"), sem("ptb_out")

            def turning(L, at, last):
                if at == 0:
                    return L, G - 1
                if last and at > LASTP + 1:
                    return L + 1, at - LASTP - 2
                return None

            def slots(e, L, slot):
                slot(L, L * UNITS, 0, L * HP, None, False)
                with e.Fori(0, UNITS // OLD - 1) as i:
                    for u in range(OLD):
                        slot(L, L * UNITS + i * OLD + u + 1, u + 1, L * HP + i * 2 + (u + 1) // G, i * 2 + u // G, False)
                i = UNITS // OLD - 1
                for u in range(OLD):
                    slot(L, L * UNITS + i * OLD + u + 1, u + 1,
                         L * HP + i * 2 + (u + 1) // G if u < OLD - 1 else None, i * 2 + u // G, True)

            with nc.Block() as block:
                @block.sync
                def _(e):
                    def load(m, a):
                        e.dma_start(W[a][:, :, :, :], wall[m].rearrange("j (c p) n -> p j c n", p=P)).then_inc(w_in[a], 16)

                    ct, xt = (v.rearrange("(t p) d -> p t d", p=P) for v in (ctx_in, x))
                    for g in range(G):
                        ts = slice(g * GT, (g + 1) * GT)
                        if g >= 2:
                            e.wait_ge(ctx_turned, (g - 1) * DC)
                        e.dma_start(cin[g % 2][:, :, :], ct[:, ts, :]).then_inc(ctx_in_g[g], 16)
                        e.dma_start(X[:, ts, :], xt[:, ts, :]).then_inc(x_in[g], 16)
                        if g == 0:
                            load(0, 0)
                    load(1, 1)
                    with e.Fori(1, SETS // 2) as i:
                        for a in range(2):
                            m = i * 2
                            e.wait_ge(w_split, m + a - 1)
                            e.wait_ge(bw_done, m + a - 1)
                            load(m + a, a)

                @block.gpsimd
                def _(e):
                    e.memset(one, 1.0).then_inc(ident_one, 1)
                    e.wait_ge(ident_one, 1)
                    e.affine_select(out=ident[:, :], in_=one, compare_op=ALU.is_equal, fill=0.0, base=0,
                                    pattern=[[-1, P]], channel_multiplier=1).then_inc(ident_done, 1)
                    e.memset(EA[:, :, :], 0.0)
                    e.memset(EB[:, :, :], 0.0).then_inc(e_made, 1)
                    e.memset(PTB[:, :, :], 1.0)
                    e.memset(PRT[:, :, :], 0.0).then_inc(zeros_set, 1)

                    def split(m, a):
                        e.wait_ge(w_hi, m + 1)
                        for j in range(4):
                            i = e.tensor_tensor(WLO[a][:, j, :, :], W[a][:, j, :, :],
                                                WHI[a][:, j, :, :].bitcast(F32), ALU.subtract)
                        e.tensor_tensor(E2[a][:, :, :], EA[:, bass.ds(2 * m, 2), :], EB[:, bass.ds(2 * m, 2), :],
                                        ALU.subtract)
                        e.tensor_copy(PB[a][:, :, :], PH[:, :, bass.ds(2 * m, 2)]).then_inc(w_split, 1)

                    e.wait_ge(e_made, 3)
                    split(0, 0)
                    for g in range(G - 1):
                        norm_lo(e, norm, 0, g)
                    with e.Fori(0, NL) as L:
                        norm_lo(e, norm, L, G - 1)
                        split(L * HP + 1, 1)
                        with e.Fori(0, HP // 2 - 1) as i:
                            for a in range(2):
                                split(L * HP + i * 2 + 2 + a, a)
                        split(L * HP + HP, 0)
                        for g in range(G - 1):
                            norm_lo(e, norm, L + 1, g)

                @block.tensor
                def _(e):
                    def slot(L, n, at, pair, hp, last):
                        g, a, ab = at % G, (at // G) % 2, ((at - 1) // G) % 2
                        front, back = pair is not None, hp is not None
                        toks = slice(g * GTOK, (g + 1) * GTOK)
                        norm_now, bridge = turning(L, at, last), last and at > LASTP
                        if front:
                            if g == 0:
                                e.wait_ge(w_split, pair + 1)
                            if at < G:
                                e.wait_ge(norm.lo, (L * G + at + 1) * DC)
                            for j, half, done, free in ((0, 1, q_done, v_out), (1, 0, k_done, k_out)):
                                if j == 1 and norm_now is not None:
                                    e.wait_ge(norm.scaled, (norm_now[0] * G + norm_now[1]) * DC)
                                if j == 1 and at == 1:
                                    e.wait_ge(norm.scaled, (L + 1) * G * DC)
                                if j == 1 and last and at > LASTP + 1:
                                    e.wait_ge(ptb_out, L * G + at - LASTP - 1)
                                    e.wait_ge(bw_out, L + 1)
                                for h in range(2):
                                    if back:
                                        e.wait_ge(free, 2 * n - 1 + h)
                                    for c in range(DC):
                                        i = three(e, PROJ[2 * j + h][:, :], WHI[a][:, j, c, h * K:(h + 1) * K],
                                                  WLO[a][:, j, c, h * K:(h + 1) * K], SRC_HI[:, half, c, toks],
                                                  SRC_LO[:, half, c, toks], c == 0, c == DC - 1)
                                    i.then_inc(done, 1)
                        def values(j):
                            e.wait_ge(q_out, 2 * n + j + 1)
                            for p in range(2):
                                t = g * GT + 2 * j + p
                                for c in range(DC):
                                    i = three(e, PROJ[j][:, p * 256:(p + 1) * 256],
                                              SRC_HI[:, 0, c, t * P:(t + 1) * P], SRC_LO[:, 0, c, t * P:(t + 1) * P],
                                              WHI[a][:, 2, c, :], WLO[a][:, 2, c, :], c == 0, c == DC - 1)
                            i.then_inc(v_done, 1)

                        if front:
                            values(0)
                        if bridge:
                            e.wait_ge(p_ready, n)
                            if front:
                                e.wait_ge(k_out, 2 * n + 2)
                            else:
                                e.wait_ge(norm.scaled, ((L + 1) * G + G - 2) * DC)
                            gb = at - LASTP - 1
                            for p in range(GT):
                                i = e.transpose(PROJ[2][0:32, p * P:(p + 1) * P], PTB[:, gb * GT + p, :], ident[:, :])
                            i.then_inc(ptb_turned, 1)
                            if gb == 0:
                                e.wait_ge(bwt_sum, (L + 1) * BWTN)
                                for c in range(DC):
                                    i = e.transpose(PROJ[3][0:32, c * P:(c + 1) * P], BWT[:, c, :], ident[:, :])
                                i.then_inc(bw_turned, 1)
                        if back:
                            e.wait_ge(v_out, 2 * n)
                            e.wait_ge(pt_out, n)
                            e.wait_ge(x_settled, 2 * n)
                            for h in range(2):
                                for p in range(GT):
                                    i = e.matmul(bank[3 + h][:, p * P:(p + 1) * P],
                                                 V[(at - 1) % 2][:, p, h * K:(h + 1) * K],
                                                 PRT[:, h * GT + p, :], start=True, stop=True)
                                i.then_inc(c_done, 1)
                        if front:
                            values(1)
                        if at == 0:
                            e.wait_ge(k_out, 2 * n + 2)
                            norm_turn(e, norm, *norm_now, PROJ[2:])
                        if front:
                            e.wait_ge(q_out, 2 * n + 2)
                            e.wait_ge(k_out, 2 * n + 2)
                            e.wait_ge(kb_set, n + 1)
                            if back:
                                e.wait_ge(sub_done, n)
                            if g == 0:
                                for c in range(DC):
                                    for h in range(2):
                                        i = e.matmul(logits[:, 1, 448 + 32 * c:480 + 32 * c],
                                                     W[a][:, 3, h, c * P:(c + 1) * P], E2[a][:, h, :],
                                                     start=(h == 0), stop=(h == 1))
                                i.then_inc(bw_done, 1)
                            for h in range(2):
                                for q in range(GTOK // S):
                                    p, b = q // 2, q % 2
                                    i = e.matmul(logits[b * S:(b + 1) * S, h, p * KEYS:(p + 1) * KEYS],
                                                 QT[:, h, q * S:(q + 1) * S], KT[:, h, q, :], start=True, stop=True)
                            i.then_inc(s_done, 1)
                        if norm_now is not None and bridge and front:
                            e.wait_ge(ptb_out, L * G + at - LASTP)
                            norm_turn(e, norm, *norm_now, PROJ[2:])
                        if back:
                            e.wait_ge(c_lo, 2 * n)
                            if bridge:
                                e.wait_ge(bw_out, L + 1)
                                e.wait_ge(ptb_out, L * G + at - LASTP)
                            for j in range(2):
                                for p in range(2):
                                    ts = slice((2 * j + p) * P, (2 * j + p + 1) * P)
                                    dst = bank[3 + j][:, p * 256:(p + 1) * 256]
                                    if bridge:
                                        e.matmul(dst, PTT[:, (at - LASTP - 1) % 2, ts], BW[:, :], start=True, stop=False)
                                    for h in range(2):
                                        i = three(e, dst, CHI[:, h, ts], CLO[:, h, ts], WHI[ab][:, 3, h, :],
                                                  WLO[ab][:, 3, h, :], h == 0 and not bridge, h == 1)
                                i.then_inc(o_done, 1)
                        if norm_now is not None and not front:
                            norm_turn(e, norm, *norm_now, PROJ[2:])
                    e.wait_ge(ident_done, 1)
                    e.wait_ge(vec_in, 32)
                    half = ROWS_H // 2
                    for a in range(2):
                        e.transpose(bank[3][:, a * half:(a + 1) * half], vh[:, a, :], ident[0:half, 0:half])
                    e.transpose(bank[3][:, ROWS_H:ROWS_H + ROWS_M], vm,
                                ident[0:ROWS_M, 0:ROWS_M]).then_inc(vec_turned, 1)
                    for g in range(G):
                        e.wait_ge(ctx_in_g[g], 16)
                        if g == 1:
                            e.wait_ge(vec_copied, 2)
                        if g >= 2:
                            e.wait_ge(ctx_lo, (g - 1) * DC)
                        for c in range(DC):
                            for p in range(GT):
                                i = e.transpose(CB[g % 2][c][:, p * P:(p + 1) * P], cin[g % 2][:, p, c * P:(c + 1) * P],
                                                ident[:, :])
                            i.then_inc(ctx_turned, 1)
                        for k in ((), (), (0,), (1, 2))[g]:
                            if k >= 1:
                                e.wait_ge(norm.scaled, k * DC)
                            norm_turn(e, norm, 0, k, PROJ[2:])
                    e.wait_ge(ctx_lo, G * DC)
                    with e.Fori(0, NL) as L:
                        slots(e, L, slot)

                @block.scalar
                def _(e):
                    def slot(L, n, at, pair, hp, last):
                        a = (at // G) % 2
                        front, back = pair is not None, hp is not None
                        norm_now, bridge = turning(L, at, last), last and at > LASTP
                        if front:
                            for h in range(2):
                                e.wait_ge(q_done, 2 * n + h + 1)
                                e.activation(QT[:, h, :], PROJ[h][:, :], ACT.Identity,
                                             bias=PB[a][:, 0, h:h + 1]).then_inc(q_out, 1)
                            for h in range(2):
                                e.wait_ge(k_done, 2 * n + h + 1)
                                e.activation(KT[:, h, :, 0:S], PROJ[2 + h][:, :].rearrange("p (q k) -> p q k", k=S),
                                             ACT.Identity, bias=PB[a][:, 1, h:h + 1]).then_inc(k_out, 1)
                        def values_out(j):
                            e.wait_ge(v_done, 2 * n + j + 1)
                            e.activation(V[at % 2][:, 2 * j:2 * j + 2, :],
                                         PROJ[j][:, :].rearrange("p (t n) -> p t n", n=256),
                                         ACT.Copy).then_inc(v_out, 1)

                        if at == 0:
                            norm_sqrt(e, norm, *norm_now)
                        if front:
                            values_out(0)
                        if bridge:
                            e.wait_ge(ptb_turned, L * G + at - LASTP)
                            e.activation(PTT[:, (at - LASTP - 1) % 2, :], PROJ[2][0:32, :], ACT.Copy).then_inc(ptb_out, 1)
                        if bridge and norm_now is not None and front:
                            norm_sqrt(e, norm, *norm_now)
                        if back:
                            for h in range(2):
                                e.wait_ge(c_done, 2 * n - 1 + h)
                                e.activation(CHI[:, h, :], bank[3 + h][:, :], ACT.Copy).then_inc(c_hi, 1)
                        if norm_now is not None and not front:
                            norm_sqrt(e, norm, *norm_now)
                        if front:
                            values_out(1)
                        if at == 0:
                            e.wait_ge(cur_set, norm_now[0] + 1)
                            norm_scale(e, norm, *norm_now, PROJ[2:])
                        if front:
                            e.wait_ge(sub_done, n + 1)
                            e.activation(ex[:, :, :], sub[:, :, :], ACT.Exp, scale=SCALE).then_inc(exp_done, 1)
                        if bridge and norm_now is not None:
                            e.wait_ge(cur_set, norm_now[0] + 1)
                            norm_scale(e, norm, *norm_now, PROJ[2:])

                    e.dma_start(vh, vech.rearrange("(a r) k -> r a k", a=2)).then_inc(vec_in, 16)
                    e.dma_start(vm, vecm).then_inc(vec_in, 16)
                    def ctx_round(g):
                        for c in range(DC):
                            e.wait_ge(ctx_turned, g * DC + c + 1)
                            e.activation(SRC_HI[:, 0, c, g * GTOK:(g + 1) * GTOK], CB[g % 2][c][:, :],
                                         ACT.Copy).then_inc(ctx_hi, 1)

                    ctx_round(0)
                    norm_sqrt(e, norm, 0, 0)
                    ctx_round(1)
                    ctx_round(2)
                    e.wait_ge(cur_set, 1)
                    norm_scale(e, norm, 0, 0, PROJ[2:])
                    norm_sqrt(e, norm, 0, 1)
                    ctx_round(3)
                    norm_sqrt(e, norm, 0, 2)
                    norm_scale(e, norm, 0, 1, PROJ[2:])
                    norm_scale(e, norm, 0, 2, PROJ[2:])
                    with e.Fori(0, NL) as L:
                        slots(e, L, slot)

                @block.vector
                def _(e):
                    logit = logits[:, :, 0:GT * KEYS].rearrange("p h (t k) -> p h t k", k=KEYS)

                    def slot(L, n, at, pair, hp, last):
                        g, a, gb = at % G, (at // G) % 2, (at - 1) % G
                        front, back = pair is not None, hp is not None
                        norm_now, bridge = turning(L, at, last), last and at > LASTP
                        if front:
                            if g == 0:
                                e.wait_ge(w_split, pair + 1)
                            e.tensor_copy(KT[:, :, :, S], PB[a][:, 2, :].unsqueeze(2).to_broadcast([P, 2, GTOK // S])
                                          ).then_inc(kb_set, 1)
                        if back:
                            e.wait_ge(exp_done, n)
                            e.tensor_reduce(sm[:, :], ex[:, :, :], AX_X, ALU.add).then_inc(sm_done, 1)
                            e.wait_ge(sm_done, n)
                            e.reciprocal(ri[:, :], sm[:, :]).then_inc(ri_done, 1)
                            e.wait_ge(ri_done, n)
                            e.tensor_tensor(PTB[:, gb * GT:(gb + 1) * GT, bass.ds(2 * hp, 2)].rearrange("p t h -> p h t"),
                                            ex[:, :, S].rearrange("p (h t) -> p h t", h=2),
                                            ri[:, :].rearrange("p (h t) -> p h t", h=2), ALU.mult)
                            e.tensor_tensor(PR[:, :, :], ex[:, :, 0:S], ri[:, :].unsqueeze(2).to_broadcast([P, 2 * GT, S]),
                                            ALU.mult).then_inc(p_ready, 1)
                            e.wait_ge(p_ready, n)
                            for b in range(2):
                                for y in range(0, S, 32):
                                    for z in range(0, S, 32):
                                        i = e.transpose(PRT[b * S + z:b * S + z + 32, :, b * S + y:b * S + y + 32],
                                                        PR[b * S + y:b * S + y + 32, :, z:z + 32])
                            i.then_inc(pt_out, 1)
                        if bridge and gb == 0:
                            e.wait_ge(bw_turned, L + 1)
                            e.tensor_copy(BW[:, :], PROJ[3][0:32, 0:D]).then_inc(bw_out, 1)
                            e.tensor_copy(CUR[:, :], PM[:, bass.ds((L + 1) * LNP, 4)]).then_inc(cur_set, 1)
                        if norm_now is not None and front:
                            e.wait_ge(x_settled, 2 * n if back else 2 * n + 2)
                            norm_stats(e, norm, *norm_now)
                            norm_rstd(e, norm, *norm_now)
                            norm_apply(e, norm, *norm_now)
                        if front and g == 1:
                            round_set(pair + 1, 1 - a)
                        if back:
                            for h in range(2):
                                e.wait_ge(c_hi, 2 * n - 1 + h)
                                e.tensor_tensor(CLO[:, h, :], bank[3 + h][:, :], CHI[:, h, :].bitcast(F32),
                                                ALU.subtract).then_inc(c_lo, 1)
                        if norm_now is not None and not front:
                            e.wait_ge(x_settled, 2 * n)
                            norm_stats(e, norm, *norm_now)
                            norm_rstd(e, norm, *norm_now)
                            norm_apply(e, norm, *norm_now)
                        if front:
                            e.wait_ge(s_done, n + 1)
                            if g == 0:
                                e.wait_ge(bwt_sum, (BWTN - HP) * L + 2 + pair)
                                e.tensor_tensor(BWT[:, :, :], BWT[:, :, :],
                                                logits[:, 1, 448:512].rearrange("p (c n) -> p c n", n=32),
                                                ALU.add).then_inc(bwt_sum, 1)
                            e.tensor_reduce(mx[:, :].rearrange("p (h t) -> p h t", h=2), logit, AX_X,
                                            ALU.max).then_inc(mx_done, 1)
                            e.wait_ge(mx_done, n + 1)
                            e.tensor_tensor(sub[:, :, :].rearrange("p (h t) k -> p h t k", h=2), logit,
                                            mx[:, :].rearrange("p (h t) -> p h t", h=2).unsqueeze(3)
                                            .to_broadcast([P, 2, GT, KEYS]), ALU.subtract).then_inc(sub_done, 1)
                        if back:
                            for j in range(2):
                                e.wait_ge(o_done, 2 * n - 1 + j)
                                xs = X[:, gb * GT + 2 * j:gb * GT + 2 * j + 2, :]
                                e.tensor_tensor(xs, xs, bank[3 + j][:, :].rearrange("p (t n) -> p t n", n=256),
                                                ALU.add).then_inc(x_settled, 1)


                    def round_set(m, a):
                        e.wait_ge(w_in[a], 8 * (m - a) + 16)
                        e.tensor_copy(WHI[a][:, :, :, :], W[a][:, :, :, :]).then_inc(w_hi, 1)

                    e.memset(PH[:, :, NL * H:2 * SETS], 0.0)
                    e.wait_ge(vec_turned, 1)
                    e.tensor_copy(PH[:, :, 0:NL * H], bank[3][:, 0:ROWS_H].rearrange("p (j h) -> p j h", j=5)
                                  ).then_inc(vec_copied, 1)
                    e.tensor_copy(PM[:, :], bank[3][:, ROWS_H:ROWS_H + ROWS_M]).then_inc(vec_copied, 1)
                    e.wait_ge(vec_copied, 2)
                    e.tensor_copy(CUR[:, :], PM[:, 0:4]).then_inc(cur_set, 1)
                    e.wait_ge(zeros_set, 1)
                    e.wait_ge(e_made, 1)
                    for t, j in ((EA, 4), (EB, 3)):
                        flat = t[:, :, :].rearrange("p m n -> p (m n)")
                        for L in range(NL):
                            e.tensor_copy(flat[:, L * H * 32:L * H * 32 + (H - 1) * 33 + 1:33],
                                          PH[:, j, L * H:(L + 1) * H])
                    e.tensor_scalar(EB[:, 0:NL * H, H], PH[:, 3, 0:NL * H], -1.0, None, ALU.mult).then_inc(e_made, 2)
                    def ctx_rest(g):
                        for c in range(DC):
                            e.wait_ge(ctx_hi, g * DC + c + 1)
                            dst = (slice(None), 0, c, slice(g * GTOK, (g + 1) * GTOK))
                            e.tensor_tensor(SRC_LO[dst], CB[g % 2][c][:, :], SRC_HI[dst].bitcast(F32),
                                            ALU.subtract).then_inc(ctx_lo, 1)

                    ctx_rest(0)
                    for g in range(G - 1):
                        e.wait_ge(x_in[g], 16)
                        norm_stats(e, norm, 0, g)
                        ctx_rest(g + 1)
                        norm_rstd(e, norm, 0, g)
                        norm_apply(e, norm, 0, g)
                        if g == 0:
                            round_set(0, 0)
                    e.wait_ge(x_in[G - 1], 16)
                    e.memset(mx[:, :], 0.0).then_inc(x_settled, 2)
                    with e.Fori(0, NL) as L:
                        e.memset(BWT[:, :, :], 0.0).then_inc(bwt_sum, 1)
                        e.wait_ge(bwt_sum, L * BWTN + 1)
                        e.tensor_copy(BWT[:, :, H + 1], PM[:, bass.ds(L * LNP + 4, 2)]).then_inc(bwt_sum, 1)
                        slots(e, L, slot)

        def mlp(tag, norm, k, b1, w, ready, b2d, func, dst, more):
            LAG, NB = 3, 4
            (w1h, w1l), (w2h, w2l) = w
            TB = logits[:, 0, :], logits[:, 1, :]
            with ExitStack() as ph:
                b2b = sb(tag + "b2b", [P, D], scope=ph)
                gf = sb(tag + "gf", [P, NB, 512], scope=ph)
                gh, gl = sb(tag + "gh", [P, NB, 512], F32R, scope=ph), sb(tag + "gl", [P, NB, 512], F32R, scope=ph)
                b2_in = sem(tag + "b2_in")
                up_done, g_full, g_hi, g_lo = sem(tag + "up"), sem(tag + "full"), sem(tag + "hi"), sem(tag + "lo")
                down_used, y_added, b2_added = sem(tag + "dn"), sem(tag + "ya"), sem(tag + "b2a")
                stored = sem(tag + "st")

                def groups(e, body, tail=None):
                    body(0, True)
                    with e.Fori(1, G) as g:
                        body(g, False)
                    if tail is not None:
                        tail()

                with nc.Block() as block:
                    @block.sync
                    def _(e):
                        e.dma_start(b2b[:, :], b2d.partition_broadcast(P)).then_inc(b2_in, 16)
                        if "sync" in more:
                            more["sync"](e)
                        if dst is not None:
                            for g in range(G):
                                e.wait_ge(y_added, 2 * (g + 1))
                                e.dma_start(dst[:, g * GT:(g + 1) * GT, :], X[:, g * GT:(g + 1) * GT, :]).then_inc(stored, 16)
                            e.wait_ge(stored, 16 * G)

                    @block.gpsimd
                    def _(e):
                        def body(g, first):
                            for j in range(FC):
                                q = g * FC + j
                                e.wait_ge(g_hi, q + 1)
                                e.tensor_tensor(gl[:, j % NB, :], gf[:, j % NB, :], gh[:, j % NB, :].bitcast(F32),
                                                ALU.subtract).then_inc(g_lo, 1)
                                if first and j == 2:
                                    norm_lo(e, norm, k, G - 1)
                                    e.wait_ge(b2_in, 16)
                                if first and j == FC - 1 and "gpsimd" in more:
                                    more["gpsimd"](e)
                                if j == 3:
                                    xs = X[:, bass.ds(g * GT, GT), :]
                                    e.tensor_tensor(xs, xs, b2b[:, :].unsqueeze(1).to_broadcast([P, GT, D]),
                                                    ALU.add).then_inc(b2_added, 1)

                        groups(e, body)

                    @block.scalar
                    def _(e):
                        def body(g, first):
                            for j in range(FC):
                                q = g * FC + j
                                e.wait_ge(up_done, q + 1)
                                if not first or j >= NB:
                                    e.wait_ge(g_lo, q - NB + 1)
                                e.activation(gf[:, j % NB, :], PROJ[j % 4][:, :], func,
                                             bias=b1[:, j:j + 1]).then_inc(g_full, 1)
                                if first and j == 2:
                                    norm_scale(e, norm, k, G - 1, TB)

                        norm_sqrt(e, norm, k, G - 1)
                        if "scalar_first" in more:
                            more["scalar_first"](e)
                        groups(e, body)

                    @block.vector
                    def _(e):
                        def add(g):
                            e.wait_ge(b2_added, g + 1)
                            e.wait_ge(down_used, FC * (g + 1))
                            for j in range(2):
                                xs = X[:, bass.ds(g * GT + 2 * j, 2), :]
                                e.tensor_tensor(xs, xs, bank[3 + j][:, :].rearrange("p (t n) -> p t n", n=256),
                                                ALU.add).then_inc(y_added, 1)

                        def body(g, first):
                            for j in range(FC):
                                q = g * FC + j
                                if j == LAG and not first:
                                    add(g - 1)
                                e.wait_ge(g_full, q + 1)
                                if not first or j >= NB:
                                    e.wait_ge(down_used, q - NB + 1)
                                e.tensor_copy(gh[:, j % NB, :], gf[:, j % NB, :]).then_inc(g_hi, 1)
                                if first and j == FC - 1 and "vector" in more:
                                    more["vector"](e)

                        if not norm.rms:
                            norm_stats(e, norm, k, G - 1)
                        norm_rstd(e, norm, k, G - 1)
                        norm_apply(e, norm, k, G - 1)
                        more["vector_first"](e)
                        groups(e, body, lambda: add(G - 1))

                    @block.tensor
                    def _(e):
                        def down(g, q, j, first):
                            e.wait_ge(g_lo, q + 1)
                            if j == 0 and not first:
                                e.wait_ge(y_added, 2 * g)
                            for t in range(GT):
                                ts = slice(t * P, (t + 1) * P)
                                i = three(e, bank[3 + t // 2][:, (t % 2) * 256:(t % 2 + 1) * 256],
                                          gh[:, j % NB, ts], gl[:, j % NB, ts], w2h[:, j // 2, j % 2, :],
                                          w2l[:, j // 2, j % 2, :], j == 0 and t % 2 == 0, j == FC - 1,
                                          skip_group_check=True)
                            i.then_inc(down_used, 1)

                        def body(g, first):
                            toks = bass.ds(g * GTOK, GTOK)
                            for j in range(FC):
                                q = g * FC + j
                                if not first or j >= 4:
                                    e.wait_ge(g_full, q - 3)
                                for c in range(DC):
                                    fs = slice(j % 2 * P, (j % 2 + 1) * P)
                                    i = three(e, PROJ[j % 4][:, :], w1h[:, j // 2, c, fs], w1l[:, j // 2, c, fs],
                                              SRC_HI[:, 1, c, toks], SRC_LO[:, 1, c, toks], c == 0, c == DC - 1)
                                i.then_inc(up_done, 1)
                                if first and j == 2:
                                    norm_turn(e, norm, k, G - 1, TB)
                                if first and j == LAG:
                                    e.wait_ge(*ready[1])
                                if j >= LAG:
                                    down(g, q - LAG, j - LAG, first)
                                elif not first:
                                    down(g - 1, q - LAG, j - LAG + FC, first)
                            if first:
                                e.wait_ge(norm.lo, (k + 1) * G * DC)

                        e.wait_ge(norm.lo, (k + 1) * G * DC - DC)
                        e.wait_ge(*ready[0])
                        groups(e, body, lambda: [down(G - 1, G * FC - LAG + t, FC - LAG + t, False) for t in range(LAG)])

        def round_fc2(e):
            e.wait_ge(w_in[1], 8 * SETS)
            e.activation(WHI[1][:, :, :, :].rearrange("p j c n -> p (j c n)"),
                         W[1][:, :, :, :].rearrange("p j c n -> p (j c n)"), ACT.Copy).then_inc(w_hi, 1)

        def split_fc2(e):
            e.wait_ge(w_hi, SETS)
            e.tensor_tensor(WLO[1][:, :, :, :], W[1][:, :, :, :], WHI[1][:, :, :, :].bitcast(F32),
                            ALU.subtract).then_inc(w_split, 1)

        def load_l1(e):
            e.wait_ge(w_split, SETS - 1)
            for j, w in enumerate((qw, kw, vw)):
                e.dma_start(W[0][:, j, :, :], w.rearrange("(c p) n -> p c n", p=P)).then_inc(wr_in, 16)

        def round_l1(e):
            e.wait_ge(wr_in, 48)
            e.tensor_copy(wh[:, :, :, :], W[0][:, 0:3, :, :]).then_inc(wh_done, 1)

        def split_l1(e):
            e.wait_ge(wh_done, 1)
            e.tensor_tensor(wl[:, :, :, :], W[0][:, 0:3, :, :], wh[:, :, :, :].bitcast(F32), ALU.subtract).then_inc(wl_done, 1)

        mlp("m0", norm, NL, PM[:, C_M0 + 4:C_M0 + 12], list(zip(WHI, WLO)), ((w_split, SETS - 1), (w_split, SETS)),
            b_fc2, ACT.Gelu, None,
            {"sync": load_l1, "scalar_first": round_fc2, "vector_first": split_fc2, "vector": round_l1,
             "gpsimd": split_l1})

        NK = 2 * S
        GH = NH // DC
        JP = GH // 2
        VW = DH + 1
        HALF = slice(0, S), slice(S, P)
        wt.close()
        with ExitStack() as l1:
            KL = sb("KL", [P, DC, B, NK], scope=l1)
            VL = sb("VL", [P, B, NH, VW], scope=l1)
            QL = sb("QL", [P, DC, TOK], scope=l1)
            MA = sb("MA", [P, B, S], BF16, scope=l1)
            ONE = sb("ONE", [P, P], BF16, scope=l1)
            HM = sb("HM", [P, GH], scope=l1)
            swap = sb("swap", [P, P], scope=l1)
            KQ = KL[:, :, :, :].rearrange("p m (t a) (h k) -> p m t (a h) k", a=2, h=2)
            QB, KB, VB = PM[:, C_QB:C_QB + 2], PM[:, C_KB:C_KB + 2], PM[:, C_VB:C_VB + 2]
            ow_in = sem("ow_in")
            with ExitStack() as ph:
                mask_in = sem("mask_in")
                owr = HT[:, 0, :].rearrange("p (e n) -> p e n", n=D)
                xl_turned, xl_hi, xl_lo = sem("xl_turned"), sem("xl_hi"), sem("xl_lo")
                one_set, ma_set, v_one = sem("one_set"), sem("ma_set"), sem("v_one")
                ql_done, ql_out, vl_done, vl_out = sem("ql_done"), sem("ql_out"), sem("vl_done"), sem("vl_out")
                swap_set = sem("swap_set")
                mrow = XN[0:1, :, :, :].rearrange("p a t d -> p (a t d)").bitcast(I32)
                VBK = [bank[3], bank[4], bank[7]]
                with nc.Block() as block:
                    @block.sync
                    def _(e):
                        e.dma_start(owr, ow.rearrange("e p n -> p e n")).then_inc(ow_in, 16)
                        e.dma_start(mrow, mask.rearrange("(a b) s -> a (b s)", a=1)).then_inc(mask_in, 16)

                    @block.gpsimd
                    def _(e):
                        e.memset(VL[:, :, :, DH], 1.0).then_inc(v_one, 1)
                        e.memset(ONE[:, :], 0.0).then_inc(one_set, 1)
                        e.memset(MA[:, :, :], 0.0).then_inc(ma_set, 1)
                        e.wait_ge(one_set, 1)
                        e.memset(ONE[0:1, :], 1.0).then_inc(one_set, 1)

                    @block.scalar
                    def _(e):
                        for g in range(G):
                            for c in range(DC):
                                e.wait_ge(xl_turned, g * DC + c + 1)
                                e.activation(SRC_HI[:, 1, c, g * GTOK:(g + 1) * GTOK], PROJ[2 * (g % 2) + c][:, :],
                                             ACT.Copy).then_inc(xl_hi, 1)
                        q = 0
                        for g in range(G):
                            for m in range(DC):
                                e.wait_ge(ql_done, q + 1)
                                e.activation(QL[:, m, g * GTOK:(g + 1) * GTOK], bank[q % 3][:, :], ACT.Identity,
                                             bias=QB[:, m:m + 1]).then_inc(ql_out, 1)
                                q += 1
                        for g in range(G):
                            for half in range(2):
                                for m in range(DC):
                                    e.wait_ge(ql_done, q + 1)
                                    part = bank[q % 3][:, :].rearrange("p (t a k) -> p t a k", a=2, k=S)
                                    tiles = slice(g * GT, (g + 1) * GT)
                                    if half == 0:
                                        i = e.activation(KQ[:, m, tiles, 0:4:3, :], part, ACT.Identity, bias=KB[:, m:m + 1])
                                    else:
                                        e.activation(KQ[:, m, tiles, 2, :], part[:, :, 0, :], ACT.Identity, bias=KB[:, m:m + 1])
                                        i = e.activation(KQ[:, m, tiles, 1, :], part[:, :, 1, :], ACT.Identity, bias=KB[:, m:m + 1])
                                    i.then_inc(ql_out, 1)
                                    q += 1

                    @block.vector
                    def _(e):
                        e.tensor_copy(swap[:, 0:S], ident[:, S:P]).then_inc(swap_set, 1)
                        e.tensor_copy(swap[:, S:P], ident[:, 0:S]).then_inc(swap_set, 1)
                        e.tensor_reduce(HM[:, :], ident[:, :].rearrange("p (h d) -> p h d", d=DH), AX_X, ALU.add)
                        for g in range(G):
                            for c in range(DC):
                                e.wait_ge(xl_hi, g * DC + c + 1)
                                toks = slice(g * GTOK, (g + 1) * GTOK)
                                e.tensor_tensor(SRC_LO[:, 1, c, toks], PROJ[2 * (g % 2) + c][:, :],
                                                SRC_HI[:, 1, c, toks].bitcast(F32), ALU.subtract).then_inc(xl_lo, 1)
                        e.wait_ge(mask_in, 16)
                        e.wait_ge(ma_set, 1)
                        e.tensor_scalar(MA[0:1, :, :], mrow.rearrange("p (b s) -> p b s", s=S), 0.0, MASKED,
                                        ALU.is_equal, ALU.mult).then_inc(ma_set, 1)
                        e.wait_ge(v_one, 1)
                        for t in range(NT):
                            e.wait_ge(vl_done, t + 1)
                            part = VBK[t % 3][:, :].rearrange("p (h j d) -> p h j d", h=2, d=DH)
                            e.tensor_copy(VL[HALF[0], 2 * t:2 * t + 2, :, 0:DH], part[HALF[0], :, :, :])
                            e.tensor_copy(VL[HALF[1], 2 * t + 1, :, 0:DH], part[HALF[1], 0, :, :])
                            e.tensor_copy(VL[HALF[1], 2 * t, :, 0:DH], part[HALF[1], 1, :, :]).then_inc(vl_out, 1)

                    @block.tensor
                    def _(e):
                        e.wait_ge(swap_set, 2)
                        for g in range(G):
                            if g >= 2:
                                e.wait_ge(xl_lo, (g - 1) * DC)
                            for c in range(DC):
                                for p in range(GT):
                                    i = e.transpose(PROJ[2 * (g % 2) + c][:, p * P:(p + 1) * P],
                                                    X[:, g * GT + p, c * P:(c + 1) * P], swap[:, :])
                                i.then_inc(xl_turned, 1)
                        e.wait_ge(xl_lo, G * DC)
                        e.wait_ge(wl_done, 1)
                        q = 0
                        for g in range(G):
                            for m in range(DC):
                                if q >= 3:
                                    e.wait_ge(ql_out, q - 2)
                                toks, cols = slice(g * GTOK, (g + 1) * GTOK), slice(m * P, (m + 1) * P)
                                for c in range(DC):
                                    i = three(e, bank[q % 3][:, :], wh[:, 0, c, cols], wl[:, 0, c, cols],
                                              SRC_HI[:, 1, c, toks], SRC_LO[:, 1, c, toks], c == 0, c == DC - 1)
                                i.then_inc(ql_done, 1)
                                q += 1
                        for g in range(G):
                            toks = slice(g * GTOK, (g + 1) * GTOK)
                            for half in range(2):
                                for m in range(DC):
                                    e.wait_ge(ql_out, q - 2)
                                    cols = slice(m * P, (m + 1) * P)
                                    for c in range(DC):
                                        i = three(e, bank[q % 3][:, :], wh[:, 1, c, cols], wl[:, 1, c, cols],
                                                  SRC_HI[:, half, c, toks], SRC_LO[:, half, c, toks], c == 0, c == DC - 1)
                                    i.then_inc(ql_done, 1)
                                    q += 1
                            for t in range(g * GT, (g + 1) * GT):
                                if t >= 3:
                                    e.wait_ge(vl_out, t - 2)
                                ks = slice(t * P, (t + 1) * P)
                                for half in range(2):
                                    for c in range(DC):
                                        i = three(e, VBK[t % 3][:, half * 256:(half + 1) * 256],
                                                  SRC_HI[:, half, c, ks], SRC_LO[:, half, c, ks],
                                                  wh[:, 2, c, :], wl[:, 2, c, :], c == 0, c == DC - 1)
                                i.then_inc(vl_done, 1)

            with ExitStack() as ph:
                QE = [sb(f"QE{a}", [P, GH, S], scope=ph) for a in range(4)]
                PTL = [HT[:, a, :].rearrange("p (j k) -> p j k", k=P) for a in range(2)]
                SUB = [XN[:, a, 0:2, :].rearrange("p t d -> p (t d)") for a in range(2)]
                EXP = [XN[:, a, 2:4, :].rearrange("p t d -> p (t d)") for a in range(2)]
                ml = [sb(f"ml{a}", [P, JP], scope=ph) for a in range(2)]
                rl = [sb(f"rl{a}", [P, JP], scope=ph) for a in range(2)]
                AN = [sb(f"AN{a}", [P, DC, JP, DH], scope=ph) for a in range(2)]
                AT = [sb(f"AT{a}", [P, 2, S], scope=ph) for a in range(2)]
                VS = [sb(f"VS{a}", [P, NH, VW], scope=ph) for a in range(2)]
                vs_set = sem("vs_set")
                owh, owl = wh[:, 0, :, :], wl[:, 0, :, :]
                owh_done, owl_done = sem("owh_done"), sem("owl_done")
                qe_set, sl_done, ml_done = sem("qe_set"), sem("sl_done"), sem("ml_done")
                subl_done, expl_done, tl_done, tl_out = sem("subl_done"), sem("expl_done"), sem("tl_done"), sem("tl_out")
                al_done, rl_done, an_done = sem("al_done"), sem("rl_done"), sem("an_done")
                at_done, at_out, ao_hi, ao_lo = sem("at_done"), sem("at_out"), sem("ao_hi"), sem("ao_lo")
                STEPS = B * DC
                LT, LP, LA, LR = 2, 3, 6, 8

                def steps(e, slot):
                    for s in range(LR + 1):
                        slot(s, s, 0)
                    rest = (STEPS - LR - 1) // 4
                    with e.Fori(0, rest) as i:
                        for r in range(LR + 1, LR + 5):
                            slot(i * 4 + r, r, i * 2)
                    for s in range(LR + 1 + rest * 4, STEPS + LR):
                        slot(s, s, 0)

                def runs(r, lag):
                    return 0 <= r - lag < STEPS

                with nc.Block() as block:
                    @block.gpsimd
                    def _(e):
                        def slot(s, r, b0):
                            if runs(r, 0):
                                if r >= 4:
                                    e.wait_ge(sl_done, s - 3)
                                other = r // 2 + (1 if r // 2 % 2 == 0 else -1)
                                q = QL[:, r % 2, bass.ds((b0 + other) * S, S)]
                                e.tensor_tensor(QE[r % 4][:, :, :], q.unsqueeze(1).to_broadcast([P, GH, S]),
                                                HM[:, :].unsqueeze(2).to_broadcast([P, GH, S]),
                                                ALU.mult).then_inc(qe_set, 1)
                            if runs(r, LR) and (r - LR) % 2 == 0:
                                b = b0 + (r - LR) // 2
                                e.wait_ge(ao_hi, b + 1)
                                toks = bass.ds(b * S, S)
                                e.tensor_tensor(SRC_LO[:, 1, :, toks], AT[(r - LR) // 2 % 2][:, :, :],
                                                SRC_HI[:, 1, :, toks].bitcast(F32), ALU.subtract).then_inc(ao_lo, 1)

                        steps(e, slot)

                    @block.tensor
                    def _(e):
                        def slot(s, r, b0):
                            if runs(r, 0):
                                b = b0 + r // 2
                                e.wait_ge(qe_set, s + 1)
                                if r >= 2:
                                    e.wait_ge(subl_done, s - 1)
                                for j in range(JP):
                                    e.matmul(bank[r % 2][:, j * NK:(j + 1) * NK], QE[r % 4][:, 2 * j:2 * j + 2, :],
                                             KL[:, r % 2, b, :], start=(j == 0), stop=False, skip_group_check=True)
                                half = HALF[r // 2 % 2]
                                i = e.matmul(bank[r % 2][:, :].rearrange("p (j k) -> p j k", k=NK)[:, :, half], ONE[:, :],
                                             MA[:, b, :].unsqueeze(1).to_broadcast([P, JP, S]), start=False, stop=True,
                                             skip_group_check=True)
                                i.then_inc(sl_done, 1)
                            if runs(r, LT):
                                a = (r - LT) % 2
                                e.wait_ge(expl_done, s - LT + 1)
                                if r - LT >= 2:
                                    e.wait_ge(tl_out, s - LT - 1)
                                for j in range(JP):
                                    i = e.transpose(PROJ[2 + a][:, j * P:(j + 1) * P], EXP[a][:, j * NK:(j + 1) * NK],
                                                    ident[:, :])
                                i.then_inc(tl_done, 1)
                            if runs(r, LP):
                                a, b = (r - LP) % 2, b0 + (r - LP) // 2
                                e.wait_ge(tl_out, s - LP + 1)
                                e.wait_ge(vs_set, b + 1)
                                if r - LP >= 2:
                                    e.wait_ge(an_done, s - LP - 1)
                                for j in range(JP):
                                    for h in range(2):
                                        i = e.matmul(bank[3 + a][HALF[h], j * VW:(j + 1) * VW], PTL[a][:, j, HALF[h]],
                                                     VS[(r - LP) // 2 % 2][:, (a * JP + j) * 2 + h, :],
                                                     start=True, stop=True)
                                i.then_inc(al_done, 1)
                            if runs(r, LA) and (r - LA) % 2 == 0:
                                b, c = b0 + (r - LA) // 2, (r - LA) // 2 % 2
                                e.wait_ge(an_done, 2 * b + 2)
                                if r - LA >= 4:
                                    e.wait_ge(at_out, 2 * b - 2)
                                e.transpose(logits[:, c, 0:P], AN[c][:, :, :, :].rearrange("p m j d -> p (m j d)"),
                                            ident[:, :]).then_inc(at_done, 1)

                        steps(e, slot)

                    @block.scalar
                    def _(e):
                        def slot(s, r, b0):
                            if runs(r, LT):
                                a = (r - LT) % 2
                                e.wait_ge(tl_done, s - LT + 1)
                                if r == LT:
                                    e.wait_ge(owl_done, 1)
                                e.activation(HT[:, a, :], PROJ[2 + a][:, :], ACT.Copy).then_inc(tl_out, 1)
                                if a == 0:
                                    b = b0 + (r - LT) // 2
                                    if r - LT >= 4:
                                        e.wait_ge(al_done, 2 * b - 2)
                                    e.activation(VS[(r - LT) // 2 % 2][:, :, :].rearrange("p h d -> p (h d)"),
                                                 VL[:, b, :, :].rearrange("p h d -> p (h d)"), ACT.Copy).then_inc(vs_set, 1)
                            if runs(r, LA) and (r - LA) % 2 == 0:
                                b, c = b0 + (r - LA) // 2, (r - LA) // 2 % 2
                                e.wait_ge(at_done, b + 1)
                                if r - LA >= 4:
                                    e.wait_ge(ao_lo, b - 1)
                                for h in range(2):
                                    e.activation(AT[c][:, h, :], logits[:, c, h * S:(h + 1) * S], ACT.Identity,
                                                 bias=VB[:, h:h + 1]).then_inc(at_out, 1)
                            if runs(r, 0):
                                e.wait_ge(subl_done, s + 1)
                                e.activation(EXP[r % 2], SUB[r % 2], ACT.Exp, scale=1.0 / DH).then_inc(expl_done, 1)

                        steps(e, slot)

                    @block.vector
                    def _(e):
                        def slot(s, r, b0):
                            if runs(r, 0):
                                a = r % 2
                                e.wait_ge(sl_done, s + 1)
                                lg = bank[a][:, :].rearrange("p (j k) -> p j k", k=NK)
                                e.tensor_reduce(ml[a][:, :], lg, AX_X, ALU.max).then_inc(ml_done, 1)
                                e.wait_ge(ml_done, s + 1)
                                if r >= 2:
                                    e.wait_ge(expl_done, s - 1)
                                e.tensor_tensor(SUB[a].rearrange("p (j k) -> p j k", k=NK), lg,
                                                ml[a][:, :].unsqueeze(2).to_broadcast([P, JP, NK]),
                                                ALU.subtract).then_inc(subl_done, 1)
                            if runs(r, LP):
                                a, c = (r - LP) % 2, (r - LP) // 2 % 2
                                e.wait_ge(al_done, s - LP + 1)
                                res = bank[3 + a][:, 0:JP * VW].rearrange("p (j d) -> p j d", d=VW)
                                e.reciprocal(rl[a][:, :], res[:, :, DH]).then_inc(rl_done, 1)
                                e.wait_ge(rl_done, s - LP + 1)
                                if a == 0 and r - LP >= 4:
                                    e.wait_ge(at_done, b0 + (r - LP) // 2 - 1)
                                e.tensor_tensor(AN[c][:, a, :, :], res[:, :, 0:DH],
                                                rl[a][:, :].unsqueeze(2).to_broadcast([P, JP, DH]), ALU.mult).then_inc(an_done, 1)
                            if runs(r, LA) and (r - LA) % 2 == 0:
                                b, c = b0 + (r - LA) // 2, (r - LA) // 2 % 2
                                e.wait_ge(at_out, 2 * b + 2)
                                e.tensor_copy(SRC_HI[:, 1, :, bass.ds(b * S, S)], AT[c][:, :, :]).then_inc(ao_hi, 1)

                        e.wait_ge(ow_in, 16)
                        e.tensor_copy(owh, owr).then_inc(owh_done, 1)
                        e.wait_ge(owh_done, 1)
                        e.tensor_tensor(owl, owr, owh.bitcast(F32), ALU.subtract).then_inc(owl_done, 1)
                        steps(e, slot)

        Y = sb("Y", [P, NT, D])
        W2 = [sb(f"mlp_w{a}", [P, 4, DC, 256]) for a in range(2)]
        W2HI = [sb(f"mlp_whi{a}", [P, 4, DC, 256], F32R) for a in range(2)]
        W2LO = [sb(f"mlp_wlo{a}", [P, 4, DC, 256], F32R) for a in range(2)]
        w2_in, w2_hi, w2_split = [sem(f"mlp_w_in{a}") for a in range(2)], sem("mlp_w_hi"), sem("mlp_w_split")
        norm1 = Norm("rn", Y, True, RMS_EPS, PM[:, C_PN:C_PN + 2])
        sq = sb("sq", [P, GT, D])
        eps_col = sb("eps_col", [P, 1])
        norm1.squares, norm1.eps_col = sq, eps_col
        with ExitStack() as ph:
            obb = sb("obb", [P, D], scope=ph)
            eps_set, ob_in = sem("eps_set"), sem("ob_in")
            OB = [bank[3], bank[4]]
            y_prod, y_sum = sem("y_prod"), sem("y_sum")
            y_base = [sem(f"y_base{g}") for g in range(G)]

            def base(e, g):
                ts = slice(g * GT, (g + 1) * GT)
                e.tensor_tensor(Y[:, ts, :], X[:, ts, :], obb[:, :].unsqueeze(1).to_broadcast([P, GT, D]),
                                ALU.add).then_inc(y_base[g], 1)

            with nc.Block() as block:
                @block.sync
                def _(e):
                    e.dma_start(obb[:, :], out_b.partition_broadcast(P)).then_inc(ob_in, 16)
                    for a in range(2):
                        e.dma_start(W2[a][:, :, :, :], (w1, w2)[a].rearrange("j (c p) n -> p j c n", p=P)
                                    ).then_inc(w2_in[a], 16)

                @block.gpsimd
                def _(e):
                    e.memset(eps_col[:, :], RMS_EPS).then_inc(eps_set, 1)
                    e.wait_ge(ob_in, 16)
                    for g in range(1, G):
                        base(e, g)
                    e.wait_ge(w2_hi, 1)
                    e.tensor_tensor(W2LO[0][:, :, :, :], W2[0][:, :, :, :], W2HI[0][:, :, :, :].bitcast(F32),
                                    ALU.subtract).then_inc(w2_split, 1)
                    for g in range(G - 1):
                        norm_lo(e, norm1, 0, g)

                @block.scalar
                def _(e):
                    e.wait_ge(eps_set, 1)
                    for g in range(G):
                        if g < G - 1:
                            e.wait_ge(y_sum, 2 * g + 2)
                            norm_sqrt(e, norm1, 0, g)
                        if g < 2:
                            e.wait_ge(w2_in[g], 16)
                            e.activation(W2HI[g][:, :, :, :].rearrange("p j c n -> p (j c n)"),
                                         W2[g][:, :, :, :].rearrange("p j c n -> p (j c n)"), ACT.Copy).then_inc(w2_hi, 1)
                        if g >= 1:
                            norm_scale(e, norm1, 0, g - 1, PROJ[2:])

                @block.vector
                def _(e):
                    e.wait_ge(ob_in, 16)
                    base(e, 0)
                    for g in range(G):
                        e.wait_ge(y_base[g], 1)
                        for v in (2 * g, 2 * g + 1):
                            e.wait_ge(y_prod, v + 1)
                            ys = Y[:, 2 * v:2 * v + 2, :]
                            e.tensor_tensor(ys, ys, OB[v % 2][:, :].rearrange("p (t n) -> p t n", n=256),
                                            ALU.add).then_inc(y_sum, 1)
                        if g >= 1:
                            norm_rstd(e, norm1, 0, g - 1)
                            norm_apply(e, norm1, 0, g - 1)
                    e.wait_ge(y_sum, 2 * G)

                @block.tensor
                def _(e):
                    e.wait_ge(owl_done, 1)
                    for g in range(G):
                        for v in (2 * g, 2 * g + 1):
                            if v >= 2:
                                e.wait_ge(y_sum, v - 1)
                            for t in (2 * v, 2 * v + 1):
                                ts = slice(t * P, (t + 1) * P)
                                for h in range(2):
                                    i = three(e, OB[v % 2][:, (t % 2) * 256:(t % 2 + 1) * 256], SRC_HI[:, 1, h, ts],
                                              SRC_LO[:, 1, h, ts], owh[:, h, :], owl[:, h, :], h == 0, h == 1)
                            i.then_inc(y_prod, 1)
                        for k in ((), (), (0,), (1, 2))[g]:
                            if k >= 1:
                                e.wait_ge(norm1.scaled, k * DC)
                            norm_turn(e, norm1, 0, k, PROJ[2:])

        def split_w2(e):
            e.wait_ge(w2_hi, 2)
            e.tensor_tensor(W2LO[1][:, :, :, :], W2[1][:, :, :, :], W2HI[1][:, :, :, :].bitcast(F32),
                            ALU.subtract).then_inc(w2_split, 1)

        mlp("m1", norm1, 0, PM[:, C_B1:C_B1 + 8], list(zip(W2HI, W2LO)), ((w2_split, 1), (w2_split, 2)), b2,
            ACT.Gelu_apprx_tanh, out.rearrange("(t p) d -> p t d", p=P), {"vector_first": split_w2})


def kernel(**inputs):
    import numpy as np
    import concourse.bacc as bacc
    from concourse.bass_utils import run_bass_kernel_spmd

    def given(name):
        return np.asarray(inputs[name])

    def both(name):
        return [given(f"L0_xattn_{name}{i}") for i in (1, 2)]

    def pairs(ws):
        return np.stack([w.reshape(D, HP, 2 * K).transpose(1, 0, 2) for w in ws])

    def sets(up, down):
        return [given(up).reshape(D, 4, 256).transpose(1, 0, 2)[None], given(down).reshape(1, 4, 256, D)]

    def rows(*vs):
        return np.concatenate([v.reshape(-1, P) for v in vs])

    kv_w, kv_b = given("L1_xattn_kv_w").reshape(D, D, 2), given("L1_xattn_kv_b").reshape(D, 2)
    arrays = {
        "x": given("x").reshape(TOK, D),
        "ctx": given("ctx_2048").reshape(TOK, D),
        "mask": given("mask_BxS2_ik0"),
        "wall": np.concatenate([np.stack([pairs(both("wq")), pairs(both("wk")), pairs(both("wv")),
                          np.stack([w.reshape(HP, 2 * K, D) for w in both("wo")])], axis=2
                         ).reshape(NL * HP, 4, 256, 256), *sets("L0_xattn_w_fc1", "L0_xattn_w_fc2")]),
        "vech": rows(*both("bq"), *both("bk"), *both("bias_k"), *both("bv"), *both("bias_v")),
        "vecm": rows(*[given(f"L0_xattn_{n}") for i in (1, 2)
                       for n in (f"ln{i}_scale", f"ln{i}_offset", f"bo{i}")],
                     given("L0_xattn_ln_mlp_scale"), given("L0_xattn_ln_mlp_offset"), given("L0_xattn_b_fc1"),
                     given("L1_xattn_q_b"), kv_b[:, 0],
                     kv_b[:, 1].reshape(NH // 2, 2, DH).transpose(1, 0, 2),
                     given("L1_xattn_postnorm_w"), given("L1_xattn_mlp_b1")),
        "b_fc2": given("L0_xattn_b_fc2"),
        "qw": given("L1_xattn_q_w"), "kw": kv_w[:, :, 0], "vw": kv_w[:, :, 1],
        "ow": given("L1_xattn_out_w").reshape(NH // 2, 2, DH, D).transpose(1, 0, 2, 3).reshape(2, P, D),
        "out_b": given("L1_xattn_out_b"),
        "w1": sets("L1_xattn_mlp_w1", "L1_xattn_mlp_w2")[0][0], "w2": sets("L1_xattn_mlp_w1", "L1_xattn_mlp_w2")[1][0], "b2": given("L1_xattn_mlp_b2"),
    }
    nc = bacc.Bacc("TRN2", target_bir_lowering=False, num_devices=1)
    arrays = {f"in_{k}": np.ascontiguousarray(v) for k, v in arrays.items()}
    args = [nc.dram_tensor(k, v.shape, mybir.dt.from_np(v.dtype), kind="ExternalInput").ap()
            for k, v in arrays.items()]
    out = nc.dram_tensor("out", (TOK, D), F32, kind="ExternalOutput").ap()
    program(nc, *args, out)
    r = run_bass_kernel_spmd(nc, [arrays], core_ids=[0])
    return r.results[0]["out"].reshape(B, S, D)
```
